# Optimizing a Trainium2 kernel written in Bass

```python
import numpy as np
import jax
import jax.numpy as jnp

def _softmax(x, axis=-1):
    return jax.nn.softmax(x, axis=axis)

def _gelu(x):
    return jax.nn.gelu(x, approximate=True)

def _silu(x):
    return jax.nn.silu(x)

def _sigmoid(x):
    return jax.nn.sigmoid(x)

def _layernorm(x, axis=-1, eps=1e-05):
    m = jnp.mean(x, axis=axis, keepdims=True)
    v = jnp.var(x, axis=axis, keepdims=True)
    return (x - m) / jnp.sqrt(v + eps)

def _scatter_add(tgt, idx, src, axis=0):
    return tgt.at[idx].add(src)

def _segment_sum(src, seg, n):
    return jax.ops.segment_sum(src, seg, n)
kernel_name = 'mk_audio_tower_d2_tok_audfeat768_r4_2b9d48'

def setup_inputs(seed: int=0):
    np.random.seed(seed)
    _w = jnp.asarray

    def _rec_inputs():
        import jax
        import jax.numpy as jnp
        _rk = jax.random.key(seed)
        x = -4.65018e-05 + 0.999886 * jax.random.normal(jax.random.fold_in(_rk, 1), (64, 256, 192), jnp.float32)
        return x
    x = _rec_inputs()

    def _L0_tok_setup():
        import jax, jax.numpy as jnp
        import numpy as np
        POOL_SIZE = 2
        STRIDE = 2
        CHANNELS = 192
        key = jax.random.key(seed)
        k1, = jax.random.split(key, 1)
        x = jax.random.normal(k1, (8, 2048, CHANNELS), dtype=jnp.float32)
        w = jnp.eye(CHANNELS, dtype=jnp.float32) * 2.0
        return {'x': x, 'w': w}
    _L0_tok_all = _L0_tok_setup()
    _L0_tok_in = {k: v for k, v in _L0_tok_all.items() if k in ('w',)}
    del _L0_tok_all

    def _L0_attn_setup():
        import jax, jax.numpy as jnp
        import numpy as np
        import math
        N_LAYER, N_EMBD, LAYER_ID = (12, 192, 0)
        B, T, C = (32, 256, N_EMBD)

        def _init_params():
            r01 = LAYER_ID / (N_LAYER - 1)
            r1a0 = 1.0 - LAYER_ID / N_LAYER
            h = np.arange(C, dtype=np.float32)
            time_decay = (-5.0 + 8.0 * (h / (C - 1)) ** (0.7 + 1.3 * r01)).astype(np.float32)
            zigzag = np.array([(i + 1) % 3 - 1 for i in range(C)], dtype=np.float32) * 0.5
            time_first = (np.ones(C, dtype=np.float32) * math.log(0.3) + zigzag).astype(np.float32)
            xlin = (np.arange(C, dtype=np.float32) / C).reshape(1, 1, C)
            time_mix_k = np.power(xlin, r1a0).astype(np.float32)
            time_mix_v = (np.power(xlin, r1a0) + 0.3 * r01).astype(np.float32)
            time_mix_r = np.power(xlin, 0.5 * r1a0).astype(np.float32)
            return (time_decay, time_first, time_mix_k, time_mix_v, time_mix_r)

        def _wkv(w, u, k, v):

            def step(carry, kv):
                p, q, o = carry
                kt, vt = kv
                no = jnp.maximum(o, u + kt)
                A = jnp.exp(o - no)
                Bc = jnp.exp(u + kt - no)
                y = (A * p + Bc * vt) / (A * q + Bc)
                no2 = jnp.maximum(w + o, kt)
                A2 = jnp.exp(w + o - no2)
                B2 = jnp.exp(kt - no2)
                return ((A2 * p + B2 * vt, A2 * q + B2, no2), y)
            b = k.shape[0]
            init = (jnp.zeros((b, C), jnp.float32), jnp.zeros((b, C), jnp.float32), jnp.full((b, C), -1e+38, jnp.float32))
            kT = jnp.swapaxes(k, 0, 1)
            vT = jnp.swapaxes(v, 0, 1)
            _, ys = jax.lax.scan(step, init, (kT, vT))
            return jnp.swapaxes(ys, 0, 1)
        key = jax.random.key(seed)
        ks = jax.random.split(key, 5)
        td, tf, tmk, tmv, tmr = _init_params()
        scale = 0.02
        return {'x': jax.random.normal(ks[0], (B, T, C), dtype=jnp.float32), 'time_decay': jnp.asarray(td), 'time_first': jnp.asarray(tf), 'time_mix_k': jnp.asarray(tmk), 'time_mix_v': jnp.asarray(tmv), 'time_mix_r': jnp.asarray(tmr), 'Wk': jax.random.normal(ks[1], (C, C), dtype=jnp.float32) * scale, 'Wv': jax.random.normal(ks[2], (C, C), dtype=jnp.float32) * scale, 'Wr': jax.random.normal(ks[3], (C, C), dtype=jnp.float32) * scale, 'Wo': jax.random.normal(ks[4], (C, C), dtype=jnp.float32) * scale}
    _L0_attn_all = _L0_attn_setup()
    _L0_attn_in = {k: v for k, v in _L0_attn_all.items() if k in ('time_decay', 'time_first', 'time_mix_k', 'time_mix_v', 'time_mix_r', 'Wk', 'Wv', 'Wr', 'Wo')}
    del _L0_attn_all

    def _L0_ffn_setup():
        import jax, jax.numpy as jnp
        import numpy as np
        B, S, D_IN, D_HID, D_OUT = (32, 128, 192, 768, 192)
        key = jax.random.key(seed)
        k1, k2, k3, k4 = jax.random.split(key, 4)
        init_k = float(np.sqrt(1.0 / D_IN))
        init_k2 = float(np.sqrt(1.0 / D_HID))
        x = jax.random.normal(k1, (B, S, D_IN), dtype=jnp.float32)
        in_weight = jax.random.uniform(k2, (D_HID, D_IN), dtype=jnp.float32, minval=-init_k, maxval=init_k)
        in_bias = jax.random.uniform(k3, (D_HID,), dtype=jnp.float32, minval=-init_k, maxval=init_k)
        out_weight = jax.random.uniform(k4, (D_HID, D_OUT), dtype=jnp.float32, minval=-init_k2, maxval=init_k2)
        return {'x': x, 'in_weight': in_weight, 'in_bias': in_bias, 'out_weight': out_weight}
    _L0_ffn_all = _L0_ffn_setup()
    _L0_ffn_in = {k: v for k, v in _L0_ffn_all.items() if k in ('in_weight', 'in_bias', 'out_weight')}
    del _L0_ffn_all

    def _L1_attn_setup():
        import jax, jax.numpy as jnp
        import numpy as np
        NHEAD = 12
        EPS = 1e-05

        def layernorm_nobias(x, gamma):
            mu = jnp.mean(x, axis=-1, keepdims=True)
            var = jnp.var(x, axis=-1, keepdims=True)
            return (x - mu) * jax.lax.rsqrt(var + EPS) * gamma
        key = jax.random.key(seed)
        ks = jax.random.split(key, 10)
        b, l, d = (4, 512, 192)
        s = d ** (-0.5)
        return {'x': jax.random.normal(ks[0], (b, l, d), jnp.float32), 'Wq': jax.random.normal(ks[1], (d, d), jnp.float32) * s, 'Wk': jax.random.normal(ks[2], (d, d), jnp.float32) * s, 'bk': jax.random.normal(ks[3], (d,), jnp.float32) * 0.02, 'Wv': jax.random.normal(ks[4], (d, d), jnp.float32) * s, 'bv': jax.random.normal(ks[5], (d,), jnp.float32) * 0.02, 'gq': jnp.ones((d,), jnp.float32), 'gk': jnp.ones((d,), jnp.float32), 'Wo': jax.random.normal(ks[6], (d, d), jnp.float32) * s, 'bo': jnp.zeros((d,), jnp.float32)}
    _L1_attn_all = _L1_attn_setup()
    _L1_attn_in = {k: v for k, v in _L1_attn_all.items() if k in ('Wq', 'Wk', 'bk', 'Wv', 'bv', 'gq', 'gk', 'Wo', 'bo')}
    del _L1_attn_all

    def _L1_ffn_setup():
        import jax, jax.numpy as jnp
        import numpy as np
        E, C, F, K = (8, 192, 768, 2)
        key = jax.random.key(seed)
        k0, k1, k2, k3 = jax.random.split(key, 4)
        B, T = (8, 512)
        return {'x': jax.random.normal(k0, (B, T, C), jnp.float32), 'router_w': jax.random.normal(k1, (E, C), jnp.float32) * 0.02, 'w1': jax.random.normal(k2, (E, C, F), jnp.float32) * 0.02, 'b1': jnp.zeros((E, F), jnp.float32), 'w2': jax.random.normal(k3, (E, F, C), jnp.float32) * 0.02, 'b2': jnp.zeros((E, C), jnp.float32)}
    _L1_ffn_all = _L1_ffn_setup()
    _L1_ffn_in = {k: v for k, v in _L1_ffn_all.items() if k in ('router_w', 'w1', 'b1', 'w2', 'b2')}
    del _L1_ffn_all
    return {'x': x, 'L0_tok_w': _L0_tok_in['w'], 'L0_attn_time_decay': _L0_attn_in['time_decay'], 'L0_attn_time_first': _L0_attn_in['time_first'], 'L0_attn_time_mix_k': _L0_attn_in['time_mix_k'], 'L0_attn_time_mix_v': _L0_attn_in['time_mix_v'], 'L0_attn_time_mix_r': _L0_attn_in['time_mix_r'], 'L0_attn_Wk': _L0_attn_in['Wk'], 'L0_attn_Wv': _L0_attn_in['Wv'], 'L0_attn_Wr': _L0_attn_in['Wr'], 'L0_attn_Wo': _L0_attn_in['Wo'], 'L0_ffn_in_weight': _L0_ffn_in['in_weight'], 'L0_ffn_in_bias': _L0_ffn_in['in_bias'], 'L0_ffn_out_weight': _L0_ffn_in['out_weight'], 'L1_attn_Wq': _L1_attn_in['Wq'], 'L1_attn_Wk': _L1_attn_in['Wk'], 'L1_attn_bk': _L1_attn_in['bk'], 'L1_attn_Wv': _L1_attn_in['Wv'], 'L1_attn_bv': _L1_attn_in['bv'], 'L1_attn_gq': _L1_attn_in['gq'], 'L1_attn_gk': _L1_attn_in['gk'], 'L1_attn_Wo': _L1_attn_in['Wo'], 'L1_attn_bo': _L1_attn_in['bo'], 'L1_ffn_router_w': _L1_ffn_in['router_w'], 'L1_ffn_w1': _L1_ffn_in['w1'], 'L1_ffn_b1': _L1_ffn_in['b1'], 'L1_ffn_w2': _L1_ffn_in['w2'], 'L1_ffn_b2': _L1_ffn_in['b2']}

def reference(x, L0_tok_w, L0_attn_time_decay, L0_attn_time_first, L0_attn_time_mix_k, L0_attn_time_mix_v, L0_attn_time_mix_r, L0_attn_Wk, L0_attn_Wv, L0_attn_Wr, L0_attn_Wo, L0_ffn_in_weight, L0_ffn_in_bias, L0_ffn_out_weight, L1_attn_Wq, L1_attn_Wk, L1_attn_bk, L1_attn_Wv, L1_attn_bv, L1_attn_gq, L1_attn_gk, L1_attn_Wo, L1_attn_bo, L1_ffn_router_w, L1_ffn_w1, L1_ffn_b1, L1_ffn_w2, L1_ffn_b2):
    import jax
    import jax.numpy as jnp

    def _L0_tok_ref(x, w):
        import jax, jax.numpy as jnp
        import numpy as np
        POOL_SIZE = 2
        STRIDE = 2
        CHANNELS = 192
        B, S, C = x.shape
        n_windows = (S - POOL_SIZE) // STRIDE + 1
        window = jnp.stack([x[:, i::STRIDE, :][:, :n_windows, :] for i in range(POOL_SIZE)], axis=2)
        scores = jnp.einsum('bnpc,cd->bnpd', window, w)
        weights = jax.nn.softmax(scores, axis=2)
        return jnp.sum(weights * window, axis=2)

    def _L0_attn_ref(x, time_decay, time_first, time_mix_k, time_mix_v, time_mix_r, Wk, Wv, Wr, Wo):
        import jax, jax.numpy as jnp
        import numpy as np
        import math
        N_LAYER, N_EMBD, LAYER_ID = (12, 192, 0)
        B, T, C = (32, 256, N_EMBD)

        def _init_params():
            r01 = LAYER_ID / (N_LAYER - 1)
            r1a0 = 1.0 - LAYER_ID / N_LAYER
            h = np.arange(C, dtype=np.float32)
            time_decay = (-5.0 + 8.0 * (h / (C - 1)) ** (0.7 + 1.3 * r01)).astype(np.float32)
            zigzag = np.array([(i + 1) % 3 - 1 for i in range(C)], dtype=np.float32) * 0.5
            time_first = (np.ones(C, dtype=np.float32) * math.log(0.3) + zigzag).astype(np.float32)
            xlin = (np.arange(C, dtype=np.float32) / C).reshape(1, 1, C)
            time_mix_k = np.power(xlin, r1a0).astype(np.float32)
            time_mix_v = (np.power(xlin, r1a0) + 0.3 * r01).astype(np.float32)
            time_mix_r = np.power(xlin, 0.5 * r1a0).astype(np.float32)
            return (time_decay, time_first, time_mix_k, time_mix_v, time_mix_r)

        def _wkv(w, u, k, v):

            def step(carry, kv):
                p, q, o = carry
                kt, vt = kv
                no = jnp.maximum(o, u + kt)
                A = jnp.exp(o - no)
                Bc = jnp.exp(u + kt - no)
                y = (A * p + Bc * vt) / (A * q + Bc)
                no2 = jnp.maximum(w + o, kt)
                A2 = jnp.exp(w + o - no2)
                B2 = jnp.exp(kt - no2)
                return ((A2 * p + B2 * vt, A2 * q + B2, no2), y)
            b = k.shape[0]
            init = (jnp.zeros((b, C), jnp.float32), jnp.zeros((b, C), jnp.float32), jnp.full((b, C), -1e+38, jnp.float32))
            kT = jnp.swapaxes(k, 0, 1)
            vT = jnp.swapaxes(v, 0, 1)
            _, ys = jax.lax.scan(step, init, (kT, vT))
            return jnp.swapaxes(ys, 0, 1)
        xx = jnp.pad(x, ((0, 0), (1, 0), (0, 0)))[:, :-1, :]
        xk = x * time_mix_k + xx * (1.0 - time_mix_k)
        xv = x * time_mix_v + xx * (1.0 - time_mix_v)
        xr = x * time_mix_r + xx * (1.0 - time_mix_r)
        k = jnp.einsum('btc,oc->bto', xk, Wk)
        v = jnp.einsum('btc,oc->bto', xv, Wv)
        r = jnp.einsum('btc,oc->bto', xr, Wr)
        sr = jax.nn.sigmoid(r)
        y = _wkv(time_decay, time_first, k, v)
        return jnp.einsum('btc,oc->bto', sr * y, Wo)

    def _L0_ffn_ref(x, in_weight, in_bias, out_weight):
        import jax, jax.numpy as jnp
        import numpy as np
        B, S, D_IN, D_HID, D_OUT = (32, 128, 192, 768, 192)
        lead = x.shape[:-1]
        xt = x.reshape(-1, in_weight.shape[1])
        h = jax.nn.gelu(jnp.einsum('td,hd->th', xt, in_weight) + in_bias, approximate=False)
        out = jnp.einsum('th,ho->to', h, out_weight)
        return out.reshape(*lead, out_weight.shape[1])

    def _L1_attn_ref(x, Wq, Wk, bk, Wv, bv, gq, gk, Wo, bo):
        import jax, jax.numpy as jnp
        import numpy as np
        NHEAD = 12
        EPS = 1e-05

        def layernorm_nobias(x, gamma):
            mu = jnp.mean(x, axis=-1, keepdims=True)
            var = jnp.var(x, axis=-1, keepdims=True)
            return (x - mu) * jax.lax.rsqrt(var + EPS) * gamma
        b, l, d = x.shape
        n = NHEAD
        hd = d // n
        scale = hd ** (-0.5)
        q = layernorm_nobias(x @ Wq.T, gq)
        k = layernorm_nobias(x @ Wk.T + bk, gk)
        v = x @ Wv.T + bv
        q = q.reshape(b, l, n, hd).transpose(0, 2, 1, 3)
        k = k.reshape(b, l, n, hd).transpose(0, 2, 1, 3)
        v = v.reshape(b, l, n, hd).transpose(0, 2, 1, 3)
        scores = jnp.einsum('bnqd,bnkd->bnqk', q, k) * scale
        attn = jax.nn.softmax(scores, axis=-2)
        o = jnp.einsum('bnqk,bnkd->bnqd', attn, v)
        o = o.transpose(0, 2, 1, 3).reshape(b, l, d)
        return o @ Wo.T + bo + x

    def _L1_ffn_ref(x, router_w, w1, b1, w2, b2):
        import jax, jax.numpy as jnp
        import numpy as np
        E, C, F, K = (8, 192, 768, 2)
        B, T, Cc = x.shape
        flat = x.reshape(-1, Cc)
        logits = flat @ router_w.T
        probs = jax.nn.softmax(logits.astype(jnp.float32), axis=-1)
        top_w, top_i = jax.lax.top_k(probs, K)
        top_w = (top_w / top_w.sum(-1, keepdims=True)).astype(x.dtype)
        out = jnp.zeros_like(flat)
        for e in range(E):
            w_e = jnp.sum(top_w * (top_i == e), axis=-1)[:, None]
            h = jax.nn.gelu(flat @ w1[e] + b1[e], approximate=False)
            out = out + w_e * (h @ w2[e] + b2[e])
        return out.reshape(B, T, Cc)
    h = _L0_tok_ref(x, L0_tok_w)
    h = h + _L0_attn_ref(_layernorm(h, axis=-1), L0_attn_time_decay, L0_attn_time_first, L0_attn_time_mix_k, L0_attn_time_mix_v, L0_attn_time_mix_r, L0_attn_Wk, L0_attn_Wv, L0_attn_Wr, L0_attn_Wo)
    h = h + _L0_ffn_ref(_layernorm(h, axis=-1), L0_ffn_in_weight, L0_ffn_in_bias, L0_ffn_out_weight)
    h = h + _L1_attn_ref(_layernorm(h, axis=-1), L1_attn_Wq, L1_attn_Wk, L1_attn_bk, L1_attn_Wv, L1_attn_bv, L1_attn_gq, L1_attn_gk, L1_attn_Wo, L1_attn_bo)
    h = h + _L1_ffn_ref(_layernorm(h, axis=-1), L1_ffn_router_w, L1_ffn_w1, L1_ffn_b1, L1_ffn_w2, L1_ffn_b2)
    return h

_drawn_inputs = setup_inputs


def setup_inputs(seed=0):
    import zlib

    import numpy as np

    out = dict(_drawn_inputs(seed))
    spreads = {'L1_attn_gq': (1.0, 0.6),
     'L1_attn_gk': (1.0, 0.6),
     'L1_attn_bo': (0.0, 0.1),
     'L1_ffn_b1': (0.0, 0.721),
     'L1_ffn_b2': (0.0, 0.1)}
    factors = {'L0_attn_time_first': 8.0,
     'L0_attn_time_mix_k': 8.0,
     'L0_attn_time_mix_v': 4.777,
     'L0_attn_time_mix_r': 8.0,
     'L0_attn_Wk': 8.0,
     'L0_attn_Wr': 8.0,
     'L0_ffn_in_bias': 2.733,
     'L1_attn_bk': 8.0,
     'L1_attn_bv': 4.352}
    for name, (base, spread) in spreads.items():
        noise = np.random.default_rng([zlib.crc32(name.encode()), seed]).standard_normal(out[name].shape)
        drawn = base * np.exp(spread * noise) if base else spread * noise
        out[name] = jnp.asarray(drawn.astype(out[name].dtype))
    for name, factor in factors.items():
        out[name] = (out[name] * factor).astype(out[name].dtype)
    return out
```

```python
from contextlib import ExitStack

import concourse.bass as bass
from concourse import mybir

ALU = mybir.AluOpType
ACT = mybir.ActivationFunctionType
AX = mybir.AxisListType
F32 = mybir.dt.float32
BF16 = mybir.dt.bfloat16
U32 = mybir.dt.uint32
I32 = mybir.dt.int32

P = 128
EPS = 1e-5
STATE_FLOOR = -1e38


class Chain:

    def __init__(self, engine, sem, per_round):
        self.engine, self.sem, self.per_round = engine, sem, per_round

    def begin(self, r):
        self.base, self.n = r * self.per_round, 0

    def link(self, ins, alone=None):
        self.n += 1
        ins.then_inc(self.sem, 1)
        self.engine.wait_ge(self.sem, self.base + self.n)
        if alone:
            alone(self.engine)

    def end(self):
        assert self.n == self.per_round, (self.n, self.per_round)


def build_tower(nc, a, out):
    NB, T2, C = a["x"].shape
    T = T2 // 2
    F = a["L0_ffn_upT"].shape[1]
    E = a["L1_ffn_routerT"].shape[1]
    HEADS, HD = 12, C // 12
    KC, CC = 2, C // 2
    G = 4
    NG = NB // G
    N = G * T
    FM = F // P
    HJ, HC = 4, HEADS // 4
    ET = 512
    ES = ET // P
    REGION = NB * T + ET
    NT = NB * T * 2 // ET + E - 1
    MAXT = NB * T // ET
    assert T == P and N == 512 and NT % 2 == 1

    rows_in = nc.dram_tensor("expert_rows_in", (E * REGION, C), F32).ap()
    rows_out = nc.dram_tensor("expert_rows_out", (NT * ET, C), F32).ap()
    h_kept = nc.dram_tensor("h_before_experts", (T, NB, C), F32).ap()

    with ExitStack() as ctx:
        def sb(name, shape, dt=F32):
            return ctx.enter_context(nc.sbuf_tensor(name, shape, dt))

        ps = ctx.enter_context(nc.psum_tensor("ps", [P, 8, 512], F32))

        ident = sb("ident", [P, P])
        slot_all = sb("slot_all", [P, NG, 2 * G], U32)
        weight_all = sb("weight_all", [P, NG, 2 * G])
        tile_row = sb("tile_row", [1, NT], I32)
        tile_exp = sb("tile_exp", [1, NT], I32)

        towers = ExitStack()

        def sg(name, shape, dt=F32):
            return towers.enter_context(nc.sbuf_tensor(name, shape, dt))

        before = sg("before", [P, P], BF16)
        ones_bf = sg("ones_bf", [P, P], BF16)
        neg_half = sg("neg_half", [P, 2 * G])
        lane8 = sg("lane8", [P, G, E])
        lane8_i = sg("lane8_i", [P, G, E], I32)
        region_off = sg("region_off", [P, G, E])
        region_i = sg("region_i", [P, G, E], I32)
        zero_rows = sg("zero_rows", [P, C])
        w_tok = sg("w_tok", [CC, KC, C])
        w_k = sg("w_k", [CC, KC, C])
        w_v = sg("w_v", [CC, KC, C])
        w_r = sg("w_r", [CC, KC, C])
        w_o = sg("w_o", [CC, KC, C])
        chan = sg("chan", [CC, 5, KC])
        decay = sg("decay", [CC, KC * G, T])
        w_up = sg("w_up", [CC, KC, F])
        b_up = sg("b_up", [P, FM])
        w_down = sg("w_down", [P, FM, C])
        w_qkv = sg("w_qkv", [CC + 1, KC, 3 * C])
        w_ao = sg("w_ao", [P, HC, C])
        gam = sg("gam", [P, 2, C])
        gamma = sg("gamma", [P, C])
        bo = sg("bo", [P, C])
        w_router = sg("w_router", [CC, KC, E])

        xt = sg("xt", [P, G, 2 * C])
        delta = sg("delta", [P, G, C])
        xsum = sg("xsum", [P, G, C])
        hA = sg("hA", [P, G, C])
        hnA = sg("hnA", [P, G, C])
        statsA = sg("statsA", [P, G, 6])
        mvA = sg("mvA", [P, G, 2])
        rstdA = sg("rstdA", [P, G])
        hTA = sg("hTA", [CC, KC * G, T + 1])
        tanh_r = sg("tanh_r", [CC, KC * N])
        o_s = sg("o_s", [CC, 1 + KC * N])
        p_s = sg("p_s", [CC, 1 + KC * N])
        q_s = sg("q_s", [CC, 1 + KC * N])
        sy = sg("sy", [CC, KC * N])
        buf = [sg(f"wkv{n}", [P, KC * N]) for n in range(6)]

        def flat(n):
            return buf[n][0:CC, :]

        def steps(n):
            return buf[n][0:CC, :].rearrange("p (s t) -> p s t", t=T)

        diff, z_s = steps(0), flat(0)
        xr, keep = flat(1), steps(1)
        xk, take = flat(2), flat(2)
        xv, take_v = flat(3), flat(3)
        dT, z_neg = flat(4), steps(4)
        tanh_d, z_pos = buf[5][:, 0:G * C].rearrange("p (t c) -> p t c", c=C), steps(5)

        hB = sg("hB", [P, G, C])
        hnB = sg("hnB", [P, G, C])
        resB = sg("resB", [P, G, C])
        statsB = sg("statsB", [P, G, 6])
        mvB = sg("mvB", [P, G, 2])
        rstdB = sg("rstdB", [P, G])
        hTB = sg("hTB", [CC + 1, KC, N])
        qk = sg("qk", [P, G, 2, C])
        v_s = sg("v_s", [P, G, C])
        stats_qk = sg("stats_qk", [P, 2 * G, 6])
        mv_qk = sg("mv_qk", [P, 2 * G, 2])
        rstd_qk = sg("rstd_qk", [P, 2 * G])
        qpad = sg("qpad", [P, G, HEADS, 32])
        kpad = sg("kpad", [P, G, HEADS, 32])
        qT = sg("qT", [P, G, HC * P])
        kT = sg("kT", [P, G, HC * P])
        probs = sg("probs", [P, G, HEADS, P])
        hid = probs[:, :, :, :].rearrange("p g h t -> p (g h t)")[:, 0:FM * N].rearrange("p (m n) -> p m n", n=N)
        nmax = sg("nmax", [P, G, HEADS])
        psums = sg("psums", [P, G, HEADS])
        rsums = sg("rsums", [P, G, HEADS])
        vpad = sg("vpad", [P, G, HEADS, 32])
        oT = sg("oT", [P, 2, HC * P])
        logits = sg("logits", [P, G * E])
        top8 = sg("top8", [P, G, 8])
        top_i = sg("top_i", [P, G, 8], U32)
        top_f = sg("top_f", [P, 2, G])
        gap = sg("gap", [P, G])
        egap = sg("egap", [P, G])
        esum = sg("esum", [P, G])
        hot = sg("hot", [P, 2, G, E])
        picked = sg("picked", [P, G, E], BF16)
        picked_f = sg("picked_f", [P, G, E])
        run_counts = sg("run_counts", [P, G + 1, E])
        run_bf = sg("run_bf", [P, G + 1, E], BF16)
        place = sg("place", [P, G * E])
        placed = sg("placed", [P, 2, G, E])
        slot_f = sg("slot_f", [P, 2 * G])
        slot_i = sg("slot_i", [P, 2 * G], U32)
        wts = sg("wts", [P, 2 * G])
        hnR = sg("hnR", [P, G, C])
        n_tok = sg("n_tok", [P, E])
        pad_i = sg("pad_i", [P, E, ES], I32)
        pad_f = sg("pad_f", [P, E, ES])
        pad_slot = sg("pad_slot", [P, E * ES], U32)
        mth_i = sg("mth_i", [P, E, MAXT], I32)
        mth = sg("mth", [P, E, MAXT])
        jth_i = sg("jth_i", [1, NT, E], I32)
        jth = sg("jth", [1, NT, E])
        n_tiles = sg("n_tiles", [P, E])
        shrink = sg("shrink", [P, E])
        reached = sg("reached", [P, NG * 2 * G, E])
        shift = sg("shift", [P, NG * 2 * G])
        one_row = sg("one_row", [1, E])
        tile_end = sg("tile_end", [1, E])
        passed = sg("passed", [1, NT, E])
        exp_f = sg("exp_f", [1, NT])
        off_f = sg("off_f", [1, NT])
        ok_f = sg("ok_f", [1, NT])

        towers.close()
        eup = [sb(f"eup{b}", [CC + 1, KC, F]) for b in range(2)]
        edown = [sb(f"edown{b}", [P, FM, C]) for b in range(2)]
        eb2 = [sb(f"eb2{b}", [P, C]) for b in range(2)]
        ex = [sb(f"ex{b}", [P, ES, C]) for b in range(2)]
        exT = [sb(f"exT{b}", [CC + 1, KC, ET]) for b in range(2)]
        ehid = [sb(f"ehid{b}", [P, FM, ET]) for b in range(2)]
        ey = [sb(f"ey{b}", [P, ES, C]) for b in range(2)]
        gy = [sb(f"gy{b}", [P, 2 * G, C]) for b in range(2)]
        hk = [sb(f"hk{b}", [P, G, C]) for b in range(2)]

        names = """weights_in passed gaps_zeroed pool_consts dve_consts
            x_loaded x_diffed x_summed dT_psum dT_ready tok_psum tanh_ready
            a_stats a_rstd a_hn a_hT_psum a_hT xr_ready xk_ready xv_ready r_psum k_psum v_psum tanh_r_ready
            keep_arg keep_ready take_arg take_ready z_ready zexp_ready frac_ready num_ready sy_ready
            oproj_psum hB_ready
            b_stats b_rstd b_hn b_hT_psum b_hT up_psum hid_ready down_psum
            res_ready qkv_psum qkv_out qk_stats qk_rstd q_norm k_norm k_scaled qkT_psum qT_ready kT_ready
            scores_psum max_ready exp_ready vpad_ready oT_psum oT_ready aproj_psum hF_ready h_stored
            logits_psum picked_ready place_psum gap_ready egap_ready slots_ready scattered
            counts_psum pads_ready pads_scattered table_ready
            e_xT_psum e_xT e_up_psum e_hid e_down_psum e_y e_stored
            g_out g_stored
            d_wkv d_tok d_b0 d_b1 d_b2 d_qk d_v d_route d_init d_table d_comb
            p_aln p_bln p_qln p_res p_init""".split()
        S = {n: ctx.enter_context(nc.semaphore(n)) for n in names}
        e_w = [ctx.enter_context(nc.semaphore(f"e_w{b}")) for b in range(2)]
        g_rows = [ctx.enter_context(nc.semaphore(f"g_rows{b}")) for b in range(2)]
        g_h = [ctx.enter_context(nc.semaphore(f"g_h{b}")) for b in range(2)]
        N_LOADS = 22
        PER_TILE = 5

        block = ctx.enter_context(nc.Block())

        def stand_alone(engine):
            engine.sem_inc(S["passed"], 1)

        @block.sync
        def _(sp):
            def chunked(ap):
                return ap.rearrange("(k p) n -> p k n", k=KC)

            def row(ap):
                return ap.rearrange("(o n) -> o n", o=1)

            loads = [
                (w_tok[:, :, :], chunked(a["L0_tok_w"])),
                (w_r[:, :, :], chunked(a["L0_attn_WrT"])),
                (w_k[:, :, :], chunked(a["L0_attn_WkT"])),
                (w_v[:, :, :], chunked(a["L0_attn_WvT"])),
                (w_o[:, :, :], chunked(a["L0_attn_WoT"])),
                (chan[:, :, :], a["L0_chan"]),
                (w_up[:, :, :], chunked(a["L0_ffn_upT"])),
                (b_up[:, :], a["L0_ffn_bias"]),
                (w_down[:, :, :], a["L0_ffn_out_weight"].rearrange("(m p) n -> p m n", p=P)),
                (w_qkv[0:CC, :, 0:C], chunked(a["L1_attn_WqT"])),
                (w_qkv[0:CC, :, C:2 * C], chunked(a["L1_attn_WkT"])),
                (w_qkv[0:CC, :, 2 * C:3 * C], chunked(a["L1_attn_WvT"])),
                (gam[:, 0, :], row(a["L1_attn_gq"]).to_broadcast([P, C])),
                (gam[:, 1, :], row(a["L1_attn_gk"]).to_broadcast([P, C])),
                (bo[:, :], row(a["L1_attn_bo"]).to_broadcast([P, C])),
                (w_router[:, :, :], chunked(a["L1_ffn_routerT"])),
            ]
            for dst, src in loads:
                sp.dma_start(dst, src).then_inc(S["weights_in"], 16)
            sp.wait_ge(S["gaps_zeroed"], 2)
            wo = a["L1_attn_WoT"].rearrange("(c j d) n -> j d c n", j=HJ, d=HD)
            gaps = [(w_ao[32 * j:32 * j + HD, :, :], wo[j]) for j in range(HJ)]
            gaps += [(w_qkv[CC:CC + 1, 0, C:2 * C], row(a["L1_attn_bk"])),
                     (w_qkv[CC:CC + 1, 0, 2 * C:3 * C], row(a["L1_attn_bv"]))]
            for dst, src in gaps:
                sp.dma_start(dst, src).then_inc(S["weights_in"], 16)
            assert len(loads) + len(gaps) == N_LOADS
            x_view = a["x"].rearrange("b (t two) c -> t b (two c)", two=2)

            def load_x(g):
                sp.wait_ge(S["x_diffed"], g)
                sp.wait_ge(S["x_summed"], g)
                sp.dma_start(xt[:, :, :], x_view[:, bass.ds(g * G, G), :]).then_inc(S["x_loaded"], 16)

            def store_h(g):
                sp.wait_ge(S["hF_ready"], g + 1)
                sp.dma_start(h_kept[:, bass.ds(g * G, G), :], hB[:, :, :]).then_inc(S["h_stored"], 16)

            load_x(0)
            load_x(1)
            with sp.Fori(1, NG - 1) as i:
                load_x(i + 1)
                store_h(i - 1)
            store_h(NG - 2)
            store_h(NG - 1)

            sp.wait_ge(S["h_stored"], 16 * NG)
            sp.wait_ge(S["table_ready"], 1)
            sp.wait_ge(S["scattered"], 16 * 2 * G * NG)
            sp.wait_ge(S["pads_scattered"], 16 * E * ES)

            def load_tile(j, b):
                e = sp.value_load(tile_exp[0:1, bass.ds(j, 1)], min_val=0, max_val=E - 1)
                at = sp.value_load(tile_row[0:1, bass.ds(j, 1)], min_val=0, max_val=E * REGION - ET)
                for dst, src in (
                    (eup[b][0:CC, :, :], a["L1_ffn_w1"][bass.ds(e * C, C), :].rearrange("(k p) n -> p k n", k=KC)),
                    (eup[b][CC:CC + 1, 0, :], a["L1_ffn_b1"][bass.ds(e, 1), :]),
                    (edown[b][:, :, :], a["L1_ffn_w2"][bass.ds(e * F, F), :].rearrange("(m p) n -> p m n", p=P)),
                    (eb2[b][:, :], a["L1_ffn_b2"][bass.ds(e, 1), :].to_broadcast([P, C])),
                    (ex[b][:, :, :], rows_in[bass.ds(at, ET), :].rearrange("(p s) c -> p s c", s=ES)),
                ):
                    sp.dma_start(dst, src).then_inc(e_w[b], 16)

            def store_tile(j, b):
                sp.wait_ge(S["e_y"], j + 1)
                sp.dma_start(rows_out[bass.ds(j * ET, ET), :].rearrange("(p s) c -> p s c", s=ES),
                             ey[b][:, :, :]).then_inc(S["e_stored"], 16)

            load_tile(0, 0)
            load_tile(1, 1)
            with sp.Fori(0, (NT - 3) // 2) as i:
                for b in range(2):
                    store_tile(2 * i + b, b)
                    load_tile(2 * i + b + 2, b)
            store_tile(NT - 3, 0)
            load_tile(NT - 1, 0)
            store_tile(NT - 2, 1)
            store_tile(NT - 1, 0)

            out_view = out.rearrange("b p c -> p b c")

            def load_h(g, b):
                sp.dma_start(hk[b][:, :, :], h_kept[:, bass.ds(g * G, G), :]).then_inc(g_h[b], 16)

            def store_out(g, b):
                sp.wait_ge(S["g_out"], g + 1)
                sp.dma_start(out_view[:, bass.ds(g * G, G), :], hk[b][:, :, :]).then_inc(S["g_stored"], 16)

            load_h(0, 0)
            load_h(1, 1)
            with sp.Fori(0, NG // 2 - 1) as i:
                for b in range(2):
                    store_out(2 * i + b, b)
                    sp.wait_ge(S["g_stored"], (2 * i + b + 1) * 16)
                    load_h(2 * i + b + 2, b)
            store_out(NG - 2, 0)
            store_out(NG - 1, 1)
            sp.wait_ge(S["g_stored"], 16 * NG)

        @block.tensor
        def _(pe):
            def transposes(src, bank):
                for t in range(G):
                    for k in range(KC):
                        last = nc.tensor.transpose(ps[0:CC, bank + k, t * T:(t + 1) * T],
                                                   src[:, t, k * CC:(k + 1) * CC], ident[:, :])
                return last

            def channels_out(bank, w, rhs):
                for m in range(KC):
                    for k in range(KC):
                        last = nc.tensor.matmul(ps[0:CC, bank + m, :], w[:, k, m * CC:(m + 1) * CC],
                                                rhs[:, k * N:(k + 1) * N], start=(k == 0), stop=(k == KC - 1))
                return last

            def tokens_out(bank, xT, w):
                for t in range(G):
                    o = ps[:, bank + t // 2, (t % 2) * C:(t % 2 + 1) * C]
                    for k in range(KC):
                        last = nc.tensor.matmul(o, xT[:, k * N + t * T:k * N + (t + 1) * T], w[:, k, :],
                                                start=(k == 0), stop=(k == KC - 1))
                return last

            def a_delta(g):
                pe.wait_ge(S["x_diffed"], g + 1)
                pe.wait_ge(S["hB_ready"], g)
                transposes(delta, 0).then_inc(S["dT_psum"], 1)

            def a_scores(g):
                pe.wait_ge(S["dT_ready"], g + 1)
                tokens_out(2, dT, w_tok).then_inc(S["tok_psum"], 1)

            def a_hidden(g):
                pe.wait_ge(S["a_hn"], g + 1)
                transposes(hnA, 0).then_inc(S["a_hT_psum"], 1)

            def a_rkv(g):
                pe.wait_ge(S["xr_ready"], g + 1)
                channels_out(2, w_r, xr).then_inc(S["r_psum"], 1)
                pe.wait_ge(S["xk_ready"], g + 1)
                channels_out(0, w_k, xk).then_inc(S["k_psum"], 1)
                pe.wait_ge(S["xv_ready"], g + 1)
                pe.wait_ge(S["tanh_r_ready"], g + 1)
                channels_out(2, w_v, xv).then_inc(S["v_psum"], 1)

            def a_project(g):
                pe.wait_ge(S["sy_ready"], g + 1)
                tokens_out(0, sy, w_o).then_inc(S["oproj_psum"], 1)

            def b_transposes(g, n, src):
                pe.wait_ge(S["b_hn"], 3 * g + n + 1)
                transposes(src, 4).then_inc(S["b_hT_psum"], 1)

            def b_mlp_up(g):
                pe.wait_ge(S["b_hT"], 3 * g + 1)
                for m in range(FM):
                    if m >= 4:
                        pe.wait_ge(S["hid_ready"], FM * g + m - 3)
                    for k in range(KC):
                        last = nc.tensor.matmul(ps[:, 4 + m % 4, :], w_up[:, k, m * P:(m + 1) * P],
                                                hTB[0:CC, k, :], start=(k == 0), stop=(k == KC - 1))
                    last.then_inc(S["up_psum"], 1)

            def b_mlp_down(g):
                pe.wait_ge(S["hid_ready"], FM * g + FM)
                for t in range(G):
                    for m in range(FM):
                        last = nc.tensor.matmul(ps[:, 4 + t // 2, (t % 2) * C:(t % 2 + 1) * C],
                                                hid[:, m, t * T:(t + 1) * T], w_down[:, m, :],
                                                start=(m == 0), stop=(m == FM - 1))
                last.then_inc(S["down_psum"], 1)

            def b_qkv(g):
                pe.wait_ge(S["b_hT"], 3 * g + 2)
                for t in range(G):
                    if t >= 2:
                        pe.wait_ge(S["qkv_out"], G * g + t - 1)
                    bank = 4 + 2 * (t % 2)
                    for k in range(KC):
                        r = CC + 1 if k == 0 else CC
                        nc.tensor.matmul(ps[:, bank, 0:2 * C], hTB[0:r, k, t * T:(t + 1) * T],
                                         w_qkv[0:r, k, 0:2 * C], start=(k == 0), stop=(k == KC - 1))
                    for k in range(KC):
                        r = CC + 1 if k == 0 else CC
                        last = nc.tensor.matmul(ps[:, bank + 1, 0:C], hTB[0:r, k, t * T:(t + 1) * T],
                                                w_qkv[0:r, k, 2 * C:3 * C], start=(k == 0), stop=(k == KC - 1))
                    last.then_inc(S["qkv_psum"], 1)

            def b_heads(g):
                pe.wait_ge(S["q_norm"], g + 1)
                pe.wait_ge(S["k_scaled"], g + 1)
                for t in range(G):
                    if t >= 2:
                        pe.wait_ge(S["qT_ready"], G * g + t - 1)
                        pe.wait_ge(S["kT_ready"], G * g + t - 1)
                    for n, src in enumerate((qpad, kpad)):
                        for c in range(HC):
                            last = nc.tensor.transpose(
                                ps[:, 4 + 2 * (t % 2) + n, c * P:(c + 1) * P],
                                src[:, t, HJ * c:HJ * c + HJ, :].rearrange("p h d -> p (h d)"), ident[:, :])
                    last.then_inc(S["qkT_psum"], 1)

            def b_scores(g, t, half):
                if t == 0:
                    pe.wait_ge(S["qT_ready"], G * g + G)
                    pe.wait_ge(S["kT_ready"], G * g + G)
                else:
                    pe.wait_ge(S["exp_ready"], 2 * G * g + 2 * (t - 1) + half + 1)
                for j in (2 * half, 2 * half + 1):
                    for c in range(HC):
                        last = nc.tensor.matmul(ps[:, 4 + j, c * P:(c + 1) * P],
                                                kT[32 * j:32 * j + HD, t, c * P:(c + 1) * P],
                                                qT[32 * j:32 * j + HD, t, c * P:(c + 1) * P],
                                                start=True, stop=True)
                last.then_inc(S["scores_psum"], 1)

            def b_values(g, t):
                pe.wait_ge(S["vpad_ready"], G * g + (G if t == 0 else t + 1))
                for c in range(HC):
                    for j in range(HJ):
                        last = nc.tensor.matmul(ps[32 * j:32 * j + 32, 4 + t % 2, c * P:(c + 1) * P],
                                                vpad[:, t, HC * j + c, :], probs[:, t, HC * j + c, :],
                                                start=True, stop=True)
                last.then_inc(S["oT_psum"], 1)

            def b_project(g, t):
                pe.wait_ge(S["oT_ready"], G * g + t + 1)
                for c in range(HC):
                    last = nc.tensor.matmul(ps[:, 6 + t // 2, (t % 2) * C:(t % 2 + 1) * C],
                                            oT[:, t % 2, c * P:(c + 1) * P], w_ao[:, c, :],
                                            start=(c == 0), stop=(c == HC - 1))
                if t == G - 1:
                    last.then_inc(S["aproj_psum"], 1)

            def b_logits(g):
                pe.wait_ge(S["b_hT"], 3 * g + 3)
                for t in range(G):
                    for k in range(KC):
                        last = nc.tensor.matmul(ps[:, 6, t * E:(t + 1) * E], hTB[0:CC, k, t * T:(t + 1) * T],
                                                w_router[:, k, :], start=(k == 0), stop=(k == KC - 1))
                last.then_inc(S["logits_psum"], 1)

            def b_places(g):
                pe.wait_ge(S["picked_ready"], g + 1)
                nc.tensor.matmul(ps[:, 7, 0:G * E], before[:, :], picked[:, :, :].rearrange("p t e -> p (t e)"),
                                 start=True, stop=False)
                nc.tensor.matmul(ps[:, 7, 0:G * E], ones_bf[:, :],
                                 run_bf[:, 0:G, :].rearrange("p t e -> p (t e)"),
                                 start=False, stop=True).then_inc(S["place_psum"], 1)

            def round_(ga, gb):
                A, B = ga is not None, gb is not None
                if A: a_delta(ga)
                if B: b_transposes(gb, 0, hnB)
                if A: a_scores(ga)
                if B: b_mlp_up(gb)
                if A: a_hidden(ga)
                if A: a_rkv(ga)
                if B: b_mlp_down(gb)
                if B: b_transposes(gb, 1, hnB)
                if B: b_qkv(gb)
                if B: b_heads(gb)
                if B:
                    for t in range(G):
                        for half in range(2):
                            b_scores(gb, t, half)
                    b_values(gb, 0)
                    for t in range(1, G):
                        b_values(gb, t)
                        b_project(gb, t - 1)
                    b_project(gb, G - 1)
                    b_transposes(gb, 2, hnR)
                    b_logits(gb)
                    b_places(gb)
                if A: a_project(ga)

            pe.wait_ge(S["weights_in"], 16 * N_LOADS)
            pe.wait_ge(S["pool_consts"], 1)
            pe.wait_ge(S["dve_consts"], 1)
            round_(0, None)
            round_(1, 0)
            with pe.Fori(2, NG) as i:
                round_(i, i - 1)
            round_(None, NG - 1)

            pe.wait_ge(S["slots_ready"], NG)
            nc.tensor.matmul(ps[:, 7, 0:E], ones_bf[:, :], run_bf[:, G, :],
                             start=True, stop=True).then_inc(S["counts_psum"], 1)

            def e_transposes(i, b):
                pe.wait_ge(e_w[b], (i + 1) * 16 * PER_TILE)
                for s in range(ES):
                    for k in range(KC):
                        last = nc.tensor.transpose(ps[0:CC, k, s * P:(s + 1) * P],
                                                   ex[b][:, s, k * CC:(k + 1) * CC], ident[:, :])
                last.then_inc(S["e_xT_psum"], 1)

            def e_up(j, b):
                pe.wait_ge(S["e_xT"], j + 1)
                for m in range(FM):
                    if m >= 4:
                        pe.wait_ge(S["e_hid"], FM * j + m - 3)
                    for k in range(KC):
                        r = CC + 1 if k == 0 else CC
                        last = nc.tensor.matmul(ps[:, 2 + m % 4, :], eup[b][0:r, k, m * P:(m + 1) * P],
                                                exT[b][0:r, k, :], start=(k == 0), stop=(k == KC - 1))
                    last.then_inc(S["e_up_psum"], 1)

            def e_down(j, b):
                pe.wait_ge(S["e_hid"], FM * j + FM)
                pe.wait_ge(S["e_y"], j)
                for s in range(ES):
                    for m in range(FM):
                        last = nc.tensor.matmul(ps[:, 6 + s // 2, (s % 2) * C:(s % 2 + 1) * C],
                                                ehid[b][:, m, s * P:(s + 1) * P], edown[b][:, m, :],
                                                start=(m == 0), stop=(m == FM - 1))
                last.then_inc(S["e_down_psum"], 1)

            def e_pair(i):
                e_up(2 * i, 0)
                e_transposes(i, 1)
                e_down(2 * i, 0)
                e_up(2 * i + 1, 1)
                e_transposes(i + 1, 0)
                e_down(2 * i + 1, 1)

            e_transposes(0, 0)
            e_pair(0)
            with pe.Fori(1, (NT - 1) // 2) as i:
                e_pair(i)
            e_up(NT - 1, 0)
            e_down(NT - 1, 0)

        @block.scalar
        def _(act):
            def two(bank, rows, cols):
                return ps[0:rows, bank:bank + 2, 0:cols]

            def a_delta(g):
                act.wait_ge(S["dT_psum"], g + 1)
                nc.scalar.activation(dT.rearrange("p (k n) -> p k n", k=KC), two(0, CC, N),
                                     ACT.Copy).then_inc(S["dT_ready"], 1)

            def a_scores(g):
                act.wait_ge(S["tok_psum"], g + 1)
                nc.scalar.activation(tanh_d.rearrange("p (h t) c -> p h (t c)", h=2), two(2, P, 2 * C),
                                     ACT.Tanh, scale=0.5).then_inc(S["tanh_ready"], 1)

            def a_hidden(g):
                act.wait_ge(S["a_hT_psum"], g + 1)
                nc.scalar.activation(hTA[:, :, 1:T + 1],
                                     two(0, CC, N).rearrange("p k (g t) -> p (k g) t", t=T),
                                     ACT.Copy).then_inc(S["a_hT"], 1)

            def a_gate(g):
                act.wait_ge(S["r_psum"], g + 1)
                nc.scalar.activation(tanh_r[:, :].rearrange("p (k n) -> p k n", k=KC), two(2, CC, N),
                                     ACT.Tanh, scale=0.5).then_inc(S["tanh_r_ready"], 1)

            def a_exps(g):
                act.wait_ge(S["keep_arg"], g + 1)
                nc.scalar.activation(keep[:, :, 1:T], keep[:, :, 1:T], ACT.Exp).then_inc(S["keep_ready"], 1)
                act.wait_ge(S["take_arg"], g + 1)
                nc.scalar.activation(take, take, ACT.Exp).then_inc(S["take_ready"], 1)
                act.wait_ge(S["z_ready"], g + 1)
                nc.scalar.activation(z_neg[:, :, 1:T], z_neg[:, :, 1:T], ACT.Exp)
                nc.scalar.activation(z_pos[:, :, 1:T], z_pos[:, :, 1:T], ACT.Exp,
                                     scale=-1.0).then_inc(S["zexp_ready"], 1)

            def b_transposed(g, n):
                act.wait_ge(S["b_hT_psum"], 3 * g + n + 1)
                nc.scalar.activation(hTB[0:CC, :, :], two(4, CC, N), ACT.Copy).then_inc(S["b_hT"], 1)

            def b_gelu(g):
                for m in range(FM):
                    act.wait_ge(S["up_psum"], FM * g + m + 1)
                    nc.scalar.activation(hid[:, m, :], ps[:, 4 + m % 4, :], ACT.Gelu,
                                         bias=b_up[:, m:m + 1]).then_inc(S["hid_ready"], 1)

            def b_qkv(g):
                for t in range(G):
                    act.wait_ge(S["qkv_psum"], G * g + t + 1)
                    bank = 4 + 2 * (t % 2)
                    nc.scalar.activation(qk[:, t, :, :].rearrange("p n c -> p (n c)"), ps[:, bank, 0:2 * C], ACT.Copy)
                    nc.scalar.activation(v_s[:, t, :], ps[:, bank + 1, 0:C], ACT.Copy).then_inc(S["qkv_out"], 1)

            def b_heads(g):
                for t in range(G):
                    act.wait_ge(S["qkT_psum"], G * g + t + 1)
                    nc.scalar.activation(qT[:, t, :], ps[:, 4 + 2 * (t % 2), 0:HC * P],
                                         ACT.Copy).then_inc(S["qT_ready"], 1)

            def b_exps(g, t, half):
                act.wait_ge(S["max_ready"], 2 * G * g + 2 * t + half + 1)
                for j in (2 * half, 2 * half + 1):
                    for c in range(HC):
                        n = HC * j + c
                        last = nc.scalar.activation(probs[:, t, n, :], ps[:, 4 + j, c * P:(c + 1) * P], ACT.Exp,
                                                    bias=nmax[:, t, n:n + 1], accum_out=psums[:, t, n:n + 1])
                last.then_inc(S["exp_ready"], 1)

            def b_values(g, t):
                act.wait_ge(S["oT_psum"], G * g + t + 1)
                nc.scalar.activation(oT[:, t % 2, :], ps[:, 4 + t % 2, 0:HC * P],
                                     ACT.Copy).then_inc(S["oT_ready"], 1)

            def b_gap(g):
                act.wait_ge(S["gap_ready"], g + 1)
                nc.scalar.activation(egap[:, :], gap[:, :], ACT.Exp).then_inc(S["egap_ready"], 1)

            def round_(ga, gb):
                A, B = ga is not None, gb is not None
                if A: a_delta(ga)
                if B: b_transposed(gb, 0)
                if A: a_scores(ga)
                if B: b_gelu(gb)
                if A: a_hidden(ga)
                if A: a_gate(ga)
                if A: a_exps(ga)
                if B: b_transposed(gb, 1)
                if B: b_qkv(gb)
                if B: b_heads(gb)
                if B:
                    for t in range(G):
                        for half in range(2):
                            b_exps(gb, t, half)
                    for t in range(G):
                        b_values(gb, t)
                    b_transposed(gb, 2)
                    b_gap(gb)

            act.wait_ge(S["weights_in"], 16 * N_LOADS)
            act.wait_ge(S["dve_consts"], 1)
            round_(0, None)
            round_(1, 0)
            with act.Fori(2, NG) as i:
                round_(i, i - 1)
            round_(None, NG - 1)

            def e_gelu(j, b):
                for m in range(FM):
                    act.wait_ge(S["e_up_psum"], FM * j + m + 1)
                    nc.scalar.activation(ehid[b][:, m, :], ps[:, 2 + m % 4, :],
                                         ACT.Gelu).then_inc(S["e_hid"], 1)

            with act.Fori(0, (NT - 1) // 2) as i:
                for b in range(2):
                    e_gelu(2 * i + b, b)
            e_gelu(NT - 1, 0)

        @block.gpsimd
        def _(pool):
            init = Chain(pool, S["p_init"], 10)
            init.begin(0)
            nc.gpsimd.memset(w_ao[:, :, :], 0.0).then_inc(S["gaps_zeroed"], 1)
            pool.wait_ge(S["gaps_zeroed"], 1)
            nc.gpsimd.memset(w_qkv[CC:CC + 1, 0, :], 0.0).then_inc(S["gaps_zeroed"], 1)
            pool.wait_ge(S["gaps_zeroed"], 2)
            init.link(nc.gpsimd.memset(ident[:, :], 0.0))
            init.link(nc.gpsimd.memset(ones_bf[:, :], 1.0))
            init.link(nc.gpsimd.affine_select(out=ident[:, :], in_=ident[:, :], compare_op=ALU.not_equal, fill=1.0,
                                              base=0, pattern=[[-1, P]], channel_multiplier=1))
            init.link(nc.gpsimd.affine_select(out=before[:, :], in_=ones_bf[:, :], compare_op=ALU.is_gt, fill=0.0,
                                              base=0, pattern=[[1, P]], channel_multiplier=-1))
            init.link(nc.gpsimd.memset(neg_half[:, :], -0.5))
            init.link(nc.gpsimd.iota(lane8_i[:, :, :], [[0, G], [1, E]], base=0, channel_multiplier=0))
            init.link(nc.gpsimd.iota(region_i[:, :, :], [[0, G], [REGION, E]], base=0, channel_multiplier=0))
            init.link(nc.gpsimd.iota(pad_i[:, :, :], [[0, E], [P, ES]], base=0, channel_multiplier=1))
            init.link(nc.gpsimd.iota(mth_i[:, :, :], [[0, E], [ET, MAXT]], base=0, channel_multiplier=0))
            init.link(nc.gpsimd.iota(jth_i[:, :, :], [[1, NT], [0, E]], base=0, channel_multiplier=0))
            init.end()
            nc.gpsimd.memset(zero_rows[:, :], 0.0).then_inc(S["pool_consts"], 1)
            pool.wait_ge(S["weights_in"], 16 * N_LOADS)
            pool.wait_ge(S["dve_consts"], 1)

            aln = Chain(pool, S["p_aln"], 1)
            bln = Chain(pool, S["p_bln"], 3)
            qln = Chain(pool, S["p_qln"], 1)
            res = Chain(pool, S["p_res"], 1)

            def rstd(chain, out_, mv, n):
                stand_alone(pool)
                chain.link(nc.gpsimd.tensor_scalar(out_, mv[:, :, 1], EPS, None, ALU.add))
                return nc.gpsimd.tensor_tensor(out_, out_, neg_half[:, 0:n], ALU.pow)

            def a_sum(g):
                pool.wait_ge(S["x_loaded"], 16 * (g + 1))
                pool.wait_ge(S["a_stats"], g)
                nc.gpsimd.tensor_tensor(xsum[:, :, :], xt[:, :, 0:C], xt[:, :, C:2 * C],
                                        ALU.add).then_inc(S["x_summed"], 1)

            def a_norm(g):
                pool.wait_ge(S["a_stats"], g + 1)
                aln.begin(g)
                rstd(aln, rstdA[:, :], mvA, G).then_inc(S["a_rstd"], 1)
                aln.end()

            def a_num(g):
                pool.wait_ge(S["frac_ready"], g + 1)
                nc.gpsimd.tensor_tensor(take_v, take_v, take, ALU.add).then_inc(S["num_ready"], 1)

            def b_norm(g, n):
                if n == 0:
                    bln.begin(g)
                pool.wait_ge(S["b_stats"], 3 * g + n + 1)
                rstd(bln, rstdB[:, :], mvB, G).then_inc(S["b_rstd"], 1)
                if n == 2:
                    bln.end()

            def b_residual(g):
                pool.wait_ge(S["b_hn"], 3 * g + 2)
                res.begin(g)
                res.link(nc.gpsimd.tensor_tensor(resB[:, :, :], hB[:, :, :], hnB[:, :, :], ALU.add))
                res.end()
                nc.gpsimd.tensor_tensor(resB[:, :, :], resB[:, :, :],
                                        bo[:, :].rearrange("p (o c) -> p o c", o=1).to_broadcast([P, G, C]),
                                        ALU.add).then_inc(S["res_ready"], 1)

            def b_qk_norm(g):
                pool.wait_ge(S["qk_stats"], g + 1)
                qln.begin(g)
                rstd(qln, rstd_qk[:, :], mv_qk, 2 * G).then_inc(S["qk_rstd"], 1)
                qln.end()

            def b_k_scale(g):
                pool.wait_ge(S["k_norm"], g + 1)
                for t in range(G):
                    last = nc.gpsimd.tensor_tensor(kpad[:, t, :, 0:HD], kpad[:, t, :, 0:HD],
                                                   gamma[:, :].rearrange("p (h d) -> p h d", d=HD), ALU.mult)
                last.then_inc(S["k_scaled"], 1)

            def b_scatter(g):
                pool.wait_ge(S["slots_ready"], g + 1)
                stand_alone(pool)
                for s in range(2):
                    for t in range(G):
                        n = s * G + t
                        nc.gpsimd.indirect_dma_start(
                            rows_in, bass.IndirectOffsetOnAxis(ap=slot_i[:, n:n + 1], axis=0),
                            hnR[:, t, :], None).then_inc(S["scattered"], 16)

            def round_(ga, gb):
                A, B = ga is not None, gb is not None
                if A: a_sum(ga)
                if B: b_norm(gb, 0)
                if A: a_norm(ga)
                if B: b_norm(gb, 1)
                if B: b_residual(gb)
                if B: b_qk_norm(gb)
                if B: b_k_scale(gb)
                if A: a_num(ga)
                if B: b_norm(gb, 2)
                if B: b_scatter(gb)

            round_(0, None)
            round_(1, 0)
            with pool.Fori(2, NG) as i:
                round_(i, i - 1)
            round_(None, NG - 1)

            pool.wait_ge(S["pads_ready"], 1)
            for n in range(E * ES):
                nc.gpsimd.indirect_dma_start(rows_in, bass.IndirectOffsetOnAxis(ap=pad_slot[:, n:n + 1], axis=0),
                                             zero_rows[:, :], None).then_inc(S["pads_scattered"], 16)

            pool.wait_ge(S["e_stored"], 16 * NT)
            for g in range(NG):
                b = g % 2
                if g >= 2:
                    pool.wait_ge(S["g_out"], g - 1)
                for n in range(2 * G):
                    nc.gpsimd.indirect_dma_start(
                        gy[b][:, n, :], None, rows_out,
                        bass.IndirectOffsetOnAxis(ap=slot_all[:, g, n:n + 1], axis=0)).then_inc(g_rows[b], 16)

        @block.vector
        def _(dve):
            init = Chain(dve, S["d_init"], 3)
            init.begin(0)
            nc.vector.memset(hTA[:, :, 0:1], 0.0)
            nc.vector.memset(o_s[:, 0:1], 0.0)
            nc.vector.memset(p_s[:, 0:1], 0.0)
            nc.vector.memset(q_s[:, 0:1], 0.0)
            nc.vector.memset(run_counts[:, :, :], 0.0)
            nc.vector.memset(qpad[:, :, :, :], 0.0)
            nc.vector.memset(kpad[:, :, :, :], 0.0)
            nc.vector.memset(vpad[:, :, :, :], 0.0)
            nc.vector.memset(one_row[:, :], 1.0)
            init.link(nc.vector.memset(hTB[CC:CC + 1, :, :], 1.0))
            dve.wait_ge(S["weights_in"], 16 * N_LOADS)
            dve.wait_ge(S["pool_consts"], 1)
            for k in range(KC):
                nc.vector.tensor_copy(decay[:, k * G:(k + 1) * G, :].rearrange("p g t -> p (g t)"),
                                      chan[:, 0, k:k + 1].to_broadcast([CC, N]))
            nc.vector.scalar_tensor_tensor(gamma[:, :], gam[:, 0, :], float(HD) ** -0.5, gam[:, 1, :],
                                           ALU.mult, ALU.mult)
            nc.vector.tensor_copy(lane8[:, :, :], lane8_i[:, :, :])
            nc.vector.tensor_copy(pad_f[:, :, :], pad_i[:, :, :])
            nc.vector.tensor_copy(mth[:, :, :], mth_i[:, :, :])
            nc.vector.tensor_copy(jth[:, :, :], jth_i[:, :, :])
            init.link(nc.vector.tensor_copy(region_off[:, :, :], region_i[:, :, :]))
            init.link(nc.vector.memset(decay[:, :, 0:1], STATE_FLOOR))
            nc.vector.tensor_tensor(pad_f[:, :, :], pad_f[:, :, :],
                                    region_off[:, 0, :].rearrange("p (e o) -> p e o", o=1).to_broadcast([P, E, ES]),
                                    ALU.add).then_inc(S["dve_consts"], 1)
            init.end()

            tok = Chain(dve, S["d_tok"], 4)
            wkv = Chain(dve, S["d_wkv"], 8)
            ln = [Chain(dve, S["d_b0"], 1), Chain(dve, S["d_b1"], 2), Chain(dve, S["d_b2"], 1)]
            qkc = Chain(dve, S["d_qk"], 1)
            vch = Chain(dve, S["d_v"], G)
            route = Chain(dve, S["d_route"], 17)

            def statistics(chain, src, st, mv, n):
                for t in range(n):
                    last = nc.vector.bn_stats(st[:, t, :], src(t))
                chain.link(last, stand_alone)
                for t in range(n):
                    last = nc.vector.bn_aggr(mv[:, t, :], st[:, t, :])
                return last

            def normalise(dst, src, mv, rs, ts):
                for n, t in enumerate(ts):
                    last = nc.vector.tensor_scalar(dst(n), src(n), mv[:, t, 0:1], rs[:, t:t + 1],
                                                   ALU.subtract, ALU.mult)
                return last

            def a_delta(g):
                dve.wait_ge(S["x_loaded"], 16 * (g + 1))
                nc.vector.tensor_tensor(delta[:, :, :], xt[:, :, 0:C], xt[:, :, C:2 * C],
                                        ALU.subtract).then_inc(S["x_diffed"], 1)

            def a_tokens(g):
                dve.wait_ge(S["tanh_ready"], g + 1)
                tok.begin(g)
                tok.link(nc.vector.scalar_tensor_tensor(tanh_d, tanh_d, 0.5, delta[:, :, :], ALU.mult, ALU.mult))
                dve.wait_ge(S["x_summed"], g + 1)
                tok.link(nc.vector.scalar_tensor_tensor(hA[:, :, :], xsum[:, :, :], 0.5, tanh_d, ALU.mult, ALU.add))
                statistics(tok, lambda t: hA[:, t, :], statsA, mvA, G).then_inc(S["a_stats"], 1)
                dve.wait_ge(S["a_rstd"], g + 1)
                normalise(lambda t: hnA[:, t, :], lambda t: hA[:, t, :], mvA, rstdA,
                          range(G)).then_inc(S["a_hn"], 1)

            def a_mix(g):
                dve.wait_ge(S["a_hT"], g + 1)
                tok.link(nc.vector.tensor_tensor(diff, hTA[:, :, 1:T + 1], hTA[:, :, 0:T], ALU.subtract))
                tok.end()
                for mix, dst, name in ((4, xr, "xr_ready"), (2, xk, "xk_ready"), (3, xv, "xv_ready")):
                    for k in range(KC):
                        last = nc.vector.scalar_tensor_tensor(
                            dst[:, k * N:(k + 1) * N].rearrange("p (g t) -> p g t", t=T),
                            diff[:, k * G:(k + 1) * G, :], chan[:, mix, k:k + 1],
                            hTA[:, k * G:(k + 1) * G, 0:T], ALU.mult, ALU.add)
                    last.then_inc(S[name], 1)

            k_ps = ps[0:CC, 0:2, :].rearrange("p k n -> p (k n)")
            v_ps = ps[0:CC, 2:4, :].rearrange("p k n -> p (k n)")
            M = KC * N
            keep_flat = flat(1)
            z_neg_flat, z_pos_flat = flat(4), flat(5)

            def a_exponents(g):
                dve.wait_ge(S["k_psum"], g + 1)
                wkv.begin(g)
                wkv.link(nc.vector.tensor_tensor_scan(o_s[:, 1:M + 1], decay[:, :, :].rearrange("p g t -> p (g t)"),
                                                      k_ps, 0.0, ALU.add, ALU.max))
                for k in range(KC):
                    nc.vector.scalar_tensor_tensor(
                        keep[:, k * G:(k + 1) * G, 1:T],
                        o_s[:, k * N:(k + 1) * N].rearrange("p (g t) -> p g t", t=T)[:, :, 1:T],
                        chan[:, 0, k:k + 1],
                        o_s[:, 1 + k * N:1 + (k + 1) * N].rearrange("p (g t) -> p g t", t=T)[:, :, 1:T],
                        ALU.add, ALU.subtract)
                nc.vector.memset(keep[:, :, 0:1], 0.0).then_inc(S["keep_arg"], 1)
                nc.vector.tensor_tensor(take, k_ps, o_s[:, 1:M + 1], ALU.subtract).then_inc(S["take_arg"], 1)
                for k in range(KC):
                    last = nc.vector.scalar_tensor_tensor(z_s[:, k * N:(k + 1) * N], ps[0:CC, k, :],
                                                          chan[:, 1, k:k + 1], o_s[:, k * N:(k + 1) * N],
                                                          ALU.add, ALU.subtract)
                wkv.link(last)
                z_steps = steps(0)
                nc.vector.tensor_scalar(z_neg[:, :, 1:T], z_steps[:, :, 1:T], 0.0, None, ALU.min)
                nc.vector.tensor_scalar(z_pos[:, :, 1:T], z_steps[:, :, 1:T], 0.0, None, ALU.max)
                nc.vector.memset(z_neg[:, :, 0:1], 1.0)
                nc.vector.memset(z_pos[:, :, 0:1], 0.0).then_inc(S["z_ready"], 1)

            def a_scans(g):
                dve.wait_ge(S["take_ready"], g + 1)
                dve.wait_ge(S["v_psum"], g + 1)
                wkv.link(nc.vector.tensor_tensor(take_v, take, v_ps, ALU.mult))
                dve.wait_ge(S["keep_ready"], g + 1)
                nc.vector.tensor_tensor_scan(p_s[:, 1:M + 1], keep_flat, take_v, 0.0, ALU.mult, ALU.add)
                wkv.link(nc.vector.tensor_tensor_scan(q_s[:, 1:M + 1], keep_flat, take, 0.0, ALU.mult, ALU.add))

            def a_fraction(g):
                dve.wait_ge(S["zexp_ready"], g + 1)
                nc.vector.tensor_tensor(take, z_neg_flat, v_ps, ALU.mult)
                nc.vector.tensor_tensor(take_v, z_pos_flat, p_s[:, 0:M], ALU.mult).then_inc(S["frac_ready"], 1)
                wkv.link(nc.vector.tensor_tensor(keep_flat, z_pos_flat, q_s[:, 0:M], ALU.mult))
                wkv.link(nc.vector.tensor_tensor(keep_flat, keep_flat, z_neg_flat, ALU.add))

            def a_reciprocal(g, n):
                q = M // 4
                last = nc.vector.reciprocal(keep_flat[:, n * q:(n + 1) * q], keep_flat[:, n * q:(n + 1) * q])
                if n == 3:
                    wkv.link(last)

            def a_gate(g):
                dve.wait_ge(S["num_ready"], g + 1)
                dve.wait_ge(S["tanh_r_ready"], g + 1)
                wkv.link(nc.vector.scalar_tensor_tensor(take, tanh_r[:, :], 1.0, take_v, ALU.add, ALU.mult))
                wkv.end()
                nc.vector.tensor_tensor(sy[:, :], take, keep_flat, ALU.mult).then_inc(S["sy_ready"], 1)

            def a_residual(g):
                dve.wait_ge(S["oproj_psum"], g + 1)
                dve.wait_ge(S["h_stored"], 16 * g)
                nc.vector.scalar_tensor_tensor(
                    hB[:, :, :].rearrange("p (h t) c -> p h (t c)", h=2), ps[:, 0:2, 0:2 * C], 0.5,
                    hA[:, :, :].rearrange("p (h t) c -> p h (t c)", h=2), ALU.mult, ALU.add).then_inc(S["hB_ready"], 1)

            def b_norm(g, n, dst):
                statistics(ln[n], lambda t: hB[:, t, :], statsB, mvB, G).then_inc(S["b_stats"], 1)
                dve.wait_ge(S["b_rstd"], 3 * g + n + 1)
                normalise(lambda t: dst[:, t, :], lambda t: hB[:, t, :], mvB, rstdB,
                          range(G)).then_inc(S["b_hn"], 1)

            def b_norm0(g):
                dve.wait_ge(S["hB_ready"], g + 1)
                ln[0].begin(g)
                b_norm(g, 0, hnB)
                ln[0].end()

            def b_mlp_add(g):
                dve.wait_ge(S["down_psum"], g + 1)
                ln[1].begin(g)
                h2 = hB[:, :, :].rearrange("p (h t) c -> p h (t c)", h=2)
                ln[1].link(nc.vector.tensor_tensor(h2, ps[:, 4:6, 0:2 * C], h2, ALU.add))
                b_norm(g, 1, hnB)
                ln[1].end()

            def b_qk_norm(g):
                dve.wait_ge(S["qkv_out"], G * g + G)
                qkc.begin(g)
                statistics(qkc, lambda n: qk[:, n // 2, n % 2, :], stats_qk, mv_qk, 2 * G).then_inc(S["qk_stats"], 1)
                qkc.end()
                dve.wait_ge(S["qk_rstd"], g + 1)

                def heads(ap):
                    return ap.rearrange("p (h d) -> p h d", d=HD)

                normalise(lambda t: kpad[:, t, :, 0:HD], lambda t: heads(qk[:, t, 1, :]), mv_qk, rstd_qk,
                          range(1, 2 * G, 2)).then_inc(S["k_norm"], 1)
                normalise(lambda t: qpad[:, t, :, 0:HD], lambda t: heads(qk[:, t, 0, :]), mv_qk, rstd_qk,
                          range(0, 2 * G, 2)).then_inc(S["q_norm"], 1)

            def b_heads(g):
                for t in range(G):
                    dve.wait_ge(S["qkT_psum"], G * g + t + 1)
                    nc.vector.tensor_copy(kT[:, t, :], ps[:, 5 + 2 * (t % 2), 0:HC * P]).then_inc(S["kT_ready"], 1)

            def b_max(g, t, half):
                dve.wait_ge(S["scores_psum"], 2 * G * g + 2 * t + half + 1)
                nc.vector.tensor_reduce(nmax[:, t, 6 * half:6 * half + 6],
                                        ps[:, 4 + 2 * half:6 + 2 * half, 0:HC * P].rearrange(
                                            "p j (c q) -> p j c q", q=P),
                                        AX.X, ALU.max, negate=True).then_inc(S["max_ready"], 1)

            def b_values(g, t):
                if t == 0:
                    vch.begin(g)
                dve.wait_ge(S["exp_ready"], 2 * G * g + 2 * t + 2)
                vch.link(nc.vector.reciprocal(rsums[:, t, :], psums[:, t, :]))
                nc.vector.tensor_tensor(
                    vpad[:, t, :, 0:HD].rearrange("p (j c) d -> p j c d", j=HJ),
                    v_s[:, t, :].rearrange("p (c j d) -> p j c d", j=HJ, d=HD),
                    rsums[:, t, :].rearrange("p (j c o) -> p j c o", j=HJ, o=1).to_broadcast([P, HJ, HC, HD]),
                    ALU.mult).then_inc(S["vpad_ready"], 1)
                if t == G - 1:
                    vch.end()

            def b_attn_add(g):
                dve.wait_ge(S["aproj_psum"], g + 1)
                dve.wait_ge(S["res_ready"], g + 1)
                nc.vector.tensor_tensor(hB[:, :, :].rearrange("p (h t) c -> p h (t c)", h=2),
                                        ps[:, 6:8, 0:2 * C],
                                        resB[:, :, :].rearrange("p (h t) c -> p h (t c)", h=2),
                                        ALU.add).then_inc(S["hF_ready"], 1)
                dve.wait_ge(S["hF_ready"], g + 1)
                dve.wait_ge(S["scattered"], 16 * 2 * G * g)
                ln[2].begin(g)
                b_norm(g, 2, hnR)
                ln[2].end()

            def b_route(g):
                link = route.link
                route.begin(g)
                dve.wait_ge(S["logits_psum"], g + 1)
                link(nc.vector.tensor_copy(logits[:, :], ps[:, 6, 0:G * E]), stand_alone)
                for t in range(G):
                    last = nc.vector.max(top8[:, t, :], logits[:, t * E:(t + 1) * E])
                link(last, stand_alone)
                for t in range(G):
                    last = nc.vector.max_index(top_i[:, t, :], top8[:, t, :], logits[:, t * E:(t + 1) * E])
                link(last)
                nc.vector.tensor_tensor(gap[:, :], top8[:, :, 1], top8[:, :, 0],
                                        ALU.subtract).then_inc(S["gap_ready"], 1)
                link(nc.vector.tensor_copy(top_f[:, :, :], top_i[:, :, 0:2].rearrange("p t s -> p s t")))
                for s in range(2):
                    last = nc.vector.tensor_tensor(
                        hot[:, s, :, :], lane8[:, :, :],
                        top_f[:, s, :].rearrange("p (t o) -> p t o", o=1).to_broadcast([P, G, E]), ALU.is_equal)
                link(last)
                nc.vector.tensor_copy(run_counts[:, 0, :], run_counts[:, G, :])
                nc.vector.tensor_tensor(picked[:, :, :], hot[:, 0, :, :], hot[:, 1, :, :], ALU.add)
                link(nc.vector.tensor_tensor(picked_f[:, :, :], hot[:, 0, :, :], hot[:, 1, :, :], ALU.add))
                for t in range(G):
                    link(nc.vector.tensor_tensor(run_counts[:, t + 1, :], run_counts[:, t, :], picked_f[:, t, :],
                                                 ALU.add))
                nc.vector.tensor_copy(run_bf[:, :, :], run_counts[:, :, :]).then_inc(S["picked_ready"], 1)
                dve.wait_ge(S["egap_ready"], g + 1)
                link(nc.vector.tensor_scalar(esum[:, :], egap[:, :], 1.0, None, ALU.add))
                link(nc.vector.reciprocal(wts[:, 0:G], esum[:, :]))
                link(nc.vector.tensor_tensor(wts[:, G:2 * G], wts[:, 0:G], egap[:, :], ALU.mult))
                dve.wait_ge(S["place_psum"], g + 1)
                link(nc.vector.tensor_tensor(place[:, :], ps[:, 7, 0:G * E],
                                             region_off[:, :, :].rearrange("p t e -> p (t e)"), ALU.add))
                for s in range(2):
                    last = nc.vector.tensor_tensor(placed[:, s, :, :], hot[:, s, :, :],
                                                   place[:, :].rearrange("p (t e) -> p t e", e=E), ALU.mult)
                link(last)
                link(nc.vector.tensor_reduce(slot_f[:, :], placed[:, :, :, :].rearrange("p s t e -> p (s t) e"),
                                             AX.X, ALU.add))
                link(nc.vector.tensor_copy(slot_i[:, :], slot_f[:, :]))
                nc.vector.tensor_copy(slot_all[:, bass.ds(g, 1), :].rearrange("p o n -> p (o n)"), slot_i[:, :])
                nc.vector.tensor_copy(weight_all[:, bass.ds(g, 1), :].rearrange("p o n -> p (o n)"),
                                      wts[:, :]).then_inc(S["slots_ready"], 1)
                route.end()

            def round_(ga, gb):
                A, B = ga is not None, gb is not None
                if A: a_delta(ga)
                if B: b_norm0(gb)
                if A: a_tokens(ga)
                if A: a_mix(ga)
                if A: a_exponents(ga)
                if B: b_mlp_add(gb)
                if A: a_scans(ga)
                if B: b_qk_norm(gb)
                if B: b_heads(gb)
                if A: a_fraction(ga)
                for t in range(G):
                    for half in range(2):
                        if B: b_max(gb, t, half)
                        if half == 0 and B and t > 0:
                            b_values(gb, t - 1)
                    if A: a_reciprocal(ga, t)
                if A: a_gate(ga)
                if B: b_values(gb, G - 1)
                if B: b_attn_add(gb)
                if B: b_route(gb)
                if A: a_residual(ga)

            round_(0, None)
            round_(1, 0)
            with dve.Fori(2, NG) as i:
                round_(i, i - 1)
            round_(None, NG - 1)

            table = Chain(dve, S["d_table"], 25)
            link = table.link
            table.begin(0)
            dve.wait_ge(S["counts_psum"], 1)
            link(nc.vector.tensor_copy(n_tok[:, :], ps[:, 7, 0:E]))
            link(nc.vector.tensor_tensor(pad_f[:, :, :], pad_f[:, :, :],
                                         n_tok[:, :].rearrange("p (e o) -> p e o", o=1).to_broadcast([P, E, ES]),
                                         ALU.add))
            nc.vector.tensor_copy(pad_slot[:, :], pad_f[:, :, :].rearrange("p e s -> p (e s)"))\
                .then_inc(S["pads_ready"], 1)
            link(nc.vector.tensor_tensor(mth[:, :, :], n_tok[:, :].rearrange("p (e o) -> p e o", o=1)
                                         .to_broadcast([P, E, MAXT]), mth[:, :, :], ALU.is_gt))
            link(nc.vector.tensor_reduce(n_tiles[:, :], mth[:, :, :], AX.X, ALU.add))
            link(nc.vector.tensor_tensor_scan(tile_end[:, :], one_row[:, :], n_tiles[0:1, :], 0.0, ALU.mult, ALU.add))
            link(nc.vector.tensor_tensor(passed[:, :, :], jth[:, :, :],
                                         tile_end[:, :].rearrange("p (o e) -> p o e", o=1).to_broadcast([1, NT, E]),
                                         ALU.is_ge))
            link(nc.vector.tensor_reduce(exp_f[:, :], passed[:, :, :], AX.X, ALU.add))
            link(nc.vector.tensor_tensor(passed[:, :, :], passed[:, :, :],
                                         n_tiles[0:1, :].rearrange("p (o e) -> p o e", o=1).to_broadcast([1, NT, E]),
                                         ALU.mult))
            link(nc.vector.tensor_reduce(off_f[:, :], passed[:, :, :], AX.X, ALU.add))
            link(nc.vector.tensor_tensor(off_f[:, :], jth[:, :, 0], off_f[:, :], ALU.subtract))
            link(nc.vector.tensor_scalar(ok_f[:, :], exp_f[:, :], float(E), None, ALU.is_lt))
            link(nc.vector.tensor_tensor(off_f[:, :], off_f[:, :], ok_f[:, :], ALU.mult))
            link(nc.vector.tensor_scalar(exp_f[:, :], exp_f[:, :], float(E - 1), None, ALU.min))
            link(nc.vector.tensor_copy(tile_exp[:, :], exp_f[:, :]))
            link(nc.vector.tensor_scalar(off_f[:, :], off_f[:, :], float(ET), None, ALU.mult))
            link(nc.vector.tensor_scalar(exp_f[:, :], exp_f[:, :], float(REGION), None, ALU.mult))
            link(nc.vector.tensor_tensor(off_f[:, :], off_f[:, :], exp_f[:, :], ALU.add))
            link(nc.vector.tensor_copy(tile_row[:, :], off_f[:, :]))
            slots = NG * 2 * G
            link(nc.vector.tensor_scalar(shrink[:, :], n_tiles[:, :], float(ET), float(-REGION), ALU.mult, ALU.add))
            slot_flat = slot_all[:, :, :].rearrange("p g n -> p (g n)")
            link(nc.vector.tensor_copy(shift[:, :], slot_flat))
            link(nc.vector.tensor_tensor(reached[:, :, 1:E],
                                         shift[:, :].rearrange("p (n o) -> p n o", o=1).to_broadcast([P, slots, E - 1]),
                                         region_off[:, 0, 1:E].rearrange("p (o e) -> p o e", o=1)
                                         .to_broadcast([P, slots, E - 1]), ALU.is_ge))
            link(nc.vector.tensor_tensor(reached[:, :, 1:E], reached[:, :, 1:E],
                                         shrink[:, 0:E - 1].rearrange("p (o e) -> p o e", o=1)
                                         .to_broadcast([P, slots, E - 1]), ALU.mult))
            link(nc.vector.tensor_copy(reached[:, :, 0], shift[:, :]))
            link(nc.vector.tensor_reduce(shift[:, :], reached[:, :, :], AX.X, ALU.add))
            link(nc.vector.tensor_copy(slot_flat, shift[:, :]))
            dve.wait_ge(S["scattered"], 16 * 2 * G * NG)
            dve.wait_ge(S["pads_scattered"], 16 * E * ES)
            dve.wait_ge(S["h_stored"], 16 * NG)
            for b in range(2):
                last = nc.vector.memset(exT[b][CC:CC + 1, :, :], 1.0)
            last.then_inc(S["table_ready"], 1)
            table.end()

            def e_rows(j, b):
                dve.wait_ge(S["e_xT_psum"], j + 1)
                nc.vector.tensor_copy(exT[b][0:CC, :, :], ps[0:CC, 0:2, :]).then_inc(S["e_xT"], 1)

            def e_result(j, b, head=False):
                dve.wait_ge(S["e_down_psum"], j + 1)
                if not head:
                    dve.wait_ge(S["e_stored"], (j - 1) * 16)
                for s in range(2):
                    last = nc.vector.tensor_tensor(
                        ey[b][:, 2 * s:2 * s + 2, :], ps[:, 6 + s, 0:2 * C].rearrange("p (t c) -> p t c", t=2),
                        eb2[b][:, :].rearrange("p (o c) -> p o c", o=1).to_broadcast([P, 2, C]), ALU.add)
                last.then_inc(S["e_y"], 1)

            e_rows(0, 0)
            e_rows(1, 1)
            e_result(0, 0, head=True)
            e_rows(2, 0)
            e_result(1, 1)
            with dve.Fori(1, (NT - 1) // 2) as i:
                for b in range(2):
                    e_rows(2 * i + b + 1, 1 - b)
                    e_result(2 * i + b, b)
            e_result(NT - 1, 0)

            comb = Chain(dve, S["d_comb"], 1)
            for g in range(NG):
                b = g % 2
                dve.wait_ge(g_rows[b], 16 * 2 * G * (g // 2 + 1))
                dve.wait_ge(g_h[b], 16 * (g // 2 + 1))
                comb.begin(g)
                for s in range(2):
                    for t in range(G):
                        n = s * G + t
                        last = nc.vector.scalar_tensor_tensor(hk[b][:, t, :], gy[b][:, n, :],
                                                              weight_all[:, g, n:n + 1], hk[b][:, t, :],
                                                              ALU.mult, ALU.add)
                    if s == 0:
                        comb.link(last)
                    else:
                        last.then_inc(S["g_out"], 1)
                comb.end()


def kernel(**inputs):
    import numpy as _np
    import concourse.bacc as _bacc
    from concourse import mybir as _mybir
    from concourse.bass_utils import run_bass_kernel_spmd as _run

    nc = _bacc.Bacc("TRN2", target_bir_lowering=False, num_devices=1)
    w = {k: _np.asarray(v) for k, v in inputs.items()}

    def chunks(v):
        return v.reshape(2, -1).T

    laid = {
        "x": w["x"],
        "L0_tok_w": w["L0_tok_w"],
        "L0_attn_WrT": w["L0_attn_Wr"].T, "L0_attn_WkT": w["L0_attn_Wk"].T,
        "L0_attn_WvT": w["L0_attn_Wv"].T, "L0_attn_WoT": w["L0_attn_Wo"].T,
        "L0_chan": _np.stack([chunks(w[n].reshape(-1)) for n in (
            "L0_attn_time_decay", "L0_attn_time_first", "L0_attn_time_mix_k",
            "L0_attn_time_mix_v", "L0_attn_time_mix_r")], axis=1),
        "L0_ffn_upT": w["L0_ffn_in_weight"].T,
        "L0_ffn_bias": w["L0_ffn_in_bias"].reshape(-1, 128).T,
        "L0_ffn_out_weight": w["L0_ffn_out_weight"],
        "L1_attn_WqT": w["L1_attn_Wq"].T, "L1_attn_WkT": w["L1_attn_Wk"].T,
        "L1_attn_WvT": w["L1_attn_Wv"].T, "L1_attn_WoT": w["L1_attn_Wo"].T,
        "L1_attn_gq": w["L1_attn_gq"], "L1_attn_gk": w["L1_attn_gk"],
        "L1_attn_bk": w["L1_attn_bk"], "L1_attn_bv": w["L1_attn_bv"], "L1_attn_bo": w["L1_attn_bo"],
        "L1_ffn_routerT": w["L1_ffn_router_w"].T,
        "L1_ffn_w1": w["L1_ffn_w1"].reshape(-1, w["L1_ffn_w1"].shape[-1]),
        "L1_ffn_b1": w["L1_ffn_b1"],
        "L1_ffn_w2": w["L1_ffn_w2"].reshape(-1, w["L1_ffn_w2"].shape[-1]),
        "L1_ffn_b2": w["L1_ffn_b2"],
    }
    arrays, args = {}, {}
    for name, v in laid.items():
        v = _np.ascontiguousarray(v)
        arrays[f"in_{name}"] = v
        args[name] = nc.dram_tensor(f"in_{name}", v.shape, _mybir.dt.from_np(v.dtype), kind="ExternalInput").ap()
    B, T2, C = w["x"].shape
    out = nc.dram_tensor("out_0", (B, T2 // 2, C), _mybir.dt.float32, kind="ExternalOutput").ap()
    build_tower(nc, args, out)
    return _run(nc, [arrays], core_ids=[0]).results[0]["out_0"]
```

```python
from contextlib import ExitStack

import concourse.bass as bass
from concourse import mybir

ALU = mybir.AluOpType
ACT = mybir.ActivationFunctionType
AX = mybir.AxisListType
F32 = mybir.dt.float32
F32R = mybir.dt.float32r
BF16 = mybir.dt.bfloat16
U32 = mybir.dt.uint32
I32 = mybir.dt.int32

P = 128
EPS = 1e-5
STATE_FLOOR = -1e38


class Chain:

    def __init__(self, engine, sem, per_round):
        self.engine, self.sem, self.per_round = engine, sem, per_round

    def begin(self, r):
        self.base, self.n = r * self.per_round, 0

    def link(self, ins, alone=None):
        self.n += 1
        ins.then_inc(self.sem, 1)
        self.engine.wait_ge(self.sem, self.base + self.n)
        if alone:
            alone(self.engine)

    def end(self):
        assert self.n == self.per_round, (self.n, self.per_round)


def build_tower(nc, a, out):
    NB, T2, C = a["x"].shape
    T = T2 // 2
    F = a["L0_ffn_upT"].shape[1]
    E = a["L1_ffn_routerT"].shape[1]
    HEADS, HD = 12, C // 12
    KC, CC = 2, C // 2
    G = 4
    NG = NB // G
    N = G * T
    FM = F // P
    HJ, HC = 4, HEADS // 4
    ET = 512
    ES = ET // P
    REGION = NB * T + ET
    NT = NB * T * 2 // ET + E - 1
    MAXT = NB * T // ET
    NBUF = 3
    INFO = 4
    assert T == P and N == 512 and NT % NBUF == 0

    rows_in = nc.dram_tensor("expert_rows_in", (E * REGION + ET, INFO + C), F32).ap()
    total = nc.dram_tensor("total", (NB * T + ET, C), F32).ap()

    with ExitStack() as ctx:
        def sb(name, shape, dt=F32):
            return ctx.enter_context(nc.sbuf_tensor(name, shape, dt))

        ps = ctx.enter_context(nc.psum_tensor("ps", [P, 8, 512], F32))

        ident = sb("ident", [P, P])
        tile_row = sb("tile_row", [1, NT], I32)
        tile_exp = sb("tile_exp", [1, NT], I32)
        expert_of = sb("expert_of", [P, NT])
        pad_row = sb("pad_row", [1, E], I32)

        towers = ExitStack()

        def sg(name, shape, dt=F32):
            return towers.enter_context(nc.sbuf_tensor(name, shape, dt))

        before = sg("before", [P, P], BF16)
        ones_bf = sg("ones_bf", [P, P], BF16)
        neg_half = sg("neg_half", [P, 2 * G])
        lane8 = sg("lane8", [P, G, E])
        lane8_i = sg("lane8_i", [P, G, E], I32)
        region_off = sg("region_off", [P, G, E])
        region_i = sg("region_i", [P, G, E], I32)
        w_tok = sg("w_tok", [CC, KC, C])
        w_k = sg("w_k", [CC, KC, C])
        w_v = sg("w_v", [CC, KC, C])
        w_r = sg("w_r", [CC, KC, C])
        w_o = sg("w_o", [CC, KC, C])
        chan = sg("chan", [CC, 5, KC])
        decay = sg("decay", [CC, KC * G, T])
        w_up = sg("w_up", [CC, KC, F])
        b_up = sg("b_up", [P, FM])
        w_down = sg("w_down", [P, FM, C])
        w_qkv = sg("w_qkv", [CC + 1, KC, 3 * C])
        w_ao = sg("w_ao", [P, HC, C])
        gam = sg("gam", [P, 2, C])
        gamma = sg("gamma", [P, C])
        bo = sg("bo", [P, C])
        w_router = sg("w_router", [CC, KC, E])

        xt = sg("xt", [P, G, 2 * C])
        delta = sg("delta", [P, G, C])
        xsum = sg("xsum", [P, G, C])
        hA = sg("hA", [P, G, C])
        hnA = sg("hnA", [P, G, C])
        statsA = sg("statsA", [P, G, 6])
        mvA = sg("mvA", [P, G, 2])
        rstdA = sg("rstdA", [P, G])
        hTA = sg("hTA", [CC, KC * G, T + 1])
        tanh_r = sg("tanh_r", [CC, KC * N])
        o_s = sg("o_s", [CC, 1 + KC * N])
        p_s = sg("p_s", [CC, 1 + KC * N])
        q_s = sg("q_s", [CC, 1 + KC * N])
        sy = sg("sy", [CC, KC * N])
        buf = [sg(f"wkv{n}", [P, KC * N]) for n in range(6)]

        def flat(n):
            return buf[n][0:CC, :]

        def steps(n):
            return buf[n][0:CC, :].rearrange("p (s t) -> p s t", t=T)

        diff, z_s = steps(0), flat(0)
        xr, keep = flat(1), steps(1)
        xk, take = flat(2), flat(2)
        xv, take_v = flat(3), flat(3)
        dT, z_neg = flat(4), steps(4)
        tanh_d, z_pos = buf[5][:, 0:G * C].rearrange("p (t c) -> p t c", c=C), steps(5)

        k_s = sg("k_s", [CC, KC * N])
        v_c = sg("v_c", [CC, KC * N])

        hB = sg("hB", [P, G, C])
        hnB = sg("hnB", [P, G, C])
        statsB = sg("statsB", [P, G, 6])
        mvB = sg("mvB", [P, G, 2])
        rstdB = sg("rstdB", [P, G])
        hTB = sg("hTB", [CC, KC, N])

        hC = sg("hC", [P, G, C])
        hnC = sg("hnC", [P, G, C])
        resC = sg("resC", [P, G, C])
        statsC = sg("statsC", [P, G, 6])
        mvC = sg("mvC", [P, G, 2])
        rstdC = sg("rstdC", [P, G])
        hTC = sg("hTC", [CC + 1, KC, N])
        statsR = sg("statsR", [P, G, 6])
        mvR = sg("mvR", [P, G, 2])
        rstdR = sg("rstdR", [P, G])
        qk = sg("qk", [P, G, 2, C])
        v_s = sg("v_s", [P, G, C])
        stats_qk = sg("stats_qk", [P, 2 * G, 6])
        mv_qk = sg("mv_qk", [P, 2 * G, 2])
        rstd_qk = sg("rstd_qk", [P, 2 * G])
        qpad = sg("qpad", [P, G, HEADS, 32])
        kpad = sg("kpad", [P, G, HEADS, 32])
        qT = sg("qT", [P, G, HC * P])
        kT = sg("kT", [P, G, HC * P])
        probs = sg("probs", [P, 2, HEADS, P])
        hid = sg("hid", [P, FM, N])
        nmax = sg("nmax", [P, G, HEADS])
        psums = sg("psums", [P, G, HEADS])
        rsums = sg("rsums", [P, G, HEADS])
        vpad = sg("vpad", [P, 2, HEADS, 32])
        oT = sg("oT", [P, 2, HC * P])
        logits = sg("logits", [P, G * E])
        top8 = sg("top8", [P, G, 8])
        top_i = sg("top_i", [P, G, 8], U32)
        top_f = sg("top_f", [P, 2, G])
        gap = sg("gap", [P, G])
        egap = sg("egap", [P, G])
        esum = sg("esum", [P, G])
        hot = sg("hot", [P, 2, G, E])
        picked = sg("picked", [P, G, E], BF16)
        picked_f = sg("picked_f", [P, G, E])
        run_counts = sg("run_counts", [P, G + 1, E])
        run_bf = sg("run_bf", [P, G + 1, E], BF16)
        place = sg("place", [P, G * E])
        placed = sg("placed", [P, 2, G, E])
        slot_f = sg("slot_f", [P, 2 * G])
        slot_i = sg("slot_i", [P, 2 * G], U32)
        wts = sg("wts", [P, 2 * G])
        rowR = sg("rowR", [P, G, INFO + C])
        hnR = rowR[:, :, INFO:INFO + C]
        token_i = sg("token_i", [P, G], I32)
        token_f = sg("token_f", [P, G])
        n_tok = sg("n_tok", [P, E])
        pad_token = sg("pad_token", [P, ES], I32)
        pad_tile = xt[:, :, 0:INFO + C]
        mth_i = sg("mth_i", [P, E, MAXT], I32)
        mth = sg("mth", [P, E, MAXT])
        jth_i = sg("jth_i", [P, NT, E], I32)
        jth = sg("jth", [P, NT, E])
        n_tiles = sg("n_tiles", [P, E])
        one_row = sg("one_row", [P, E])
        tile_end = sg("tile_end", [P, E])
        passed = hid[:, 0, 0:NT * E].rearrange("p (n e) -> p n e", e=E)
        exp_f = sg("exp_f", [P, NT])
        off_f = sg("off_f", [P, NT])
        ok_f = sg("ok_f", [P, NT])

        towers.close()
        def ring(name, shape, dt=F32):
            return [sb(f"{name}{b}", shape, dt) for b in range(NBUF)]

        eup = ring("eup", [CC + 1, KC, F])
        eup_hi = ring("eup_hi", [CC + 1, KC, F], F32R)
        eup_lo = ring("eup_lo", [CC + 1, KC, F], F32R)
        edown = ring("edown", [P, FM, C])
        eb2 = ring("eb2", [P, C])
        ex = ring("ex", [P, ES, INFO + C])
        exT_hi = ring("exT_hi", [CC + 1, KC, ET], F32R)
        exT_lo = ring("exT_lo", [CC + 1, KC, ET], F32R)
        ehid = ring("ehid", [P, FM, ET])
        ey = ring("ey", [P, ES, C])
        etoken = ring("etoken", [P, ES], U32)
        eweight = ring("eweight", [P, ES])
        first_is = ring("first_is", [P, ES])

        names = """weights_in passed gaps_zeroed pool_consts dve_consts
            x_loaded x_diffed x_summed dT_psum dT_ready tok_psum tanh_ready
            a_stats a_rstd a_hn a_hT_psum a_hT xr_ready xk_ready xv_ready r_psum k_psum v_psum
            tanh_r_ready k_ready v_ready
            keep_arg keep_ready take_arg take_ready z_ready zexp_ready frac_ready num_ready sy_ready
            oproj_psum hB_ready
            b_stats b_rstd b_hn b_hT_psum b_hT up_psum hid_ready down_psum hC_ready
            c_stats c_rstd c_hn c_hT_psum c_hT
            res_ready qkv_psum qkv_out qk_stats qk_rstd q_norm k_norm k_scaled qkT_psum qT_ready kT_ready
            scores_psum max_ready exp_ready vpad_ready oT_psum oT_ready aproj_psum hF_ready h_stored
            r_stats r_rstd r_hn r_hT_psum r_hT
            logits_psum picked_ready place_psum gap_ready egap_ready slots_ready scattered
            counts_psum pads_ready pads_stored table_ready
            w_high w_low e_xT_psum x_high x_low e_up_psum e_hid e_down_psum e_y e_added out_stored
            d_wkv d_tok d_b d_c d_r d_qk d_v d_route d_init d_table d_exp
            p_a p_b p_c p_r p_qk p_res p_init""".split()
        S = {n: ctx.enter_context(nc.semaphore(n)) for n in names}
        e_w = [ctx.enter_context(nc.semaphore(f"e_w{b}")) for b in range(NBUF)]
        N_LOADS = 22
        PER_TILE = 5

        block = ctx.enter_context(nc.Block())

        def stand_alone(engine):
            engine.sem_inc(S["passed"], 1)

        def stages(i):
            if isinstance(i, int):
                return [i - n if 0 <= i - n < NG else None for n in range(4)]
            return [i, i - 1, i - 2, i - 3]

        def rounds(engine, round_):
            for i in range(4):
                round_(i)
            with engine.Fori(4, NG) as i:
                round_(i)
            for i in range(NG, NG + 3):
                round_(i)

        def expert_tiles(engine, step):
            last = NT // NBUF - 1
            for b in range(NBUF):
                step(0, b)
            with engine.Fori(1, last) as i:
                for b in range(NBUF):
                    step(i, b)
            for b in range(NBUF):
                step(last, b)

        def is_first(i, b):
            return isinstance(i, int) and NBUF * i + b == 0

        def after(i, b):
            if isinstance(i, int) and NBUF * i + b == NT - 1:
                return None
            return (i, b + 1) if b + 1 < NBUF else (i + 1, 0)

        @block.sync
        def _(sp):
            def chunked(ap):
                return ap.rearrange("(k p) n -> p k n", k=KC)

            def row(ap):
                return ap.rearrange("(o n) -> o n", o=1)

            loads = [
                (w_tok[:, :, :], chunked(a["L0_tok_w"])),
                (w_r[:, :, :], chunked(a["L0_attn_WrT"])),
                (w_k[:, :, :], chunked(a["L0_attn_WkT"])),
                (w_v[:, :, :], chunked(a["L0_attn_WvT"])),
                (w_o[:, :, :], chunked(a["L0_attn_WoT"])),
                (chan[:, :, :], a["L0_chan"]),
                (w_up[:, :, :], chunked(a["L0_ffn_upT"])),
                (b_up[:, :], a["L0_ffn_bias"]),
                (w_down[:, :, :], a["L0_ffn_out_weight"].rearrange("(m p) n -> p m n", p=P)),
                (w_qkv[0:CC, :, 0:C], chunked(a["L1_attn_WqT"])),
                (w_qkv[0:CC, :, C:2 * C], chunked(a["L1_attn_WkT"])),
                (w_qkv[0:CC, :, 2 * C:3 * C], chunked(a["L1_attn_WvT"])),
                (gam[:, 0, :], row(a["L1_attn_gq"]).to_broadcast([P, C])),
                (gam[:, 1, :], row(a["L1_attn_gk"]).to_broadcast([P, C])),
                (bo[:, :], row(a["L1_attn_bo"]).to_broadcast([P, C])),
                (w_router[:, :, :], chunked(a["L1_ffn_routerT"])),
            ]
            for dst, src in loads:
                sp.dma_start(dst, src).then_inc(S["weights_in"], 16)
            sp.wait_ge(S["gaps_zeroed"], 2)
            wo = a["L1_attn_WoT"].rearrange("(c j d) n -> j d c n", j=HJ, d=HD)
            gaps = [(w_ao[32 * j:32 * j + HD, :, :], wo[j]) for j in range(HJ)]
            gaps += [(w_qkv[CC:CC + 1, 0, C:2 * C], row(a["L1_attn_bk"])),
                     (w_qkv[CC:CC + 1, 0, 2 * C:3 * C], row(a["L1_attn_bv"]))]
            for dst, src in gaps:
                sp.dma_start(dst, src).then_inc(S["weights_in"], 16)
            assert len(loads) + len(gaps) == N_LOADS
            x_view = a["x"].rearrange("b (t two) c -> t b (two c)", two=2)

            def load_x(g):
                sp.wait_ge(S["x_diffed"], g)
                sp.wait_ge(S["x_summed"], g)
                sp.dma_start(xt[:, :, :], x_view[:, bass.ds(g * G, G), :]).then_inc(S["x_loaded"], 16)

            total_view = total[0:NB * T, :].rearrange("(b p) c -> p b c", p=T)

            def store_h(g):
                sp.wait_ge(S["hF_ready"], g + 1)
                sp.dma_start(total_view[:, bass.ds(g * G, G), :], resC[:, :, :]).then_inc(S["h_stored"], 16)

            load_x(0)
            load_x(1)
            load_x(2)
            with sp.Fori(2, NG - 1) as i:
                load_x(i + 1)
                store_h(i - 2)
            for g in (NG - 3, NG - 2, NG - 1):
                store_h(g)

            sp.wait_ge(S["pads_ready"], 1)
            for e in range(E):
                at = sp.value_load(pad_row[0:1, e:e + 1], min_val=e * REGION, max_val=(e + 1) * REGION - ET)
                sp.dma_start(rows_in[bass.ds(at, ET), :].rearrange("(p s) c -> p s c", s=ES),
                             pad_tile).then_inc(S["pads_stored"], 16)
            sp.dma_start(rows_in[E * REGION:E * REGION + ET, :].rearrange("(p s) c -> p s c", s=ES),
                         pad_tile).then_inc(S["pads_stored"], 16)
            sp.dma_start(total[NB * T:NB * T + ET, :].rearrange("(p s) c -> p s c", s=ES),
                         pad_tile[:, :, INFO:INFO + C]).then_inc(S["pads_stored"], 16)

            sp.wait_ge(S["h_stored"], 16 * NG)
            sp.wait_ge(S["table_ready"], 1)
            sp.wait_ge(S["scattered"], 16 * 2 * G * NG)
            sp.wait_ge(S["pads_stored"], 16 * (E + 2))

            def load_tile(j, b):
                e = sp.value_load(tile_exp[0:1, bass.ds(j, 1)], min_val=0, max_val=E - 1)
                at = sp.value_load(tile_row[0:1, bass.ds(j, 1)], min_val=0, max_val=E * REGION)
                for dst, src in (
                    (eup[b][0:CC, :, :], a["L1_ffn_w1"][bass.ds(e * C, C), :].rearrange("(k p) n -> p k n", k=KC)),
                    (eup[b][CC:CC + 1, 0, :], a["L1_ffn_b1"][bass.ds(e, 1), :]),
                    (edown[b][:, :, :], a["L1_ffn_w2"][bass.ds(e * F, F), :].rearrange("(m p) n -> p m n", p=P)),
                    (eb2[b][:, :], a["L1_ffn_b2"][bass.ds(e, 1), :].to_broadcast([P, C])),
                    (ex[b][:, :, :], rows_in[bass.ds(at, ET), :].rearrange("(p s) c -> p s c", s=ES)),
                ):
                    sp.dma_start(dst, src).then_inc(e_w[b], 16)

            for b in range(NBUF):
                load_tile(b, b)
            with sp.Fori(0, NT // NBUF - 1) as i:
                for b in range(NBUF):
                    sp.wait_ge(S["e_y"], NBUF * i + b + 1)
                    load_tile(NBUF * i + b + NBUF, b)

            sp.wait_ge(S["e_added"], 16 * ES * NT)
            sp.dma_start(out.rearrange("b p c -> (b p) c"), total[0:NB * T, :]).then_inc(S["out_stored"], 16)
            sp.wait_ge(S["out_stored"], 16)

        @block.tensor
        def _(pe):
            def transposes(src, bank):
                for t in range(G):
                    for k in range(KC):
                        last = nc.tensor.transpose(ps[0:CC, bank + k, t * T:(t + 1) * T],
                                                   src[:, t, k * CC:(k + 1) * CC], ident[:, :])
                return last

            def channels_out(bank, w, rhs):
                for m in range(KC):
                    for k in range(KC):
                        last = nc.tensor.matmul(ps[0:CC, bank + m, :], w[:, k, m * CC:(m + 1) * CC],
                                                rhs[:, k * N:(k + 1) * N], start=(k == 0), stop=(k == KC - 1))
                return last

            def tokens_out(bank, xT, w):
                for t in range(G):
                    o = ps[:, bank + t // 2, (t % 2) * C:(t % 2 + 1) * C]
                    for k in range(KC):
                        last = nc.tensor.matmul(o, xT[:, k * N + t * T:k * N + (t + 1) * T], w[:, k, :],
                                                start=(k == 0), stop=(k == KC - 1))
                return last

            def a_delta(g):
                pe.wait_ge(S["x_diffed"], g + 1)
                if not isinstance(g, int) or g > 0:
                    pe.wait_ge(S["hB_ready"], g)
                transposes(delta, 0).then_inc(S["dT_psum"], 1)

            def a_scores(g):
                pe.wait_ge(S["dT_ready"], g + 1)
                tokens_out(0, dT, w_tok).then_inc(S["tok_psum"], 1)

            def a_hidden(g):
                pe.wait_ge(S["a_hn"], g + 1)
                transposes(hnA, 0).then_inc(S["a_hT_psum"], 1)

            def a_r(g):
                pe.wait_ge(S["xr_ready"], g + 1)
                channels_out(0, w_r, xr).then_inc(S["r_psum"], 1)

            def a_k(g):
                pe.wait_ge(S["xk_ready"], g + 1)
                pe.wait_ge(S["tanh_r_ready"], g + 1)
                channels_out(0, w_k, xk).then_inc(S["k_psum"], 1)

            def a_v(g):
                pe.wait_ge(S["xv_ready"], g + 1)
                pe.wait_ge(S["k_ready"], g + 1)
                channels_out(0, w_v, xv).then_inc(S["v_psum"], 1)

            def a_project(g, gc):
                pe.wait_ge(S["sy_ready"], g + 1)
                if gc is not None:
                    pe.wait_ge(S["hF_ready"], gc + 1)
                tokens_out(0, sy, w_o).then_inc(S["oproj_psum"], 1)

            def b_transposes(g):
                pe.wait_ge(S["b_hn"], g + 1)
                transposes(hnB, 2).then_inc(S["b_hT_psum"], 1)

            def c_transposes(g):
                pe.wait_ge(S["c_hn"], g + 1)
                transposes(hnC, 4).then_inc(S["c_hT_psum"], 1)

            def r_transposes(g, gc):
                pe.wait_ge(S["r_hn"], g + 1)
                if gc is not None:
                    pe.wait_ge(S["qkv_out"], G * gc + G)
                transposes(hnR, 4).then_inc(S["r_hT_psum"], 1)

            def b_mlp_up(g, ms):
                pe.wait_ge(S["b_hT"], g + 1)
                for m in ms:
                    if m >= 2:
                        pe.wait_ge(S["hid_ready"], FM * g + m - 1)
                    for k in range(KC):
                        last = nc.tensor.matmul(ps[:, 2 + m % 2, :], w_up[:, k, m * P:(m + 1) * P],
                                                hTB[:, k, :], start=(k == 0), stop=(k == KC - 1))
                    last.then_inc(S["up_psum"], 1)

            def b_mlp_down(g, ts):
                pe.wait_ge(S["hid_ready"], FM * g + FM)
                for t in ts:
                    for m in range(FM):
                        last = nc.tensor.matmul(ps[:, 2 + t // 2, (t % 2) * C:(t % 2 + 1) * C],
                                                hid[:, m, t * T:(t + 1) * T], w_down[:, m, :],
                                                start=(m == 0), stop=(m == FM - 1))
                if t == G - 1:
                    last.then_inc(S["down_psum"], 1)

            def c_qkv(g):
                pe.wait_ge(S["c_hT"], g + 1)
                for t in range(G):
                    if t >= 2:
                        pe.wait_ge(S["qkv_out"], G * g + t - 1)
                    bank = 4 + 2 * (t % 2)
                    for k in range(KC):
                        r = CC + 1 if k == 0 else CC
                        nc.tensor.matmul(ps[:, bank, 0:2 * C], hTC[0:r, k, t * T:(t + 1) * T],
                                         w_qkv[0:r, k, 0:2 * C], start=(k == 0), stop=(k == KC - 1))
                    for k in range(KC):
                        r = CC + 1 if k == 0 else CC
                        last = nc.tensor.matmul(ps[:, bank + 1, 0:C], hTC[0:r, k, t * T:(t + 1) * T],
                                                w_qkv[0:r, k, 2 * C:3 * C], start=(k == 0), stop=(k == KC - 1))
                    last.then_inc(S["qkv_psum"], 1)

            def c_heads(g, gr):
                if gr is not None:
                    pe.wait_ge(S["slots_ready"], gr + 1)
                pe.wait_ge(S["q_norm"], g + 1)
                pe.wait_ge(S["k_scaled"], g + 1)
                for t in range(G):
                    if t >= 2:
                        pe.wait_ge(S["qT_ready"], G * g + t - 1)
                        pe.wait_ge(S["kT_ready"], G * g + t - 1)
                    for n, src in enumerate((qpad, kpad)):
                        for c in range(HC):
                            last = nc.tensor.transpose(
                                ps[:, 4 + 2 * (t % 2) + n, c * P:(c + 1) * P],
                                src[:, t, HJ * c:HJ * c + HJ, :].rearrange("p h d -> p (h d)"), ident[:, :])
                    last.then_inc(S["qkT_psum"], 1)

            def c_scores(g, t, half):
                if t == 0:
                    pe.wait_ge(S["qT_ready"], G * g + G)
                    pe.wait_ge(S["kT_ready"], G * g + G)
                else:
                    pe.wait_ge(S["exp_ready"], 2 * G * g + 2 * (t - 1) + half + 1)
                for j in (2 * half, 2 * half + 1):
                    for c in range(HC):
                        last = nc.tensor.matmul(ps[:, 4 + j, c * P:(c + 1) * P],
                                                kT[32 * j:32 * j + HD, t, c * P:(c + 1) * P],
                                                qT[32 * j:32 * j + HD, t, c * P:(c + 1) * P],
                                                start=True, stop=True)
                last.then_inc(S["scores_psum"], 1)

            def c_values(g, t, gb):
                pe.wait_ge(S["vpad_ready"], G * g + t + 1)
                if t == 0 and gb is not None:
                    pe.wait_ge(S["hC_ready"], gb + 1)
                for c in range(HC):
                    for j in range(HJ):
                        last = nc.tensor.matmul(ps[32 * j:32 * j + 32, 2 + t % 2, c * P:(c + 1) * P],
                                                vpad[:, t % 2, HC * j + c, :], probs[:, t % 2, HC * j + c, :],
                                                start=True, stop=True)
                last.then_inc(S["oT_psum"], 1)

            def c_project(g, t, ga):
                if t == 0 and ga is not None:
                    pe.wait_ge(S["v_ready"], ga + 1)
                pe.wait_ge(S["oT_ready"], G * g + t + 1)
                for c in range(HC):
                    last = nc.tensor.matmul(ps[:, t // 2, (t % 2) * C:(t % 2 + 1) * C],
                                            oT[:, t % 2, c * P:(c + 1) * P], w_ao[:, c, :],
                                            start=(c == 0), stop=(c == HC - 1))
                if t == G - 1:
                    last.then_inc(S["aproj_psum"], 1)

            def r_logits(g):
                pe.wait_ge(S["r_hT"], g + 1)
                for t in range(G):
                    for k in range(KC):
                        last = nc.tensor.matmul(ps[:, 6, t * E:(t + 1) * E], hTC[0:CC, k, t * T:(t + 1) * T],
                                                w_router[:, k, :], start=(k == 0), stop=(k == KC - 1))
                last.then_inc(S["logits_psum"], 1)

            def r_places(g):
                pe.wait_ge(S["picked_ready"], g + 1)
                nc.tensor.matmul(ps[:, 7, 0:G * E], before[:, :], picked[:, :, :].rearrange("p t e -> p (t e)"),
                                 start=True, stop=False)
                nc.tensor.matmul(ps[:, 7, 0:G * E], ones_bf[:, :],
                                 run_bf[:, 0:G, :].rearrange("p t e -> p (t e)"),
                                 start=False, stop=True).then_inc(S["place_psum"], 1)

            def round_(i):
                ga, gb, gc, gr = stages(i)
                A, B, CA, R = (g is not None for g in (ga, gb, gc, gr))
                if CA: c_transposes(gc)
                if CA: c_qkv(gc)
                if B: a_project(gb, gr)
                if R: r_transposes(gr, gc)
                if A: a_delta(ga)
                if R: r_logits(gr)
                if A: a_scores(ga)
                if B: b_transposes(gb)
                if B: b_mlp_up(gb, range(0, 3))
                if R: r_places(gr)
                if A: a_hidden(ga)
                if B: b_mlp_up(gb, range(3, FM))
                if CA: c_heads(gc, gr)
                if A: a_r(ga)
                if B: b_mlp_down(gb, (0, 1))
                if A: a_k(ga)
                if B: b_mlp_down(gb, (2, 3))
                if A: a_v(ga)
                if CA:
                    for t in range(G):
                        c_scores(gc, t, 0)
                        c_scores(gc, t, 1)
                        if t >= 2:
                            c_project(gc, t - 2, ga)
                        if t >= 1:
                            c_values(gc, t - 1, gb)
                    c_project(gc, G - 2, ga)
                    c_values(gc, G - 1, gb)
                    c_project(gc, G - 1, ga)

            pe.wait_ge(S["weights_in"], 16 * N_LOADS)
            pe.wait_ge(S["pool_consts"], 1)
            pe.wait_ge(S["dve_consts"], 1)
            rounds(pe, round_)

            pe.wait_ge(S["slots_ready"], NG)
            nc.tensor.matmul(ps[:, 7, 0:E], ones_bf[:, :], run_bf[:, G, :],
                             start=True, stop=True).then_inc(S["counts_psum"], 1)

            def e_transposes(i, b):
                pe.wait_ge(e_w[b], (i + 1) * 16 * PER_TILE)
                for s in range(ES):
                    for k in range(KC):
                        last = nc.tensor.transpose(ps[0:CC, k, s * P:(s + 1) * P],
                                                   ex[b][:, s, INFO + k * CC:INFO + (k + 1) * CC], ident[:, :])
                last.then_inc(S["e_xT_psum"], 1)

            def e_up(i, b):
                j = NBUF * i + b
                pe.wait_ge(S["x_low"], j + 1)
                pe.wait_ge(S["w_low"], j + 1)
                for m in range(FM):
                    if m >= 4:
                        pe.wait_ge(S["e_hid"], FM * j + m - 3)
                    terms = [(w, x, k) for w, x in ((eup_hi, exT_hi), (eup_hi, exT_lo), (eup_lo, exT_hi))
                             for k in range(KC)]
                    for n, (w, x, k) in enumerate(terms):
                        r = CC + 1 if k == 0 else CC
                        last = nc.tensor.matmul(ps[:, 2 + m % 4, :], w[b][0:r, k, m * P:(m + 1) * P],
                                                x[b][0:r, k, :], start=(n == 0), stop=(n == len(terms) - 1))
                    last.then_inc(S["e_up_psum"], 1)

            def e_down(i, b):
                j = NBUF * i + b
                pe.wait_ge(S["e_hid"], FM * j + FM)
                if not is_first(i, b):
                    pe.wait_ge(S["e_y"], j)
                for s in range(ES):
                    for m in range(FM):
                        last = nc.tensor.matmul(ps[:, 6 + s // 2, (s % 2) * C:(s % 2 + 1) * C],
                                                ehid[b][:, m, s * P:(s + 1) * P], edown[b][:, m, :],
                                                start=(m == 0), stop=(m == FM - 1))
                last.then_inc(S["e_down_psum"], 1)

            def e_step(i, b):
                e_up(i, b)
                if after(i, b):
                    e_transposes(*after(i, b))
                e_down(i, b)

            e_transposes(0, 0)
            expert_tiles(pe, e_step)

        @block.scalar
        def _(act):
            def two(bank, rows, cols):
                return ps[0:rows, bank:bank + 2, 0:cols]

            def a_delta(g):
                act.wait_ge(S["dT_psum"], g + 1)
                nc.scalar.activation(dT.rearrange("p (k n) -> p k n", k=KC), two(0, CC, N),
                                     ACT.Copy).then_inc(S["dT_ready"], 1)

            def a_scores(g):
                act.wait_ge(S["tok_psum"], g + 1)
                nc.scalar.activation(tanh_d.rearrange("p (h t) c -> p h (t c)", h=2), two(0, P, 2 * C),
                                     ACT.Tanh, scale=0.5).then_inc(S["tanh_ready"], 1)

            def a_hidden(g):
                act.wait_ge(S["a_hT_psum"], g + 1)
                nc.scalar.activation(hTA[:, :, 1:T + 1],
                                     two(0, CC, N).rearrange("p k (g t) -> p (k g) t", t=T),
                                     ACT.Copy).then_inc(S["a_hT"], 1)

            def a_gate(g):
                act.wait_ge(S["r_psum"], g + 1)
                nc.scalar.activation(tanh_r[:, :].rearrange("p (k n) -> p k n", k=KC), two(0, CC, N),
                                     ACT.Tanh, scale=0.5).then_inc(S["tanh_r_ready"], 1)

            def a_kv(g, name, dst):
                act.wait_ge(S[f"{name}_psum"], g + 1)
                nc.scalar.activation(dst[:, :].rearrange("p (k n) -> p k n", k=KC), two(0, CC, N),
                                     ACT.Copy).then_inc(S[f"{name}_ready"], 1)

            def a_exps(g):
                act.wait_ge(S["keep_arg"], g + 1)
                nc.scalar.activation(keep[:, :, 1:T], keep[:, :, 1:T], ACT.Exp).then_inc(S["keep_ready"], 1)
                act.wait_ge(S["take_arg"], g + 1)
                nc.scalar.activation(take, take, ACT.Exp).then_inc(S["take_ready"], 1)

            def a_z_exps(g):
                act.wait_ge(S["z_ready"], g + 1)
                nc.scalar.activation(z_neg[:, :, 1:T], z_neg[:, :, 1:T], ACT.Exp)
                nc.scalar.activation(z_pos[:, :, 1:T], z_pos[:, :, 1:T], ACT.Exp,
                                     scale=-1.0).then_inc(S["zexp_ready"], 1)

            def transposed(g, name, dst, bank):
                act.wait_ge(S[f"{name}_hT_psum"], g + 1)
                nc.scalar.activation(dst[0:CC, :, :], two(bank, CC, N), ACT.Copy).then_inc(S[f"{name}_hT"], 1)

            def b_gelu(g, ms):
                for m in ms:
                    act.wait_ge(S["up_psum"], FM * g + m + 1)
                    nc.scalar.activation(hid[:, m, :], ps[:, 2 + m % 2, :], ACT.Gelu,
                                         bias=b_up[:, m:m + 1]).then_inc(S["hid_ready"], 1)

            def c_qkv(g):
                for t in range(G):
                    act.wait_ge(S["qkv_psum"], G * g + t + 1)
                    bank = 4 + 2 * (t % 2)
                    nc.scalar.activation(qk[:, t, :, :].rearrange("p n c -> p (n c)"), ps[:, bank, 0:2 * C], ACT.Copy)
                    nc.scalar.activation(v_s[:, t, :], ps[:, bank + 1, 0:C], ACT.Copy).then_inc(S["qkv_out"], 1)

            def c_heads(g):
                for t in range(G):
                    act.wait_ge(S["qkT_psum"], G * g + t + 1)
                    nc.scalar.activation(qT[:, t, :], ps[:, 4 + 2 * (t % 2), 0:HC * P],
                                         ACT.Copy).then_inc(S["qT_ready"], 1)

            def c_exps(g, t, half):
                act.wait_ge(S["max_ready"], 2 * G * g + 2 * t + half + 1)
                for j in (2 * half, 2 * half + 1):
                    for c in range(HC):
                        n = HC * j + c
                        last = nc.scalar.activation(probs[:, t % 2, n, :], ps[:, 4 + j, c * P:(c + 1) * P], ACT.Exp,
                                                    bias=nmax[:, t, n:n + 1], accum_out=psums[:, t, n:n + 1])
                last.then_inc(S["exp_ready"], 1)

            def c_values(g, t):
                act.wait_ge(S["oT_psum"], G * g + t + 1)
                nc.scalar.activation(oT[:, t % 2, :], ps[:, 2 + t % 2, 0:HC * P],
                                     ACT.Copy).then_inc(S["oT_ready"], 1)

            def r_gap(g):
                act.wait_ge(S["gap_ready"], g + 1)
                nc.scalar.activation(egap[:, :], gap[:, :], ACT.Exp).then_inc(S["egap_ready"], 1)

            def round_(i):
                ga, gb, gc, gr = stages(i)
                A, B, CA, R = (g is not None for g in (ga, gb, gc, gr))
                if CA: transposed(gc, "c", hTC, 4)
                if CA: c_qkv(gc)
                if R: transposed(gr, "r", hTC, 4)
                if A: a_delta(ga)
                if A: a_scores(ga)
                if R: r_gap(gr)
                if B: transposed(gb, "b", hTB, 2)
                if B: b_gelu(gb, range(0, 3))
                if A: a_hidden(ga)
                if B: b_gelu(gb, range(3, FM))
                if CA: c_heads(gc)
                if A: a_gate(ga)
                if A: a_kv(ga, "k", k_s)
                if A: a_kv(ga, "v", v_c)
                for t in range(G):
                    if CA: c_exps(gc, t, 0)
                    if CA: c_exps(gc, t, 1)
                    if A and t == 0: a_exps(ga)
                    if A and t == 1: a_z_exps(ga)
                    if CA and t >= 1: c_values(gc, t - 1)
                if CA: c_values(gc, G - 1)

            act.wait_ge(S["weights_in"], 16 * N_LOADS)
            act.wait_ge(S["dve_consts"], 1)
            rounds(act, round_)

            def e_weights(i, b):
                act.wait_ge(e_w[b], (i + 1) * 16 * PER_TILE)
                nc.scalar.activation(eup_hi[b][:, :, :], eup[b][:, :, :], ACT.Copy).then_inc(S["w_high"], 1)

            def e_rows(i, b):
                act.wait_ge(S["e_xT_psum"], NBUF * i + b + 1)
                nc.scalar.activation(exT_hi[b][0:CC, :, :], ps[0:CC, 0:2, :], ACT.Copy).then_inc(S["x_high"], 1)

            def e_gelu(i, b, ms):
                for m in ms:
                    act.wait_ge(S["e_up_psum"], FM * (NBUF * i + b) + m + 1)
                    nc.scalar.activation(ehid[b][:, m, :], ps[:, 2 + m % 4, :],
                                         ACT.Gelu).then_inc(S["e_hid"], 1)

            def e_step(i, b):
                e_gelu(i, b, range(0, 3))
                if after(i, b):
                    e_weights(*after(i, b))
                e_gelu(i, b, range(3, FM))
                if after(i, b):
                    e_rows(*after(i, b))

            act.wait_ge(S["table_ready"], 1)
            e_weights(0, 0)
            e_rows(0, 0)
            expert_tiles(act, e_step)

        @block.gpsimd
        def _(pool):
            init = Chain(pool, S["p_init"], 11)
            init.begin(0)
            nc.gpsimd.memset(w_ao[:, :, :], 0.0).then_inc(S["gaps_zeroed"], 1)
            pool.wait_ge(S["gaps_zeroed"], 1)
            nc.gpsimd.memset(w_qkv[CC:CC + 1, 0, :], 0.0).then_inc(S["gaps_zeroed"], 1)
            pool.wait_ge(S["gaps_zeroed"], 2)
            init.link(nc.gpsimd.memset(ident[:, :], 0.0))
            init.link(nc.gpsimd.memset(ones_bf[:, :], 1.0))
            init.link(nc.gpsimd.affine_select(out=ident[:, :], in_=ident[:, :], compare_op=ALU.not_equal, fill=1.0,
                                              base=0, pattern=[[-1, P]], channel_multiplier=1))
            init.link(nc.gpsimd.affine_select(out=before[:, :], in_=ones_bf[:, :], compare_op=ALU.is_gt, fill=0.0,
                                              base=0, pattern=[[1, P]], channel_multiplier=-1))
            init.link(nc.gpsimd.memset(neg_half[:, :], -0.5))
            init.link(nc.gpsimd.iota(lane8_i[:, :, :], [[0, G], [1, E]], base=0, channel_multiplier=0))
            init.link(nc.gpsimd.iota(region_i[:, :, :], [[0, G], [REGION, E]], base=0, channel_multiplier=0))
            init.link(nc.gpsimd.iota(pad_token[:, :], [[1, ES]], base=NB * T, channel_multiplier=ES))
            init.link(nc.gpsimd.iota(token_i[:, :], [[T, G]], base=0, channel_multiplier=1))
            init.link(nc.gpsimd.iota(mth_i[:, :, :], [[0, E], [ET, MAXT]], base=0, channel_multiplier=0))
            init.link(nc.gpsimd.iota(jth_i[:, :, :], [[1, NT], [0, E]], base=0, channel_multiplier=0))
            init.end()
            pool.sem_inc(S["pool_consts"], 1)
            pool.wait_ge(S["weights_in"], 16 * N_LOADS)
            pool.wait_ge(S["dve_consts"], 1)

            res = Chain(pool, S["p_res"], 1)

            def rstd(g, name, out_, mv, n):
                chain = Chain(pool, S[f"p_{name}"], 1)
                chain.begin(g)
                pool.wait_ge(S[f"{name}_stats"], g + 1)
                stand_alone(pool)
                chain.link(nc.gpsimd.tensor_scalar(out_, mv[:, :, 1], EPS, None, ALU.add))
                chain.end()
                nc.gpsimd.tensor_tensor(out_, out_, neg_half[:, 0:n], ALU.pow).then_inc(S[f"{name}_rstd"], 1)

            def a_sum(g):
                pool.wait_ge(S["x_loaded"], 16 * (g + 1))
                if not isinstance(g, int) or g > 0:
                    pool.wait_ge(S["a_stats"], g)
                nc.gpsimd.tensor_tensor(xsum[:, :, :], xt[:, :, 0:C], xt[:, :, C:2 * C],
                                        ALU.add).then_inc(S["x_summed"], 1)

            def a_num(g):
                pool.wait_ge(S["frac_ready"], g + 1)
                nc.gpsimd.tensor_tensor(take_v, take_v, take, ALU.add).then_inc(S["num_ready"], 1)

            def c_residual(g):
                pool.wait_ge(S["c_hn"], g + 1)
                if not isinstance(g, int) or g > 0:
                    pool.wait_ge(S["r_hn"], g)
                    pool.wait_ge(S["h_stored"], 16 * g)
                res.begin(g)
                res.link(nc.gpsimd.tensor_tensor(resC[:, :, :], hC[:, :, :], hnC[:, :, :], ALU.add))
                res.end()
                nc.gpsimd.tensor_tensor(resC[:, :, :], resC[:, :, :],
                                        bo[:, :].rearrange("p (o c) -> p o c", o=1).to_broadcast([P, G, C]),
                                        ALU.add).then_inc(S["res_ready"], 1)

            def c_k_scale(g):
                pool.wait_ge(S["k_norm"], g + 1)
                for t in range(G):
                    last = nc.gpsimd.tensor_tensor(kpad[:, t, :, 0:HD], kpad[:, t, :, 0:HD],
                                                   gamma[:, :].rearrange("p (h d) -> p h d", d=HD), ALU.mult)
                last.then_inc(S["k_scaled"], 1)

            def r_scatter(g):
                pool.wait_ge(S["slots_ready"], g + 1)
                stand_alone(pool)
                for s in range(2):
                    for t in range(G):
                        n = s * G + t
                        nc.gpsimd.indirect_dma_start(
                            rows_in, bass.IndirectOffsetOnAxis(ap=slot_i[:, n:n + 1], axis=0),
                            rowR[:, t, :], None).then_inc(S["scattered"], 16)

            def round_(i):
                ga, gb, gc, gr = stages(i)
                A, B, CA, R = (g is not None for g in (ga, gb, gc, gr))
                if A: a_sum(ga)
                if CA: rstd(gc, "qk", rstd_qk[:, :], mv_qk, 2 * G)
                if B: rstd(gb, "b", rstdB[:, :], mvB, G)
                if CA: c_k_scale(gc)
                if A: rstd(ga, "a", rstdA[:, :], mvA, G)
                if CA: c_residual(gc)
                if R: r_scatter(gr)
                if B: rstd(gb, "c", rstdC[:, :], mvC, G)
                if A: a_num(ga)
                if CA: rstd(gc, "r", rstdR[:, :], mvR, G)

            rounds(pool, round_)

            def e_weights(i, b):
                pool.wait_ge(S["w_high"], NBUF * i + b + 1)
                nc.gpsimd.tensor_tensor(eup_lo[b][:, :, :], eup[b][:, :, :], eup_hi[b][:, :, :].bitcast(F32),
                                        ALU.subtract).then_inc(S["w_low"], 1)

            def e_add(i, b):
                j = NBUF * i + b
                pool.wait_ge(S["e_y"], j + 1)
                if not is_first(i, b):
                    pool.wait_ge(S["e_added"], 16 * ES * j)
                stand_alone(pool)
                for s in range(ES):
                    nc.gpsimd.indirect_dma_start(
                        total, bass.IndirectOffsetOnAxis(ap=etoken[b][:, s:s + 1], axis=0),
                        ey[b][:, s, :], None, compute_op=ALU.add).then_inc(S["e_added"], 16)

            def e_step(i, b):
                if after(i, b):
                    e_weights(*after(i, b))
                e_add(i, b)

            e_weights(0, 0)
            expert_tiles(pool, e_step)

        @block.vector
        def _(dve):
            init = Chain(dve, S["d_init"], 2)
            init.begin(0)
            nc.vector.memset(hTA[:, :, 0:1], 0.0)
            nc.vector.memset(o_s[:, 0:1], 0.0)
            nc.vector.memset(p_s[:, 0:1], 0.0)
            nc.vector.memset(q_s[:, 0:1], 0.0)
            nc.vector.memset(run_counts[:, :, :], 0.0)
            nc.vector.memset(qpad[:, :, :, :], 0.0)
            nc.vector.memset(kpad[:, :, :, :], 0.0)
            nc.vector.memset(vpad[:, :, :, :], 0.0)
            nc.vector.memset(one_row[:, :], 1.0)
            init.link(nc.vector.memset(hTC[CC:CC + 1, :, :], 1.0))
            dve.wait_ge(S["weights_in"], 16 * N_LOADS)
            dve.wait_ge(S["pool_consts"], 1)
            for k in range(KC):
                nc.vector.tensor_copy(decay[:, k * G:(k + 1) * G, :].rearrange("p g t -> p (g t)"),
                                      chan[:, 0, k:k + 1].to_broadcast([CC, N]))
            nc.vector.scalar_tensor_tensor(gamma[:, :], gam[:, 0, :], float(HD) ** -0.5, gam[:, 1, :],
                                           ALU.mult, ALU.mult)
            nc.vector.tensor_copy(lane8[:, :, :], lane8_i[:, :, :])
            nc.vector.tensor_copy(token_f[:, :], token_i[:, :])
            nc.vector.tensor_copy(mth[:, :, :], mth_i[:, :, :])
            nc.vector.tensor_copy(jth[:, :, :], jth_i[:, :, :])
            init.link(nc.vector.tensor_copy(region_off[:, :, :], region_i[:, :, :]))
            nc.vector.memset(decay[:, :, 0:1], STATE_FLOOR).then_inc(S["dve_consts"], 1)
            init.end()

            tok = Chain(dve, S["d_tok"], 4)
            wkv = Chain(dve, S["d_wkv"], 8)
            lns = {name: Chain(dve, S[f"d_{name}"], 1) for name in "bcr"}
            qkc = Chain(dve, S["d_qk"], 1)
            vch = Chain(dve, S["d_v"], G)
            route = Chain(dve, S["d_route"], 18)

            def statistics(chain, src, st, mv, n):
                for t in range(n):
                    last = nc.vector.bn_stats(st[:, t, :], src(t))
                chain.link(last, stand_alone)
                for t in range(n):
                    last = nc.vector.bn_aggr(mv[:, t, :], st[:, t, :])
                return last

            def normalise(dst, src, mv, rs, ts):
                for n, t in enumerate(ts):
                    last = nc.vector.tensor_scalar(dst(n), src(n), mv[:, t, 0:1], rs[:, t:t + 1],
                                                   ALU.subtract, ALU.mult)
                return last

            def a_delta(g):
                dve.wait_ge(S["x_loaded"], 16 * (g + 1))
                nc.vector.tensor_tensor(delta[:, :, :], xt[:, :, 0:C], xt[:, :, C:2 * C],
                                        ALU.subtract).then_inc(S["x_diffed"], 1)

            def a_tokens(g):
                dve.wait_ge(S["tanh_ready"], g + 1)
                tok.begin(g)
                tok.link(nc.vector.scalar_tensor_tensor(tanh_d, tanh_d, 0.5, delta[:, :, :], ALU.mult, ALU.mult))
                dve.wait_ge(S["x_summed"], g + 1)
                tok.link(nc.vector.scalar_tensor_tensor(hA[:, :, :], xsum[:, :, :], 0.5, tanh_d, ALU.mult, ALU.add))
                statistics(tok, lambda t: hA[:, t, :], statsA, mvA, G).then_inc(S["a_stats"], 1)

            def a_normalise(g):
                dve.wait_ge(S["a_rstd"], g + 1)
                normalise(lambda t: hnA[:, t, :], lambda t: hA[:, t, :], mvA, rstdA,
                          range(G)).then_inc(S["a_hn"], 1)

            def a_mix(g):
                dve.wait_ge(S["a_hT"], g + 1)
                tok.link(nc.vector.tensor_tensor(diff, hTA[:, :, 1:T + 1], hTA[:, :, 0:T], ALU.subtract))
                tok.end()
                for mix, dst, name in ((4, xr, "xr_ready"), (2, xk, "xk_ready"), (3, xv, "xv_ready")):
                    for k in range(KC):
                        last = nc.vector.scalar_tensor_tensor(
                            dst[:, k * N:(k + 1) * N].rearrange("p (g t) -> p g t", t=T),
                            diff[:, k * G:(k + 1) * G, :], chan[:, mix, k:k + 1],
                            hTA[:, k * G:(k + 1) * G, 0:T], ALU.mult, ALU.add)
                    last.then_inc(S[name], 1)

            M = KC * N
            keep_flat = flat(1)
            z_neg_flat, z_pos_flat = flat(4), flat(5)

            def a_exponents(g):
                dve.wait_ge(S["k_ready"], g + 1)
                wkv.begin(g)
                wkv.link(nc.vector.tensor_tensor_scan(o_s[:, 1:M + 1], decay[:, :, :].rearrange("p g t -> p (g t)"),
                                                      k_s[:, :], 0.0, ALU.add, ALU.max))
                for k in range(KC):
                    nc.vector.scalar_tensor_tensor(
                        keep[:, k * G:(k + 1) * G, 1:T],
                        o_s[:, k * N:(k + 1) * N].rearrange("p (g t) -> p g t", t=T)[:, :, 1:T],
                        chan[:, 0, k:k + 1],
                        o_s[:, 1 + k * N:1 + (k + 1) * N].rearrange("p (g t) -> p g t", t=T)[:, :, 1:T],
                        ALU.add, ALU.subtract)
                nc.vector.memset(keep[:, :, 0:1], 0.0).then_inc(S["keep_arg"], 1)
                nc.vector.tensor_tensor(take, k_s[:, :], o_s[:, 1:M + 1], ALU.subtract).then_inc(S["take_arg"], 1)
                for k in range(KC):
                    last = nc.vector.scalar_tensor_tensor(z_s[:, k * N:(k + 1) * N], k_s[:, k * N:(k + 1) * N],
                                                          chan[:, 1, k:k + 1], o_s[:, k * N:(k + 1) * N],
                                                          ALU.add, ALU.subtract)
                wkv.link(last)
                z_steps = steps(0)
                nc.vector.tensor_scalar(z_neg[:, :, 1:T], z_steps[:, :, 1:T], 0.0, None, ALU.min)
                nc.vector.tensor_scalar(z_pos[:, :, 1:T], z_steps[:, :, 1:T], 0.0, None, ALU.max)
                nc.vector.memset(z_neg[:, :, 0:1], 1.0)
                nc.vector.memset(z_pos[:, :, 0:1], 0.0).then_inc(S["z_ready"], 1)

            def a_scan_p(g):
                dve.wait_ge(S["take_ready"], g + 1)
                dve.wait_ge(S["v_ready"], g + 1)
                wkv.link(nc.vector.tensor_tensor(take_v, take, v_c[:, :], ALU.mult))
                dve.wait_ge(S["keep_ready"], g + 1)
                nc.vector.tensor_tensor_scan(p_s[:, 1:M + 1], keep_flat, take_v, 0.0, ALU.mult, ALU.add)

            def a_scan_q(g):
                wkv.link(nc.vector.tensor_tensor_scan(q_s[:, 1:M + 1], keep_flat, take, 0.0, ALU.mult, ALU.add))

            def a_fraction(g):
                dve.wait_ge(S["zexp_ready"], g + 1)
                nc.vector.tensor_tensor(take, z_neg_flat, v_c[:, :], ALU.mult)
                nc.vector.tensor_tensor(take_v, z_pos_flat, p_s[:, 0:M], ALU.mult).then_inc(S["frac_ready"], 1)

            def a_denominator(g):
                wkv.link(nc.vector.tensor_tensor(keep_flat, z_pos_flat, q_s[:, 0:M], ALU.mult))
                wkv.link(nc.vector.tensor_tensor(keep_flat, keep_flat, z_neg_flat, ALU.add))

            def a_reciprocal(g, n):
                q = M // 4
                last = nc.vector.reciprocal(keep_flat[:, n * q:(n + 1) * q], keep_flat[:, n * q:(n + 1) * q])
                if n == 3:
                    wkv.link(last)

            def a_gate(g):
                dve.wait_ge(S["num_ready"], g + 1)
                dve.wait_ge(S["tanh_r_ready"], g + 1)
                wkv.link(nc.vector.scalar_tensor_tensor(take, tanh_r[:, :], 1.0, take_v, ALU.add, ALU.mult))
                wkv.end()
                nc.vector.tensor_tensor(sy[:, :], take, keep_flat, ALU.mult).then_inc(S["sy_ready"], 1)

            def a_residual(g):
                dve.wait_ge(S["oproj_psum"], g + 1)
                nc.vector.scalar_tensor_tensor(
                    hB[:, :, :].rearrange("p (h t) c -> p h (t c)", h=2), ps[:, 0:2, 0:2 * C], 0.5,
                    hA[:, :, :].rearrange("p (h t) c -> p h (t c)", h=2), ALU.mult, ALU.add).then_inc(S["hB_ready"], 1)

            def ln_stats(g, name, src, st, mv):
                chain = lns[name]
                chain.begin(g)
                statistics(chain, lambda t: src[:, t, :], st, mv, G).then_inc(S[f"{name}_stats"], 1)
                chain.end()

            def ln_out(g, name, dst, src, mv, rs):
                dve.wait_ge(S[f"{name}_rstd"], g + 1)
                normalise(lambda t: dst[:, t, :], lambda t: src[:, t, :], mv, rs,
                          range(G)).then_inc(S[f"{name}_hn"], 1)

            def b_mlp_add(g, gc):
                dve.wait_ge(S["down_psum"], g + 1)
                if gc is not None:
                    dve.wait_ge(S["res_ready"], gc + 1)
                nc.vector.tensor_tensor(hC[:, :, :].rearrange("p (h t) c -> p h (t c)", h=2), ps[:, 2:4, 0:2 * C],
                                        hB[:, :, :].rearrange("p (h t) c -> p h (t c)", h=2),
                                        ALU.add).then_inc(S["hC_ready"], 1)
                dve.wait_ge(S["hC_ready"], g + 1)

            def c_qk_stats(g):
                dve.wait_ge(S["qkv_out"], G * g + G)
                qkc.begin(g)
                statistics(qkc, lambda n: qk[:, n // 2, n % 2, :], stats_qk, mv_qk, 2 * G).then_inc(S["qk_stats"], 1)
                qkc.end()

            def heads(ap):
                return ap.rearrange("p (h d) -> p h d", d=HD)

            def c_k_norm(g):
                dve.wait_ge(S["qk_rstd"], g + 1)
                normalise(lambda t: kpad[:, t, :, 0:HD], lambda t: heads(qk[:, t, 1, :]), mv_qk, rstd_qk,
                          range(1, 2 * G, 2)).then_inc(S["k_norm"], 1)

            def c_q_norm(g):
                normalise(lambda t: qpad[:, t, :, 0:HD], lambda t: heads(qk[:, t, 0, :]), mv_qk, rstd_qk,
                          range(0, 2 * G, 2)).then_inc(S["q_norm"], 1)

            def c_heads(g):
                for t in range(G):
                    dve.wait_ge(S["qkT_psum"], G * g + t + 1)
                    nc.vector.tensor_copy(kT[:, t, :], ps[:, 5 + 2 * (t % 2), 0:HC * P]).then_inc(S["kT_ready"], 1)

            def c_max(g, t, half):
                dve.wait_ge(S["scores_psum"], 2 * G * g + 2 * t + half + 1)
                nc.vector.tensor_reduce(nmax[:, t, 6 * half:6 * half + 6],
                                        ps[:, 4 + 2 * half:6 + 2 * half, 0:HC * P].rearrange(
                                            "p j (c q) -> p j c q", q=P),
                                        AX.X, ALU.max, negate=True).then_inc(S["max_ready"], 1)

            def c_values(g, t):
                if t == 0:
                    vch.begin(g)
                dve.wait_ge(S["exp_ready"], 2 * G * g + 2 * t + 2)
                vch.link(nc.vector.reciprocal(rsums[:, t, :], psums[:, t, :]))
                nc.vector.tensor_tensor(
                    vpad[:, t % 2, :, 0:HD].rearrange("p (j c) d -> p j c d", j=HJ),
                    v_s[:, t, :].rearrange("p (c j d) -> p j c d", j=HJ, d=HD),
                    rsums[:, t, :].rearrange("p (j c o) -> p j c o", j=HJ, o=1).to_broadcast([P, HJ, HC, HD]),
                    ALU.mult).then_inc(S["vpad_ready"], 1)
                if t == G - 1:
                    vch.end()

            def c_attn_add(g):
                dve.wait_ge(S["aproj_psum"], g + 1)
                dve.wait_ge(S["res_ready"], g + 1)
                r2 = resC[:, :, :].rearrange("p (h t) c -> p h (t c)", h=2)
                nc.vector.tensor_tensor(r2, ps[:, 0:2, 0:2 * C], r2, ALU.add).then_inc(S["hF_ready"], 1)
                dve.wait_ge(S["hF_ready"], g + 1)

            def r_pick(g):
                link = route.link
                route.begin(g)
                dve.wait_ge(S["logits_psum"], g + 1)
                link(nc.vector.tensor_copy(logits[:, :], ps[:, 6, 0:G * E]), stand_alone)
                for t in range(G):
                    last = nc.vector.max(top8[:, t, :], logits[:, t * E:(t + 1) * E])
                link(last, stand_alone)
                for t in range(G):
                    last = nc.vector.max_index(top_i[:, t, :], top8[:, t, :], logits[:, t * E:(t + 1) * E])
                link(last)
                nc.vector.tensor_tensor(gap[:, :], top8[:, :, 1], top8[:, :, 0],
                                        ALU.subtract).then_inc(S["gap_ready"], 1)
                link(nc.vector.tensor_copy(top_f[:, :, :], top_i[:, :, 0:2].rearrange("p t s -> p s t")))
                for s in range(2):
                    last = nc.vector.tensor_tensor(
                        hot[:, s, :, :], lane8[:, :, :],
                        top_f[:, s, :].rearrange("p (t o) -> p t o", o=1).to_broadcast([P, G, E]), ALU.is_equal)
                link(last)
                nc.vector.tensor_copy(run_counts[:, 0, :], run_counts[:, G, :])
                nc.vector.tensor_tensor(picked[:, :, :], hot[:, 0, :, :], hot[:, 1, :, :], ALU.add)
                link(nc.vector.tensor_tensor(picked_f[:, :, :], hot[:, 0, :, :], hot[:, 1, :, :], ALU.add))
                for t in range(G):
                    link(nc.vector.tensor_tensor(run_counts[:, t + 1, :], run_counts[:, t, :], picked_f[:, t, :],
                                                 ALU.add))
                nc.vector.tensor_copy(run_bf[:, :, :], run_counts[:, :, :]).then_inc(S["picked_ready"], 1)

            def r_place(g):
                link = route.link
                dve.wait_ge(S["egap_ready"], g + 1)
                link(nc.vector.tensor_scalar(esum[:, :], egap[:, :], 1.0, None, ALU.add))
                link(nc.vector.reciprocal(wts[:, 0:G], esum[:, :]))
                link(nc.vector.tensor_tensor(wts[:, G:2 * G], wts[:, 0:G], egap[:, :], ALU.mult))
                dve.wait_ge(S["place_psum"], g + 1)
                link(nc.vector.tensor_tensor(place[:, :], ps[:, 7, 0:G * E],
                                             region_off[:, :, :].rearrange("p t e -> p (t e)"), ALU.add))
                for s in range(2):
                    last = nc.vector.tensor_tensor(placed[:, s, :, :], hot[:, s, :, :],
                                                   place[:, :].rearrange("p (t e) -> p t e", e=E), ALU.mult)
                link(last)
                link(nc.vector.tensor_reduce(slot_f[:, :], placed[:, :, :, :].rearrange("p s t e -> p (s t) e"),
                                             AX.X, ALU.add))
                link(nc.vector.tensor_copy(slot_i[:, :], slot_f[:, :]))
                nc.vector.tensor_copy(rowR[:, :, 0:2], wts[:, :].rearrange("p (s t) -> p t s", s=2))
                nc.vector.tensor_copy(rowR[:, :, 2], top_f[:, 0, :])
                link(nc.vector.tensor_copy(rowR[:, :, 3], token_f[:, :]))
                nc.vector.tensor_scalar(token_f[:, :], token_f[:, :], float(N), None,
                                        ALU.add).then_inc(S["slots_ready"], 1)
                route.end()

            def round_(i):
                ga, gb, gc, gr = stages(i)
                A, B, CA, R = (g is not None for g in (ga, gb, gc, gr))
                if A: a_delta(ga)
                if CA: c_qk_stats(gc)
                if B: a_residual(gb)
                if B: dve.wait_ge(S["hB_ready"], gb + 1)
                if B: ln_stats(gb, "b", hB, statsB, mvB)
                if CA: c_k_norm(gc)
                if B: ln_out(gb, "b", hnB, hB, mvB, rstdB)
                if CA: c_q_norm(gc)
                if R: r_pick(gr)
                if A: a_tokens(ga)
                if R: r_place(gr)
                if A: a_normalise(ga)
                if A: a_mix(ga)
                if CA: c_heads(gc)
                if A: a_exponents(ga)
                for t in range(G):
                    if CA: c_max(gc, t, 0)
                    if B and t == 1:
                        b_mlp_add(gb, gc)
                        ln_stats(gb, "c", hC, statsC, mvC)
                    if A and t == 2: a_scan_q(ga)
                    if A and t == 3: a_denominator(ga)
                    if CA: c_max(gc, t, 1)
                    if CA and t > 0: c_values(gc, t - 1)
                    if A and t == 1: a_scan_p(ga)
                    if B and t == 2: ln_out(gb, "c", hnC, hC, mvC, rstdC)
                    if A and t == 2: a_fraction(ga)
                    if A and t == 3: a_reciprocal(ga, 0)
                if CA: c_values(gc, G - 1)
                if A: a_reciprocal(ga, 1)
                if A: a_reciprocal(ga, 2)
                if A: a_reciprocal(ga, 3)
                if CA:
                    c_attn_add(gc)
                    ln_stats(gc, "r", resC, statsR, mvR)
                if A: a_gate(ga)
                if CA:
                    if gr is not None:
                        dve.wait_ge(S["scattered"], 16 * 2 * G * (gr + 1))
                    ln_out(gc, "r", hnR, resC, mvR, rstdR)

            rounds(dve, round_)

            table = Chain(dve, S["d_table"], 16)
            link = table.link
            table.begin(0)
            dve.wait_ge(S["x_summed"], NG)
            dve.wait_ge(S["x_diffed"], NG)
            link(nc.vector.memset(pad_tile, 0.0))
            link(nc.vector.tensor_copy(pad_tile[:, :, 3], pad_token[:, :]))
            dve.wait_ge(S["counts_psum"], 1)
            link(nc.vector.tensor_copy(n_tok[:, :], ps[:, 7, 0:E]))
            nc.vector.tensor_tensor(pad_row[:, :], n_tok[0:1, :], region_off[0:1, 0, :],
                                    ALU.add).then_inc(S["pads_ready"], 1)
            link(nc.vector.tensor_tensor(mth[:, :, :], n_tok[:, :].rearrange("p (e o) -> p e o", o=1)
                                         .to_broadcast([P, E, MAXT]), mth[:, :, :], ALU.is_gt))
            link(nc.vector.tensor_reduce(n_tiles[:, :], mth[:, :, :], AX.X, ALU.add))
            link(nc.vector.tensor_tensor_scan(tile_end[:, :], one_row[:, :], n_tiles[:, :], 0.0, ALU.mult, ALU.add))
            link(nc.vector.tensor_tensor(passed[:, :, :], jth[:, :, :],
                                         tile_end[:, :].rearrange("p (o e) -> p o e", o=1).to_broadcast([P, NT, E]),
                                         ALU.is_ge))
            link(nc.vector.tensor_reduce(exp_f[:, :], passed[:, :, :], AX.X, ALU.add))
            link(nc.vector.tensor_tensor(passed[:, :, :], passed[:, :, :],
                                         n_tiles[:, :].rearrange("p (o e) -> p o e", o=1).to_broadcast([P, NT, E]),
                                         ALU.mult))
            link(nc.vector.tensor_reduce(off_f[:, :], passed[:, :, :], AX.X, ALU.add))
            link(nc.vector.tensor_tensor(off_f[:, :], jth[:, :, 0], off_f[:, :], ALU.subtract))
            link(nc.vector.tensor_scalar(ok_f[:, :], exp_f[:, :], float(E), float(ET), ALU.is_lt, ALU.mult))
            link(nc.vector.tensor_tensor(off_f[:, :], off_f[:, :], ok_f[:, :], ALU.mult))
            nc.vector.tensor_scalar(expert_of[:, :], exp_f[:, :], float(E - 1), None, ALU.min)
            link(nc.vector.tensor_scalar(exp_f[:, :], exp_f[:, :], float(REGION), None, ALU.mult))
            nc.vector.tensor_copy(tile_exp[:, :], expert_of[0:1, :])
            link(nc.vector.tensor_tensor(off_f[:, :], off_f[:, :], exp_f[:, :], ALU.add))
            link(nc.vector.tensor_copy(tile_row[:, :], off_f[0:1, :]))
            dve.wait_ge(S["scattered"], 16 * 2 * G * NG)
            dve.wait_ge(S["pads_stored"], 16 * (E + 2))
            dve.wait_ge(S["h_stored"], 16 * NG)
            for b in range(NBUF):
                nc.vector.memset(eup[b][CC:CC + 1, :, :], 0.0)
                nc.vector.memset(exT_hi[b][CC:CC + 1, :, :].bitcast(F32), 1.0)
                last = nc.vector.memset(exT_lo[b][CC:CC + 1, :, :].bitcast(F32), 0.0)
            last.then_inc(S["table_ready"], 1)
            table.end()

            exp_chain = Chain(dve, S["d_exp"], 4)

            def e_rows(i, b):
                dve.wait_ge(S["x_high"], NBUF * i + b + 1)
                nc.vector.tensor_tensor(exT_lo[b][0:CC, :, :], ps[0:CC, 0:2, :],
                                        exT_hi[b][0:CC, :, :].bitcast(F32), ALU.subtract).then_inc(S["x_low"], 1)

            def e_pick(i, b):
                j = NBUF * i + b
                exp_chain.begin(j)
                dve.wait_ge(e_w[b], (i + 1) * 16 * PER_TILE)
                if not isinstance(i, int) or i > 0:
                    dve.wait_ge(S["e_added"], 16 * ES * (j - NBUF + 1))
                nc.vector.tensor_copy(etoken[b][:, :], ex[b][:, :, 3])
                nc.vector.tensor_tensor(eweight[b][:, :], ex[b][:, :, 0], ex[b][:, :, 1], ALU.subtract)
                exp_chain.link(nc.vector.tensor_tensor(first_is[b][:, :], ex[b][:, :, 2],
                                                       expert_of[:, bass.ds(j, 1)].to_broadcast([P, ES]),
                                                       ALU.is_equal))
                exp_chain.link(nc.vector.tensor_tensor(eweight[b][:, :], eweight[b][:, :], first_is[b][:, :],
                                                       ALU.mult))
                exp_chain.link(nc.vector.tensor_tensor(eweight[b][:, :], eweight[b][:, :], ex[b][:, :, 1], ALU.add))

            def e_result(i, b):
                dve.wait_ge(S["e_down_psum"], NBUF * i + b + 1)
                for s in range(2):
                    last = nc.vector.tensor_tensor(
                        ey[b][:, 2 * s:2 * s + 2, :], ps[:, 6 + s, 0:2 * C].rearrange("p (t c) -> p t c", t=2),
                        eb2[b][:, :].rearrange("p (o c) -> p o c", o=1).to_broadcast([P, 2, C]), ALU.add)
                exp_chain.link(last)
                exp_chain.end()
                nc.vector.tensor_tensor(ey[b][:, :, :], ey[b][:, :, :],
                                        eweight[b][:, :].rearrange("p (s o) -> p s o", o=1).to_broadcast([P, ES, C]),
                                        ALU.mult).then_inc(S["e_y"], 1)

            def e_step(i, b):
                e_pick(i, b)
                if after(i, b):
                    e_rows(*after(i, b))
                e_result(i, b)

            e_rows(0, 0)
            expert_tiles(dve, e_step)


def kernel(**inputs):
    import numpy as _np
    import concourse.bacc as _bacc
    from concourse import mybir as _mybir
    from concourse.bass_utils import run_bass_kernel_spmd as _run

    nc = _bacc.Bacc("TRN2", target_bir_lowering=False, num_devices=1)
    w = {k: _np.asarray(v) for k, v in inputs.items()}

    def chunks(v):
        return v.reshape(2, -1).T

    laid = {
        "x": w["x"],
        "L0_tok_w": w["L0_tok_w"],
        "L0_attn_WrT": w["L0_attn_Wr"].T, "L0_attn_WkT": w["L0_attn_Wk"].T,
        "L0_attn_WvT": w["L0_attn_Wv"].T, "L0_attn_WoT": w["L0_attn_Wo"].T,
        "L0_chan": _np.stack([chunks(w[n].reshape(-1)) for n in (
            "L0_attn_time_decay", "L0_attn_time_first", "L0_attn_time_mix_k",
            "L0_attn_time_mix_v", "L0_attn_time_mix_r")], axis=1),
        "L0_ffn_upT": w["L0_ffn_in_weight"].T,
        "L0_ffn_bias": w["L0_ffn_in_bias"].reshape(-1, 128).T,
        "L0_ffn_out_weight": w["L0_ffn_out_weight"],
        "L1_attn_WqT": w["L1_attn_Wq"].T, "L1_attn_WkT": w["L1_attn_Wk"].T,
        "L1_attn_WvT": w["L1_attn_Wv"].T, "L1_attn_WoT": w["L1_attn_Wo"].T,
        "L1_attn_gq": w["L1_attn_gq"], "L1_attn_gk": w["L1_attn_gk"],
        "L1_attn_bk": w["L1_attn_bk"], "L1_attn_bv": w["L1_attn_bv"], "L1_attn_bo": w["L1_attn_bo"],
        "L1_ffn_routerT": w["L1_ffn_router_w"].T,
        "L1_ffn_w1": w["L1_ffn_w1"].reshape(-1, w["L1_ffn_w1"].shape[-1]),
        "L1_ffn_b1": w["L1_ffn_b1"],
        "L1_ffn_w2": w["L1_ffn_w2"].reshape(-1, w["L1_ffn_w2"].shape[-1]),
        "L1_ffn_b2": w["L1_ffn_b2"],
    }
    arrays, args = {}, {}
    for name, v in laid.items():
        v = _np.ascontiguousarray(v)
        arrays[f"in_{name}"] = v
        args[name] = nc.dram_tensor(f"in_{name}", v.shape, _mybir.dt.from_np(v.dtype), kind="ExternalInput").ap()
    B, T2, C = w["x"].shape
    out = nc.dram_tensor("out_0", (B, T2 // 2, C), _mybir.dt.float32, kind="ExternalOutput").ap()
    build_tower(nc, args, out)
    return _run(nc, [arrays], core_ids=[0]).results[0]["out_0"]
```

```python
from contextlib import ExitStack

import concourse.bass as bass
from concourse import mybir

ALU = mybir.AluOpType
ACT = mybir.ActivationFunctionType
AX = mybir.AxisListType
F32 = mybir.dt.float32
F32R = mybir.dt.float32r
BF16 = mybir.dt.bfloat16
U32 = mybir.dt.uint32
I32 = mybir.dt.int32

P = 128
EPS = 1e-5
STATE_FLOOR = -1e38


class Chain:

    def __init__(self, engine, sem, per_round):
        self.engine, self.sem, self.per_round = engine, sem, per_round

    def begin(self, r):
        self.base, self.n = r * self.per_round, 0

    def link(self, ins, alone=None):
        self.n += 1
        ins.then_inc(self.sem, 1)
        self.engine.wait_ge(self.sem, self.base + self.n)
        if alone:
            alone(self.engine)

    def end(self):
        assert self.n == self.per_round, (self.n, self.per_round)


def build_tower(nc, a, out):
    NB, T2, C = a["x"].shape
    T = T2 // 2
    F = a["L0_ffn_upT"].shape[1]
    E = a["L1_ffn_routerT"].shape[1]
    HEADS, HD = 12, C // 12
    KC, CC = 2, C // 2
    G = 4
    NG = NB // G
    N = G * T
    FM = F // P
    HJ, HC = 4, HEADS // 4
    ET = 512
    ES = ET // P
    REGION = NB * T + ET
    NT = NB * T * 2 // ET + E - 1
    MAXT = NB * T // ET
    NBUF = 3
    INFO = 4
    assert T == P and N == 512 and NT % NBUF == 0

    rows_in = nc.dram_tensor("expert_rows_in", (E * REGION + ET, INFO + C), F32).ap()
    total = nc.dram_tensor("total", (NB * T + ET, C), F32).ap()

    with ExitStack() as ctx:
        def sb(name, shape, dt=F32):
            return ctx.enter_context(nc.sbuf_tensor(name, shape, dt))

        ps = ctx.enter_context(nc.psum_tensor("ps", [P, 8, 512], F32))

        ident = sb("ident", [P, P])
        tile_row = sb("tile_row", [1, NT], I32)
        tile_exp = sb("tile_exp", [1, NT], I32)
        expert_of = sb("expert_of", [P, NT])
        pad_row = sb("pad_row", [1, E], I32)

        towers = ExitStack()

        def sg(name, shape, dt=F32):
            return towers.enter_context(nc.sbuf_tensor(name, shape, dt))

        before = sg("before", [P, P], BF16)
        ones_bf = sg("ones_bf", [P, P], BF16)
        neg_half = sg("neg_half", [P, 2 * G])
        lane8 = sg("lane8", [P, G, E])
        lane8_i = sg("lane8_i", [P, G, E], I32)
        region_off = sg("region_off", [P, G, E])
        region_i = sg("region_i", [P, G, E], I32)
        w_tok = sg("w_tok", [CC, KC, C])
        w_k = sg("w_k", [CC, KC, C])
        w_v = sg("w_v", [CC, KC, C])
        w_r = sg("w_r", [CC, KC, C])
        w_o = sg("w_o", [CC, KC, C])
        chan = sg("chan", [CC, 5, KC])
        decay = sg("decay", [CC, KC * G, T])
        w_up = sg("w_up", [CC, KC, F])
        b_up = sg("b_up", [P, FM])
        w_down = sg("w_down", [P, FM, C])
        w_qkv = sg("w_qkv", [CC + 1, KC, 3 * C])
        w_ao = sg("w_ao", [P, HC, C])
        gam = sg("gam", [P, 2, C])
        gamma = sg("gamma", [P, C])
        bo = sg("bo", [P, C])
        w_router = sg("w_router", [CC, KC, E])

        xt = sg("xt", [P, G, 2 * C])
        delta = xt[:, :, 0:C]
        xsum = sg("xsum", [P, G, C])
        hA = sg("hA", [P, G, C])
        hnA = sg("hnA", [P, G, C])
        statsA = sg("statsA", [P, G, 6])
        mvA = sg("mvA", [P, G, 2])
        rstdA = sg("rstdA", [P, G])
        hTA = sg("hTA", [CC, KC * G, T + 1])
        tanh_r = sg("tanh_r", [CC, KC * N])
        o_s = sg("o_s", [CC, 1 + KC * N])
        p_s = sg("p_s", [CC, 1 + KC * N])
        q_s = sg("q_s", [CC, 1 + KC * N])
        sy = sg("sy", [CC, KC * N])
        buf = [sg(f"wkv{n}", [P, KC * N]) for n in range(6)]

        def flat(n):
            return buf[n][0:CC, :]

        def steps(n):
            return buf[n][0:CC, :].rearrange("p (s t) -> p s t", t=T)

        diff, z_s = steps(0), flat(0)
        xr, keep = flat(1), steps(1)
        xk, take = flat(2), flat(2)
        xv, take_v = flat(3), flat(3)
        dT, z_neg = flat(4), steps(4)
        tanh_d, z_pos = buf[5][:, 0:G * C].rearrange("p (t c) -> p t c", c=C), steps(5)

        k_s = sg("k_s", [CC, KC * N])
        v_c = sg("v_c", [CC, KC * N])

        hB = sg("hB", [P, G, C])
        hnB = sg("hnB", [P, G, C])
        statsB = sg("statsB", [P, G, 6])
        mvB = sg("mvB", [P, G, 2])
        rstdB = sg("rstdB", [P, G])
        hTB = sg("hTB", [CC, KC, N])

        hC = sg("hC", [P, G, C])
        hnC = sg("hnC", [P, G, C])
        resC = sg("resC", [P, G, C])
        statsC = sg("statsC", [P, G, 6])
        mvC = sg("mvC", [P, G, 2])
        rstdC = sg("rstdC", [P, G])
        hTC = sg("hTC", [CC + 1, KC, N])
        statsR = sg("statsR", [P, G, 6])
        mvR = sg("mvR", [P, G, 2])
        rstdR = sg("rstdR", [P, G])
        qk = sg("qk", [P, G, 2, C])
        v_s = sg("v_s", [P, G, C])
        stats_qk = sg("stats_qk", [P, 2 * G, 6])
        mv_qk = sg("mv_qk", [P, 2 * G, 2])
        rstd_qk = sg("rstd_qk", [P, 2 * G])
        qpad = sg("qpad", [P, G, HEADS, 32])
        kpad = sg("kpad", [P, G, HEADS, 32])
        q_block = sg("q_block", [P, 2, HC, HJ, P])
        kT = sg("kT", [P, G, HC * P])
        probs = sg("probs", [P, 2, HEADS, P])
        hid = sg("hid", [P, FM, N])
        nmax = sg("nmax", [P, G, HEADS])
        psums = sg("psums", [P, G, HEADS])
        rsums = sg("rsums", [P, G, HEADS])
        vpad = sg("vpad", [P, 2, HEADS, 32])
        oT = sg("oT", [P, 2, HC * P])
        logits = sg("logits", [P, G * E])
        top8 = sg("top8", [P, G, 8])
        top_i = sg("top_i", [P, G, 8], U32)
        top_f = sg("top_f", [P, 2, G])
        gap = sg("gap", [P, G])
        egap = sg("egap", [P, G])
        esum = sg("esum", [P, G])
        hot = sg("hot", [P, 2, G, E])
        picked = sg("picked", [P, G, E], BF16)
        picked_f = sg("picked_f", [P, G, E])
        run_counts = sg("run_counts", [P, G + 1, E])
        run_bf = sg("run_bf", [P, G + 1, E], BF16)
        place = sg("place", [P, G * E])
        placed = sg("placed", [P, 2, G, E])
        slot_f = sg("slot_f", [P, 2 * G])
        slot_i = sg("slot_i", [P, 2 * G], U32)
        wts = sg("wts", [P, 2 * G])
        rowR = sg("rowR", [P, G, INFO + C])
        hnR = rowR[:, :, INFO:INFO + C]
        token_i = sg("token_i", [P, G], I32)
        token_f = sg("token_f", [P, G])
        n_tok = sg("n_tok", [P, E])
        pad_token = sg("pad_token", [P, ES], I32)
        pad_tile = xt[:, :, 0:INFO + C]
        mth_i = sg("mth_i", [P, E, MAXT], I32)
        mth = sg("mth", [P, E, MAXT])
        jth_i = sg("jth_i", [P, NT, E], I32)
        jth = sg("jth", [P, NT, E])
        n_tiles = sg("n_tiles", [P, E])
        one_row = sg("one_row", [P, E])
        tile_end = sg("tile_end", [P, E])
        passed = hid[:, 0, 0:NT * E].rearrange("p (n e) -> p n e", e=E)
        exp_f = sg("exp_f", [P, NT])
        off_f = sg("off_f", [P, NT])
        ok_f = sg("ok_f", [P, NT])

        towers.close()
        def ring(name, shape, dt=F32):
            return [sb(f"{name}{b}", shape, dt) for b in range(NBUF)]

        eup = ring("eup", [CC + 1, KC, F])
        eup_hi = ring("eup_hi", [CC + 1, KC, F], F32R)
        eup_lo = ring("eup_lo", [CC + 1, KC, F], F32R)
        edown = ring("edown", [P, FM, C])
        eb2 = ring("eb2", [P, C])
        ex = ring("ex", [P, ES, INFO + C])
        exT_hi = ring("exT_hi", [CC + 1, KC, ET], F32R)
        exT_lo = ring("exT_lo", [CC + 1, KC, ET], F32R)
        ehid = ring("ehid", [P, FM, ET])
        ey = ring("ey", [P, ES, C])
        etoken = ring("etoken", [P, ES], U32)
        eweight = ring("eweight", [P, ES])
        first_is = ring("first_is", [P, ES])

        names = """weights_in passed gaps_zeroed pool_consts dve_consts
            x_loaded x_diffed x_summed dT_psum dT_ready tok_psum tanh_ready
            a_stats a_rstd a_hn a_hT_psum a_hT xr_ready xk_ready xv_ready r_psum k_psum v_psum
            tanh_r_ready k_ready v_ready
            keep_arg keep_ready take_arg take_ready z_ready zexp_ready scans_done num_ready sy_ready
            oproj_psum hB_ready
            b_stats b_rstd b_hn b_hT_psum b_hT up_psum hid_ready down_psum hC_ready
            c_stats c_rstd c_hn c_hT_psum c_hT
            res_ready qkv_psum qkv_out qk_stats qk_rstd q_norm k_norm k_scaled kT_psum kT_ready qT_psum q_low_heads q_high_heads
            scores_psum max_ready exp_ready vpad_ready oT_psum oT_ready aproj_psum hF_ready h_stored
            r_stats r_rstd r_hn r_hT_psum r_hT
            logits_psum picked_ready place_psum gap_ready egap_ready slots_ready scattered
            counts_psum pads_ready pads_stored table_ready extra_rows
            w_high w_low e_xT_psum x_high x_low e_up_psum e_hid e_down_psum e_y e_added out_stored
            d_wkv d_tok d_b d_c d_r d_qk d_v d_route d_init d_table d_exp
            p_a p_b p_c p_r p_qk p_res p_num p_init""".split()
        S = {n: ctx.enter_context(nc.semaphore(n)) for n in names}
        e_w = [ctx.enter_context(nc.semaphore(f"e_w{b}")) for b in range(NBUF)]
        N_LOADS, SP_LOADS = 22, 6
        PER_TILE = 4
        e_rows_in = [ctx.enter_context(nc.semaphore(f"e_rows_in{b}")) for b in range(NBUF)]

        block = ctx.enter_context(nc.Block())

        def stand_alone(engine):
            engine.sem_inc(S["passed"], 1)

        def queries_out(j, t):
            return (q_block[32 * j:32 * j + 32, t % 2, :, j, :],
                    ps[32 * j:32 * j + 32, 7, 0:HC * P].rearrange("p (c q) -> p c q", c=HC))

        def stages(i):
            if isinstance(i, int):
                return [i - n if 0 <= i - n < NG else None for n in range(4)]
            return [i, i - 1, i - 2, i - 3]

        def rounds(engine, round_):
            for i in range(4):
                round_(i)
            with engine.Fori(4, NG) as i:
                round_(i)
            for i in range(NG, NG + 3):
                round_(i)

        def expert_tiles(engine, step):
            last = NT // NBUF - 1
            for b in range(NBUF):
                step(0, b)
            with engine.Fori(1, last) as i:
                for b in range(NBUF):
                    step(i, b)
            for b in range(NBUF):
                step(last, b)

        def is_first(i, b):
            return isinstance(i, int) and NBUF * i + b == 0

        def after(i, b):
            if isinstance(i, int) and NBUF * i + b == NT - 1:
                return None
            return (i, b + 1) if b + 1 < NBUF else (i + 1, 0)

        def chunked(ap):
            return ap.rearrange("(k p) n -> p k n", k=KC)

        def row(ap):
            return ap.rearrange("(o n) -> o n", o=1)

        @block.sync
        def _(sp):
            x_view = a["x"].rearrange("b (t two) c -> t b (two c)", two=2)
            sp.dma_start(xt[:, :, :], x_view[:, 0:G, :]).then_inc(S["x_loaded"], 16)
            loads = [
                (w_tok[:, :, :], chunked(a["L0_tok_w"])),
                (w_r[:, :, :], chunked(a["L0_attn_WrT"])),
                (w_k[:, :, :], chunked(a["L0_attn_WkT"])),
                (w_v[:, :, :], chunked(a["L0_attn_WvT"])),
                (w_o[:, :, :], chunked(a["L0_attn_WoT"])),
                (chan[:, :, :], a["L0_chan"]),
            ]
            for dst, src in loads:
                sp.dma_start(dst, src).then_inc(S["weights_in"], 16)
            assert len(loads) == SP_LOADS


            def load_x(g):
                sp.wait_ge(S["a_stats"], g)
                sp.dma_start(xt[:, :, :], x_view[:, bass.ds(g * G, G), :]).then_inc(S["x_loaded"], 16)

            total_view = total[0:NB * T, :].rearrange("(b p) c -> p b c", p=T)

            def store_h(g):
                sp.wait_ge(S["hF_ready"], g + 1)
                sp.dma_start(total_view[:, bass.ds(g * G, G), :], resC[:, :, :]).then_inc(S["h_stored"], 16)

            load_x(1)
            load_x(2)
            with sp.Fori(2, NG - 1) as i:
                load_x(i + 1)
                store_h(i - 2)
            for g in (NG - 3, NG - 2, NG - 1):
                store_h(g)

            sp.wait_ge(S["h_stored"], 16 * NG)
            sp.wait_ge(S["scattered"], 16 * 2 * G * NG)
            sp.wait_ge(S["table_ready"], 1)

            def load_weights(j, b):
                e = sp.value_load(tile_exp[0:1, bass.ds(j, 1)], min_val=0, max_val=E - 1)
                for dst, src in (
                    (eup[b][0:CC, :, :], a["L1_ffn_w1"][bass.ds(e * C, C), :].rearrange("(k p) n -> p k n", k=KC)),
                    (eup[b][CC:CC + 1, 0, :], a["L1_ffn_b1"][bass.ds(e, 1), :]),
                    (edown[b][:, :, :], a["L1_ffn_w2"][bass.ds(e * F, F), :].rearrange("(m p) n -> p m n", p=P)),
                    (eb2[b][:, :], a["L1_ffn_b2"][bass.ds(e, 1), :].to_broadcast([P, C])),
                ):
                    sp.dma_start(dst, src).then_inc(e_w[b], 16)

            def load_rows(j, b):
                at = sp.value_load(tile_row[0:1, bass.ds(j, 1)], min_val=0, max_val=E * REGION)
                sp.dma_start(ex[b][:, :, :], rows_in[bass.ds(at, ET), :].rearrange("(p s) c -> p s c", s=ES))\
                    .then_inc(e_rows_in[b], 16)

            load_weights(0, 0)
            sp.wait_ge(S["pads_stored"], 16 * (E + 2))
            load_rows(0, 0)
            for b in range(1, NBUF):
                load_rows(b, b)
                load_weights(b, b)
            with sp.Fori(0, NT // NBUF - 1) as i:
                for b in range(NBUF):
                    sp.wait_ge(S["e_y"], NBUF * i + b + 1)
                    load_rows(NBUF * i + b + NBUF, b)
                    load_weights(NBUF * i + b + NBUF, b)

            sp.wait_ge(S["e_added"], 16 * ES * NT)
            sp.dma_start(out.rearrange("b p c -> (b p) c"), total[0:NB * T, :]).then_inc(S["out_stored"], 16)
            sp.wait_ge(S["out_stored"], 16)

        @block.tensor
        def _(pe):
            def transposes(src, bank):
                for t in range(G):
                    for k in range(KC):
                        last = nc.tensor.transpose(ps[0:CC, bank + k, t * T:(t + 1) * T],
                                                   src[:, t, k * CC:(k + 1) * CC], ident[:, :])
                return last

            def channels_out(bank, w, rhs):
                for m in range(KC):
                    for k in range(KC):
                        last = nc.tensor.matmul(ps[0:CC, bank + m, :], w[:, k, m * CC:(m + 1) * CC],
                                                rhs[:, k * N:(k + 1) * N], start=(k == 0), stop=(k == KC - 1))
                return last

            def tokens_out(bank, xT, w):
                for t in range(G):
                    o = ps[:, bank + t // 2, (t % 2) * C:(t % 2 + 1) * C]
                    for k in range(KC):
                        last = nc.tensor.matmul(o, xT[:, k * N + t * T:k * N + (t + 1) * T], w[:, k, :],
                                                start=(k == 0), stop=(k == KC - 1))
                return last

            def a_delta(g):
                pe.wait_ge(S["x_diffed"], g + 1)
                if not isinstance(g, int) or g > 0:
                    pe.wait_ge(S["hB_ready"], g)
                transposes(xt, 0).then_inc(S["dT_psum"], 1)

            def a_scores(g):
                pe.wait_ge(S["dT_ready"], g + 1)
                tokens_out(0, dT, w_tok).then_inc(S["tok_psum"], 1)

            def a_hidden(g):
                pe.wait_ge(S["a_hn"], g + 1)
                transposes(hnA, 0).then_inc(S["a_hT_psum"], 1)

            def a_r(g):
                pe.wait_ge(S["xr_ready"], g + 1)
                channels_out(0, w_r, xr).then_inc(S["r_psum"], 1)

            def a_k(g):
                pe.wait_ge(S["xk_ready"], g + 1)
                pe.wait_ge(S["tanh_r_ready"], g + 1)
                channels_out(0, w_k, xk).then_inc(S["k_psum"], 1)

            def a_v(g):
                pe.wait_ge(S["xv_ready"], g + 1)
                pe.wait_ge(S["k_ready"], g + 1)
                channels_out(0, w_v, xv).then_inc(S["v_psum"], 1)

            def a_project(g, gc):
                pe.wait_ge(S["sy_ready"], g + 1)
                if gc is not None:
                    pe.wait_ge(S["hF_ready"], gc + 1)
                tokens_out(0, sy, w_o).then_inc(S["oproj_psum"], 1)

            def b_transposes(g):
                pe.wait_ge(S["b_hn"], g + 1)
                transposes(hnB, 2).then_inc(S["b_hT_psum"], 1)

            def c_transposes(g):
                pe.wait_ge(S["c_hn"], g + 1)
                transposes(hnC, 4).then_inc(S["c_hT_psum"], 1)

            def r_transposes(g, gc):
                pe.wait_ge(S["r_hn"], g + 1)
                if gc is not None:
                    pe.wait_ge(S["qkv_out"], G * gc + G)
                transposes(hnR, 4).then_inc(S["r_hT_psum"], 1)

            def b_mlp_up(g, ms):
                pe.wait_ge(S["b_hT"], g + 1)
                for m in ms:
                    if m >= 2:
                        pe.wait_ge(S["hid_ready"], FM * g + m - 1)
                    for k in range(KC):
                        last = nc.tensor.matmul(ps[:, 2 + m % 2, :], w_up[:, k, m * P:(m + 1) * P],
                                                hTB[:, k, :], start=(k == 0), stop=(k == KC - 1))
                    last.then_inc(S["up_psum"], 1)

            def b_mlp_down(g, ts):
                pe.wait_ge(S["hid_ready"], FM * g + FM)
                for t in ts:
                    for m in range(FM):
                        last = nc.tensor.matmul(ps[:, 2 + t // 2, (t % 2) * C:(t % 2 + 1) * C],
                                                hid[:, m, t * T:(t + 1) * T], w_down[:, m, :],
                                                start=(m == 0), stop=(m == FM - 1))
                if t == G - 1:
                    last.then_inc(S["down_psum"], 1)

            def c_qkv(g, ts):
                pe.wait_ge(S["c_hT"], g + 1)
                for t in ts:
                    if t >= 2:
                        pe.wait_ge(S["qkv_out"], G * g + t - 1)
                    bank = 4 + 2 * (t % 2)
                    for k in range(KC):
                        r = CC + 1 if k == 0 else CC
                        nc.tensor.matmul(ps[:, bank, 0:2 * C], hTC[0:r, k, t * T:(t + 1) * T],
                                         w_qkv[0:r, k, 0:2 * C], start=(k == 0), stop=(k == KC - 1))
                    for k in range(KC):
                        r = CC + 1 if k == 0 else CC
                        last = nc.tensor.matmul(ps[:, bank + 1, 0:C], hTC[0:r, k, t * T:(t + 1) * T],
                                                w_qkv[0:r, k, 2 * C:3 * C], start=(k == 0), stop=(k == KC - 1))
                    last.then_inc(S["qkv_psum"], 1)

            def heads_transposed(bank, src, t):
                for c in range(HC):
                    last = nc.tensor.transpose(ps[:, bank, c * P:(c + 1) * P],
                                               src[:, t, HJ * c:HJ * c + HJ, :].rearrange("p h d -> p (h d)"),
                                               ident[:, :])
                return last

            def c_keys(g, gr):
                if gr is not None:
                    pe.wait_ge(S["slots_ready"], gr + 1)
                pe.wait_ge(S["k_scaled"], g + 1)
                for t in range(G):
                    heads_transposed(4 + t, kpad, t).then_inc(S["kT_psum"], 1)

            def c_queries(g, t):
                if t == 0:
                    pe.wait_ge(S["q_norm"], g + 1)
                    pe.wait_ge(S["kT_ready"], G * g + G)
                else:
                    pe.wait_ge(S["q_low_heads"], G * g + t)
                    pe.wait_ge(S["q_high_heads"], G * g + t)
                heads_transposed(7, qpad, t).then_inc(S["qT_psum"], 1)

            def c_scores(g, t, c):
                if c == 0:
                    pe.wait_ge(S["q_low_heads"], G * g + t + 1)
                    pe.wait_ge(S["q_high_heads"], G * g + t + 1)
                if t == 0:
                    pe.wait_ge(S["kT_ready"], G * g + G)
                else:
                    pe.wait_ge(S["exp_ready"], HC * (G * g + t - 1) + c + 1)
                nc.tensor.matmul(ps[:, 4 + c, :], kT[:, t, c * P:(c + 1) * P],
                                 q_block[:, t % 2, c, :, :].rearrange("p j q -> p (j q)"),
                                 start=True, stop=True).then_inc(S["scores_psum"], 1)

            def c_values(g, t, gb):
                pe.wait_ge(S["vpad_ready"], G * g + t + 1)
                if t == 0 and gb is not None:
                    pe.wait_ge(S["hC_ready"], gb + 1)
                for c in range(HC):
                    for j in range(HJ):
                        last = nc.tensor.matmul(ps[32 * j:32 * j + 32, 2 + t % 2, c * P:(c + 1) * P],
                                                vpad[:, t % 2, HJ * c + j, :], probs[:, t % 2, HJ * c + j, :],
                                                start=True, stop=True)
                last.then_inc(S["oT_psum"], 1)

            def c_project(g, t, ga):
                if t == 0 and ga is not None:
                    pe.wait_ge(S["v_ready"], ga + 1)
                pe.wait_ge(S["oT_ready"], G * g + t + 1)
                for c in range(HC):
                    last = nc.tensor.matmul(ps[:, t // 2, (t % 2) * C:(t % 2 + 1) * C],
                                            oT[:, t % 2, c * P:(c + 1) * P], w_ao[:, c, :],
                                            start=(c == 0), stop=(c == HC - 1))
                if t == G - 1:
                    last.then_inc(S["aproj_psum"], 1)

            def r_logits(g):
                pe.wait_ge(S["r_hT"], g + 1)
                for t in range(G):
                    for k in range(KC):
                        last = nc.tensor.matmul(ps[:, 6, t * E:(t + 1) * E], hTC[0:CC, k, t * T:(t + 1) * T],
                                                w_router[:, k, :], start=(k == 0), stop=(k == KC - 1))
                last.then_inc(S["logits_psum"], 1)

            def r_places(g):
                pe.wait_ge(S["picked_ready"], g + 1)
                nc.tensor.matmul(ps[:, 7, 0:G * E], before[:, :], picked[:, :, :].rearrange("p t e -> p (t e)"),
                                 start=True, stop=False)
                nc.tensor.matmul(ps[:, 7, 0:G * E], ones_bf[:, :],
                                 run_bf[:, 0:G, :].rearrange("p t e -> p (t e)"),
                                 start=False, stop=True).then_inc(S["place_psum"], 1)

            def round_(i):
                ga, gb, gc, gr = stages(i)
                A, B, CA, R = (g is not None for g in (ga, gb, gc, gr))
                if CA: c_transposes(gc)
                if CA: c_qkv(gc, (0,))
                if CA: c_qkv(gc, (1,))
                if CA: c_qkv(gc, (2,))
                if CA: c_qkv(gc, (3,))
                if B: a_project(gb, gr)
                if R: r_transposes(gr, gc)
                if A: a_delta(ga)
                if R: r_logits(gr)
                if A: a_scores(ga)
                if B: b_transposes(gb)
                if B: b_mlp_up(gb, (0,))
                if B: b_mlp_up(gb, (1,))
                if R: r_places(gr)
                if B: b_mlp_up(gb, (2,))
                if A: a_hidden(ga)
                if B: b_mlp_up(gb, (3,))
                if B: b_mlp_up(gb, (4,))
                if B: b_mlp_up(gb, (5,))
                if CA: c_keys(gc, gr)
                if A: a_r(ga)
                if B: b_mlp_down(gb, (0,))
                if A: a_k(ga)
                if B: b_mlp_down(gb, (1,))
                if A: a_v(ga)
                if CA: c_queries(gc, 0)
                if B: b_mlp_down(gb, (2,))
                if B: b_mlp_down(gb, (3,))
                if CA: c_scores(gc, 0, 0)
                if CA: c_scores(gc, 0, 1)
                if CA: c_scores(gc, 0, 2)
                if CA: c_queries(gc, 1)
                if CA: c_scores(gc, 1, 0)
                if CA: c_scores(gc, 1, 1)
                if CA: c_queries(gc, 2)
                if CA: c_scores(gc, 1, 2)
                if CA: c_values(gc, 0, gb)
                if CA: c_scores(gc, 2, 0)
                if CA: c_scores(gc, 2, 1)
                if CA: c_queries(gc, 3)
                if CA: c_scores(gc, 2, 2)
                if CA: c_values(gc, 1, gb)
                if CA: c_scores(gc, 3, 0)
                if CA: c_scores(gc, 3, 1)
                if CA: c_project(gc, 0, ga)
                if CA: c_scores(gc, 3, 2)
                if CA: c_project(gc, 1, ga)
                if CA: c_values(gc, 2, gb)
                if CA: c_project(gc, 2, ga)
                if CA: c_values(gc, 3, gb)
                if CA: c_project(gc, 3, ga)

            pe.wait_ge(S["weights_in"], 16 * N_LOADS)
            pe.wait_ge(S["pool_consts"], 1)
            pe.wait_ge(S["dve_consts"], 1)
            rounds(pe, round_)

            pe.wait_ge(S["slots_ready"], NG)
            nc.tensor.matmul(ps[:, 7, 0:E], ones_bf[:, :], run_bf[:, G, :],
                             start=True, stop=True).then_inc(S["counts_psum"], 1)

            def e_transposes(i, b):
                pe.wait_ge(e_rows_in[b], (i + 1) * 16)
                for s in range(ES):
                    for k in range(KC):
                        last = nc.tensor.transpose(ps[0:CC, k, s * P:(s + 1) * P],
                                                   ex[b][:, s, INFO + k * CC:INFO + (k + 1) * CC], ident[:, :])
                last.then_inc(S["e_xT_psum"], 1)

            def e_up(i, b):
                j = NBUF * i + b
                pe.wait_ge(S["x_low"], j + 1)
                pe.wait_ge(S["w_low"], j + 1)
                for m in range(FM):
                    if m >= 4:
                        pe.wait_ge(S["e_hid"], FM * j + m - 3)
                    terms = [(w, x, k) for w, x in ((eup_hi, exT_hi), (eup_hi, exT_lo), (eup_lo, exT_hi))
                             for k in range(KC)]
                    for n, (w, x, k) in enumerate(terms):
                        r = CC + 1 if k == 0 else CC
                        last = nc.tensor.matmul(ps[:, 2 + m % 4, :], w[b][0:r, k, m * P:(m + 1) * P],
                                                x[b][0:r, k, :], start=(n == 0), stop=(n == len(terms) - 1))
                    last.then_inc(S["e_up_psum"], 1)

            def e_down(i, b):
                j = NBUF * i + b
                pe.wait_ge(S["e_hid"], FM * j + FM)
                pe.wait_ge(e_w[b], (i + 1) * 16 * PER_TILE)
                if not is_first(i, b):
                    pe.wait_ge(S["e_y"], j)
                for s in range(ES):
                    for m in range(FM):
                        last = nc.tensor.matmul(ps[:, 6 + s // 2, (s % 2) * C:(s % 2 + 1) * C],
                                                ehid[b][:, m, s * P:(s + 1) * P], edown[b][:, m, :],
                                                start=(m == 0), stop=(m == FM - 1))
                last.then_inc(S["e_down_psum"], 1)

            def e_step(i, b):
                e_up(i, b)
                if after(i, b):
                    e_transposes(*after(i, b))
                e_down(i, b)

            e_transposes(0, 0)
            pe.wait_ge(S["extra_rows"], NBUF)
            expert_tiles(pe, e_step)

        @block.scalar
        def _(act):
            def two(bank, rows, cols):
                return ps[0:rows, bank:bank + 2, 0:cols]

            def a_delta(g):
                act.wait_ge(S["dT_psum"], g + 1)
                nc.scalar.activation(dT.rearrange("p (k n) -> p k n", k=KC), two(0, CC, N),
                                     ACT.Copy).then_inc(S["dT_ready"], 1)

            def a_scores(g):
                act.wait_ge(S["tok_psum"], g + 1)
                nc.scalar.activation(tanh_d.rearrange("p (h t) c -> p h (t c)", h=2), two(0, P, 2 * C),
                                     ACT.Tanh, scale=0.5).then_inc(S["tanh_ready"], 1)

            def a_hidden(g):
                act.wait_ge(S["a_hT_psum"], g + 1)
                nc.scalar.activation(hTA[:, :, 1:T + 1],
                                     two(0, CC, N).rearrange("p k (g t) -> p (k g) t", t=T),
                                     ACT.Copy).then_inc(S["a_hT"], 1)

            def a_gate(g):
                act.wait_ge(S["r_psum"], g + 1)
                nc.scalar.activation(tanh_r[:, :].rearrange("p (k n) -> p k n", k=KC), two(0, CC, N),
                                     ACT.Tanh, scale=0.5).then_inc(S["tanh_r_ready"], 1)

            def a_kv(g, name, dst):
                act.wait_ge(S[f"{name}_psum"], g + 1)
                nc.scalar.activation(dst[:, :].rearrange("p (k n) -> p k n", k=KC), two(0, CC, N),
                                     ACT.Copy).then_inc(S[f"{name}_ready"], 1)

            def a_keep_exp(g):
                act.wait_ge(S["keep_arg"], g + 1)
                nc.scalar.activation(keep[:, :, 1:T], keep[:, :, 1:T], ACT.Exp).then_inc(S["keep_ready"], 1)

            def a_take_exp(g):
                act.wait_ge(S["take_arg"], g + 1)
                nc.scalar.activation(take, take, ACT.Exp).then_inc(S["take_ready"], 1)

            def a_z_exps(g):
                act.wait_ge(S["z_ready"], g + 1)
                nc.scalar.activation(z_neg[:, :, 1:T], z_neg[:, :, 1:T], ACT.Exp)
                nc.scalar.activation(z_pos[:, :, 1:T], z_pos[:, :, 1:T], ACT.Exp,
                                     scale=-1.0).then_inc(S["zexp_ready"], 1)

            def transposed(g, name, dst, bank):
                act.wait_ge(S[f"{name}_hT_psum"], g + 1)
                nc.scalar.activation(dst[0:CC, :, :], two(bank, CC, N), ACT.Copy).then_inc(S[f"{name}_hT"], 1)

            def b_gelu(g, m):
                act.wait_ge(S["up_psum"], FM * g + m + 1)
                nc.scalar.activation(hid[:, m, :], ps[:, 2 + m % 2, :], ACT.Gelu,
                                     bias=b_up[:, m:m + 1]).then_inc(S["hid_ready"], 1)

            def c_qkv(g, t):
                act.wait_ge(S["qkv_psum"], G * g + t + 1)
                bank = 4 + 2 * (t % 2)
                nc.scalar.activation(qk[:, t, :, :].rearrange("p n c -> p (n c)"), ps[:, bank, 0:2 * C], ACT.Copy)
                nc.scalar.activation(v_s[:, t, :], ps[:, bank + 1, 0:C], ACT.Copy).then_inc(S["qkv_out"], 1)

            def c_queries(g, t):
                act.wait_ge(S["qT_psum"], G * g + t + 1)
                for j in range(0, 2):
                    last = nc.scalar.activation(*queries_out(j, t), ACT.Copy)
                last.then_inc(S["q_low_heads"], 1)

            def c_exps(g, t, c):
                act.wait_ge(S["max_ready"], HC * (G * g + t) + c + 1)
                for j in range(HJ):
                    n = HJ * c + j
                    last = nc.scalar.activation(probs[:, t % 2, n, :], ps[:, 4 + c, j * P:(j + 1) * P], ACT.Exp,
                                                bias=nmax[:, t, n:n + 1], accum_out=psums[:, t, n:n + 1])
                last.then_inc(S["exp_ready"], 1)

            def c_values(g, t):
                act.wait_ge(S["oT_psum"], G * g + t + 1)
                nc.scalar.activation(oT[:, t % 2, :], ps[:, 2 + t % 2, 0:HC * P],
                                     ACT.Copy).then_inc(S["oT_ready"], 1)

            def r_gap(g):
                act.wait_ge(S["gap_ready"], g + 1)
                nc.scalar.activation(egap[:, :], gap[:, :], ACT.Exp).then_inc(S["egap_ready"], 1)

            def round_(i):
                ga, gb, gc, gr = stages(i)
                A, B, CA, R = (g is not None for g in (ga, gb, gc, gr))
                if CA: transposed(gc, "c", hTC, 4)
                if CA: c_qkv(gc, 0)
                if CA: c_qkv(gc, 1)
                if CA: c_qkv(gc, 2)
                if CA: c_qkv(gc, 3)
                if R: transposed(gr, "r", hTC, 4)
                if A: a_delta(ga)
                if A: a_scores(ga)
                if B: transposed(gb, "b", hTB, 2)
                if R: r_gap(gr)
                if B: b_gelu(gb, 0)
                if B: b_gelu(gb, 1)
                if B: b_gelu(gb, 2)
                if A: a_hidden(ga)
                if B: b_gelu(gb, 3)
                if B: b_gelu(gb, 4)
                if B: b_gelu(gb, 5)
                if A: a_gate(ga)
                if A: a_kv(ga, "k", k_s)
                if A: a_kv(ga, "v", v_c)
                if CA: c_queries(gc, 0)
                if CA: c_exps(gc, 0, 0)
                if CA: c_queries(gc, 1)
                if CA: c_exps(gc, 0, 1)
                if A: a_take_exp(ga)
                if CA: c_exps(gc, 0, 2)
                if A: a_keep_exp(ga)
                if CA: c_exps(gc, 1, 0)
                if CA: c_exps(gc, 1, 1)
                if CA: c_queries(gc, 2)
                if CA: c_exps(gc, 1, 2)
                if A: a_z_exps(ga)
                if CA: c_exps(gc, 2, 0)
                if CA: c_exps(gc, 2, 1)
                if CA: c_queries(gc, 3)
                if CA: c_values(gc, 0)
                if CA: c_exps(gc, 2, 2)
                if CA: c_values(gc, 1)
                if CA: c_exps(gc, 3, 0)
                if CA: c_exps(gc, 3, 1)
                if CA: c_exps(gc, 3, 2)
                if CA: c_values(gc, 2)
                if CA: c_values(gc, 3)

            loads = [
                (w_up[:, :, :], chunked(a["L0_ffn_upT"])),
                (b_up[:, :], a["L0_ffn_bias"]),
                (w_down[:, :, :], a["L0_ffn_out_weight"].rearrange("(m p) n -> p m n", p=P)),
                (w_qkv[0:CC, :, 0:C], chunked(a["L1_attn_WqT"])),
                (w_qkv[0:CC, :, C:2 * C], chunked(a["L1_attn_WkT"])),
                (w_qkv[0:CC, :, 2 * C:3 * C], chunked(a["L1_attn_WvT"])),
                (gam[:, 0, :], row(a["L1_attn_gq"]).to_broadcast([P, C])),
                (gam[:, 1, :], row(a["L1_attn_gk"]).to_broadcast([P, C])),
                (bo[:, :], row(a["L1_attn_bo"]).to_broadcast([P, C])),
                (w_router[:, :, :], chunked(a["L1_ffn_routerT"])),
            ]
            for dst, src in loads:
                act.dma_start(dst, src).then_inc(S["weights_in"], 16)
            act.wait_ge(S["gaps_zeroed"], 2)
            wo = a["L1_attn_WoT"].rearrange("(c j d) n -> j d c n", j=HJ, d=HD)
            gaps = [(w_ao[32 * j:32 * j + HD, :, :], wo[j]) for j in range(HJ)]
            gaps += [(w_qkv[CC:CC + 1, 0, C:2 * C], row(a["L1_attn_bk"])),
                     (w_qkv[CC:CC + 1, 0, 2 * C:3 * C], row(a["L1_attn_bv"]))]
            for dst, src in gaps:
                act.dma_start(dst, src).then_inc(S["weights_in"], 16)
            assert len(loads) + len(gaps) == N_LOADS - SP_LOADS
            act.wait_ge(S["weights_in"], 16 * N_LOADS)
            act.wait_ge(S["dve_consts"], 1)
            rounds(act, round_)

            act.wait_ge(S["pads_ready"], 1)
            for e in range(E):
                at = act.value_load(pad_row[0:1, e:e + 1], min_val=e * REGION, max_val=(e + 1) * REGION - ET)
                act.dma_start(rows_in[bass.ds(at, ET), :].rearrange("(p s) c -> p s c", s=ES),
                             pad_tile).then_inc(S["pads_stored"], 16)
            act.dma_start(rows_in[E * REGION:E * REGION + ET, :].rearrange("(p s) c -> p s c", s=ES),
                         pad_tile).then_inc(S["pads_stored"], 16)
            act.dma_start(total[NB * T:NB * T + ET, :].rearrange("(p s) c -> p s c", s=ES),
                         pad_tile[:, :, INFO:INFO + C]).then_inc(S["pads_stored"], 16)

            def e_weights(i, b):
                act.wait_ge(e_w[b], (i + 1) * 16 * PER_TILE)
                nc.scalar.activation(eup_hi[b][:, :, :], eup[b][:, :, :], ACT.Copy).then_inc(S["w_high"], 1)

            def e_rows(i, b):
                act.wait_ge(S["e_xT_psum"], NBUF * i + b + 1)
                nc.scalar.activation(exT_hi[b][0:CC, :, :], ps[0:CC, 0:2, :], ACT.Copy).then_inc(S["x_high"], 1)

            def e_gelu(i, b, ms):
                for m in ms:
                    act.wait_ge(S["e_up_psum"], FM * (NBUF * i + b) + m + 1)
                    nc.scalar.activation(ehid[b][:, m, :], ps[:, 2 + m % 4, :],
                                         ACT.Gelu).then_inc(S["e_hid"], 1)

            def e_step(i, b):
                e_gelu(i, b, range(0, 3))
                if after(i, b):
                    e_weights(*after(i, b))
                e_gelu(i, b, range(3, FM))
                if after(i, b):
                    e_rows(*after(i, b))

            act.wait_ge(S["extra_rows"], NBUF)
            e_weights(0, 0)
            e_rows(0, 0)
            expert_tiles(act, e_step)

        @block.gpsimd
        def _(pool):
            init = Chain(pool, S["p_init"], 11)
            init.begin(0)
            nc.gpsimd.memset(w_ao[:, :, :], 0.0).then_inc(S["gaps_zeroed"], 1)
            pool.wait_ge(S["gaps_zeroed"], 1)
            nc.gpsimd.memset(w_qkv[CC:CC + 1, 0, :], 0.0).then_inc(S["gaps_zeroed"], 1)
            pool.wait_ge(S["gaps_zeroed"], 2)
            init.link(nc.gpsimd.memset(ident[:, :], 0.0))
            init.link(nc.gpsimd.memset(ones_bf[:, :], 1.0))
            init.link(nc.gpsimd.affine_select(out=ident[:, :], in_=ident[:, :], compare_op=ALU.not_equal, fill=1.0,
                                              base=0, pattern=[[-1, P]], channel_multiplier=1))
            init.link(nc.gpsimd.affine_select(out=before[:, :], in_=ones_bf[:, :], compare_op=ALU.is_gt, fill=0.0,
                                              base=0, pattern=[[1, P]], channel_multiplier=-1))
            init.link(nc.gpsimd.memset(neg_half[:, :], -0.5))
            init.link(nc.gpsimd.iota(lane8_i[:, :, :], [[0, G], [1, E]], base=0, channel_multiplier=0))
            init.link(nc.gpsimd.iota(region_i[:, :, :], [[0, G], [REGION, E]], base=0, channel_multiplier=0))
            init.link(nc.gpsimd.iota(pad_token[:, :], [[1, ES]], base=NB * T, channel_multiplier=ES))
            init.link(nc.gpsimd.iota(token_i[:, :], [[T, G]], base=0, channel_multiplier=1))
            init.link(nc.gpsimd.iota(mth_i[:, :, :], [[0, E], [ET, MAXT]], base=0, channel_multiplier=0))
            init.link(nc.gpsimd.iota(jth_i[:, :, :], [[1, NT], [0, E]], base=0, channel_multiplier=0))
            init.end()
            pool.sem_inc(S["pool_consts"], 1)
            pool.wait_ge(S["weights_in"], 16 * N_LOADS)
            pool.wait_ge(S["dve_consts"], 1)

            res = Chain(pool, S["p_res"], 1)
            num = Chain(pool, S["p_num"], 1)

            def rstd(g, name, out_, mv, n):
                chain = Chain(pool, S[f"p_{name}"], 1)
                chain.begin(g)
                pool.wait_ge(S[f"{name}_stats"], g + 1)
                stand_alone(pool)
                chain.link(nc.gpsimd.tensor_scalar(out_, mv[:, :, 1], EPS, None, ALU.add))
                chain.end()
                nc.gpsimd.tensor_tensor(out_, out_, neg_half[:, 0:n], ALU.pow).then_inc(S[f"{name}_rstd"], 1)

            def a_sum(g):
                pool.wait_ge(S["x_loaded"], 16 * (g + 1))
                if not isinstance(g, int) or g > 0:
                    pool.wait_ge(S["a_stats"], g)
                nc.gpsimd.tensor_tensor(xsum[:, :, :], xt[:, :, 0:C], xt[:, :, C:2 * C],
                                        ALU.add).then_inc(S["x_summed"], 1)

            def a_num(g):
                num.begin(g)
                pool.wait_ge(S["scans_done"], g + 1)
                pool.wait_ge(S["zexp_ready"], g + 1)
                nc.gpsimd.tensor_tensor(take_v, buf[5][0:CC, :], p_s[:, 0:KC * N], ALU.mult)
                num.link(nc.gpsimd.tensor_tensor(take, buf[4][0:CC, :], v_c[:, :], ALU.mult))
                num.end()
                nc.gpsimd.tensor_tensor(take_v, take_v, take, ALU.add).then_inc(S["num_ready"], 1)

            def c_residual(g):
                pool.wait_ge(S["c_hn"], g + 1)
                if not isinstance(g, int) or g > 0:
                    pool.wait_ge(S["r_hn"], g)
                    pool.wait_ge(S["h_stored"], 16 * g)
                res.begin(g)
                res.link(nc.gpsimd.tensor_tensor(resC[:, :, :], hC[:, :, :], hnC[:, :, :], ALU.add))
                res.end()
                nc.gpsimd.tensor_tensor(resC[:, :, :], resC[:, :, :],
                                        bo[:, :].rearrange("p (o c) -> p o c", o=1).to_broadcast([P, G, C]),
                                        ALU.add).then_inc(S["res_ready"], 1)

            def c_k_scale(g):
                pool.wait_ge(S["k_norm"], g + 1)
                for t in range(G):
                    last = nc.gpsimd.tensor_tensor(kpad[:, t, :, 0:HD], kpad[:, t, :, 0:HD],
                                                   gamma[:, :].rearrange("p (h d) -> p h d", d=HD), ALU.mult)
                last.then_inc(S["k_scaled"], 1)

            def r_scatter(g):
                pool.wait_ge(S["slots_ready"], g + 1)
                stand_alone(pool)
                for s in range(2):
                    for t in range(G):
                        n = s * G + t
                        nc.gpsimd.indirect_dma_start(
                            rows_in, bass.IndirectOffsetOnAxis(ap=slot_i[:, n:n + 1], axis=0),
                            rowR[:, t, :], None).then_inc(S["scattered"], 16)

            def round_(i):
                ga, gb, gc, gr = stages(i)
                A, B, CA, R = (g is not None for g in (ga, gb, gc, gr))
                if A: a_sum(ga)
                if R: rstd(gr, "r", rstdR[:, :], mvR, G)
                if CA: rstd(gc, "qk", rstd_qk[:, :], mv_qk, 2 * G)
                if B: rstd(gb, "b", rstdB[:, :], mvB, G)
                if A: rstd(ga, "a", rstdA[:, :], mvA, G)
                if CA: c_k_scale(gc)
                if CA: c_residual(gc)
                if B: rstd(gb, "c", rstdC[:, :], mvC, G)
                if R: r_scatter(gr)
                if A: a_num(ga)

            rounds(pool, round_)

            def e_weights(i, b):
                pool.wait_ge(S["w_high"], NBUF * i + b + 1)
                nc.gpsimd.tensor_tensor(eup_lo[b][:, :, :], eup[b][:, :, :], eup_hi[b][:, :, :].bitcast(F32),
                                        ALU.subtract).then_inc(S["w_low"], 1)

            def e_add(i, b):
                j = NBUF * i + b
                pool.wait_ge(S["e_y"], j + 1)
                if not is_first(i, b):
                    pool.wait_ge(S["e_added"], 16 * ES * j)
                stand_alone(pool)
                for s in range(ES):
                    nc.gpsimd.indirect_dma_start(
                        total, bass.IndirectOffsetOnAxis(ap=etoken[b][:, s:s + 1], axis=0),
                        ey[b][:, s, :], None, compute_op=ALU.add).then_inc(S["e_added"], 16)

            def e_step(i, b):
                if after(i, b):
                    e_weights(*after(i, b))
                e_add(i, b)

            pool.wait_ge(S["pads_stored"], 16 * (E + 2))
            e_weights(0, 0)
            expert_tiles(pool, e_step)

        @block.vector
        def _(dve):
            init = Chain(dve, S["d_init"], 2)
            init.begin(0)
            nc.vector.memset(hTA[:, :, 0:1], 0.0)
            nc.vector.memset(o_s[:, 0:1], 0.0)
            nc.vector.memset(p_s[:, 0:1], 0.0)
            nc.vector.memset(q_s[:, 0:1], 0.0)
            nc.vector.memset(run_counts[:, :, :], 0.0)
            nc.vector.memset(qpad[:, :, :, :], 0.0)
            nc.vector.memset(q_block[:, :, :, :, :], 0.0)
            nc.vector.memset(kpad[:, :, :, :], 0.0)
            nc.vector.memset(vpad[:, :, :, :], 0.0)
            nc.vector.memset(one_row[:, :], 1.0)
            init.link(nc.vector.memset(hTC[CC:CC + 1, :, :], 1.0))
            dve.wait_ge(S["weights_in"], 16 * N_LOADS)
            dve.wait_ge(S["pool_consts"], 1)
            for k in range(KC):
                nc.vector.tensor_copy(decay[:, k * G:(k + 1) * G, :].rearrange("p g t -> p (g t)"),
                                      chan[:, 0, k:k + 1].to_broadcast([CC, N]))
            nc.vector.scalar_tensor_tensor(gamma[:, :], gam[:, 0, :], float(HD) ** -0.5, gam[:, 1, :],
                                           ALU.mult, ALU.mult)
            nc.vector.tensor_copy(lane8[:, :, :], lane8_i[:, :, :])
            nc.vector.tensor_copy(token_f[:, :], token_i[:, :])
            nc.vector.tensor_copy(mth[:, :, :], mth_i[:, :, :])
            nc.vector.tensor_copy(jth[:, :, :], jth_i[:, :, :])
            init.link(nc.vector.tensor_copy(region_off[:, :, :], region_i[:, :, :]))
            nc.vector.memset(decay[:, :, 0:1], STATE_FLOOR).then_inc(S["dve_consts"], 1)
            init.end()

            tok = Chain(dve, S["d_tok"], 4)
            wkv = Chain(dve, S["d_wkv"], 8)
            lns = {name: Chain(dve, S[f"d_{name}"], 1) for name in "bcr"}
            qkc = Chain(dve, S["d_qk"], 1)
            vch = Chain(dve, S["d_v"], G)
            route = Chain(dve, S["d_route"], 18)

            def statistics(chain, src, st, mv, n):
                for t in range(n):
                    last = nc.vector.bn_stats(st[:, t, :], src(t))
                chain.link(last, stand_alone)
                for t in range(n):
                    last = nc.vector.bn_aggr(mv[:, t, :], st[:, t, :])
                return last

            def normalise(dst, src, mv, rs, ts):
                for n, t in enumerate(ts):
                    last = nc.vector.tensor_scalar(dst(n), src(n), mv[:, t, 0:1], rs[:, t:t + 1],
                                                   ALU.subtract, ALU.mult)
                return last

            def a_delta(g):
                dve.wait_ge(S["x_summed"], g + 1)
                nc.vector.tensor_tensor(delta, xt[:, :, 0:C], xt[:, :, C:2 * C],
                                        ALU.subtract).then_inc(S["x_diffed"], 1)

            def a_tokens(g):
                dve.wait_ge(S["tanh_ready"], g + 1)
                tok.begin(g)
                tok.link(nc.vector.scalar_tensor_tensor(tanh_d, tanh_d, 0.5, delta, ALU.mult, ALU.mult))
                dve.wait_ge(S["x_summed"], g + 1)
                tok.link(nc.vector.scalar_tensor_tensor(hA[:, :, :], xsum[:, :, :], 0.5, tanh_d, ALU.mult, ALU.add))
                statistics(tok, lambda t: hA[:, t, :], statsA, mvA, G).then_inc(S["a_stats"], 1)

            def a_normalise(g):
                dve.wait_ge(S["a_rstd"], g + 1)
                normalise(lambda t: hnA[:, t, :], lambda t: hA[:, t, :], mvA, rstdA,
                          range(G)).then_inc(S["a_hn"], 1)

            def a_mix(g):
                dve.wait_ge(S["a_hT"], g + 1)
                tok.link(nc.vector.tensor_tensor(diff, hTA[:, :, 1:T + 1], hTA[:, :, 0:T], ALU.subtract))
                tok.end()
                for mix, dst, name in ((4, xr, "xr_ready"), (2, xk, "xk_ready"), (3, xv, "xv_ready")):
                    for k in range(KC):
                        last = nc.vector.scalar_tensor_tensor(
                            dst[:, k * N:(k + 1) * N].rearrange("p (g t) -> p g t", t=T),
                            diff[:, k * G:(k + 1) * G, :], chan[:, mix, k:k + 1],
                            hTA[:, k * G:(k + 1) * G, 0:T], ALU.mult, ALU.add)
                    last.then_inc(S[name], 1)

            M = KC * N
            keep_flat = flat(1)
            z_neg_flat, z_pos_flat = flat(4), flat(5)

            def a_exponents(g):
                dve.wait_ge(S["k_ready"], g + 1)
                wkv.begin(g)
                wkv.link(nc.vector.tensor_tensor_scan(o_s[:, 1:M + 1], decay[:, :, :].rearrange("p g t -> p (g t)"),
                                                      k_s[:, :], 0.0, ALU.add, ALU.max))
                for k in range(KC):
                    nc.vector.scalar_tensor_tensor(
                        keep[:, k * G:(k + 1) * G, 1:T],
                        o_s[:, k * N:(k + 1) * N].rearrange("p (g t) -> p g t", t=T)[:, :, 1:T],
                        chan[:, 0, k:k + 1],
                        o_s[:, 1 + k * N:1 + (k + 1) * N].rearrange("p (g t) -> p g t", t=T)[:, :, 1:T],
                        ALU.add, ALU.subtract)
                nc.vector.memset(keep[:, :, 0:1], 0.0).then_inc(S["keep_arg"], 1)
                nc.vector.tensor_tensor(take, k_s[:, :], o_s[:, 1:M + 1], ALU.subtract).then_inc(S["take_arg"], 1)

            def a_fraction_args(g):
                for k in range(KC):
                    last = nc.vector.scalar_tensor_tensor(z_s[:, k * N:(k + 1) * N], k_s[:, k * N:(k + 1) * N],
                                                          chan[:, 1, k:k + 1], o_s[:, k * N:(k + 1) * N],
                                                          ALU.add, ALU.subtract)
                wkv.link(last)
                z_steps = steps(0)
                nc.vector.tensor_scalar(z_neg[:, :, 1:T], z_steps[:, :, 1:T], 0.0, None, ALU.min)
                nc.vector.tensor_scalar(z_pos[:, :, 1:T], z_steps[:, :, 1:T], 0.0, None, ALU.max)
                nc.vector.memset(z_neg[:, :, 0:1], 1.0)
                nc.vector.memset(z_pos[:, :, 0:1], 0.0).then_inc(S["z_ready"], 1)

            def a_scan_p(g):
                dve.wait_ge(S["take_ready"], g + 1)
                dve.wait_ge(S["v_ready"], g + 1)
                wkv.link(nc.vector.tensor_tensor(take_v, take, v_c[:, :], ALU.mult))
                dve.wait_ge(S["keep_ready"], g + 1)
                nc.vector.tensor_tensor_scan(p_s[:, 1:M + 1], keep_flat, take_v, 0.0, ALU.mult, ALU.add)

            def a_scan_q(g):
                wkv.link(nc.vector.tensor_tensor_scan(q_s[:, 1:M + 1], keep_flat, take, 0.0, ALU.mult, ALU.add))
                dve.sem_inc(S["scans_done"], 1)

            def a_denominator(g):
                dve.wait_ge(S["zexp_ready"], g + 1)
                wkv.link(nc.vector.tensor_tensor(keep_flat, z_pos_flat, q_s[:, 0:M], ALU.mult))
                wkv.link(nc.vector.tensor_tensor(keep_flat, keep_flat, z_neg_flat, ALU.add))

            def a_reciprocal(g, n):
                q = M // 4
                last = nc.vector.reciprocal(keep_flat[:, n * q:(n + 1) * q], keep_flat[:, n * q:(n + 1) * q])
                if n == 3:
                    wkv.link(last)

            def a_gate(g):
                dve.wait_ge(S["num_ready"], g + 1)
                dve.wait_ge(S["tanh_r_ready"], g + 1)
                wkv.link(nc.vector.scalar_tensor_tensor(take, tanh_r[:, :], 1.0, take_v, ALU.add, ALU.mult))
                wkv.end()
                nc.vector.tensor_tensor(sy[:, :], take, keep_flat, ALU.mult).then_inc(S["sy_ready"], 1)

            def a_residual(g):
                dve.wait_ge(S["oproj_psum"], g + 1)
                nc.vector.scalar_tensor_tensor(
                    hB[:, :, :].rearrange("p (h t) c -> p h (t c)", h=2), ps[:, 0:2, 0:2 * C], 0.5,
                    hA[:, :, :].rearrange("p (h t) c -> p h (t c)", h=2), ALU.mult, ALU.add).then_inc(S["hB_ready"], 1)

            def ln_stats(g, name, src, st, mv):
                chain = lns[name]
                chain.begin(g)
                statistics(chain, lambda t: src[:, t, :], st, mv, G).then_inc(S[f"{name}_stats"], 1)
                chain.end()

            def ln_out(g, name, dst, src, mv, rs):
                dve.wait_ge(S[f"{name}_rstd"], g + 1)
                normalise(lambda t: dst[:, t, :], lambda t: src[:, t, :], mv, rs,
                          range(G)).then_inc(S[f"{name}_hn"], 1)

            def b_mlp_add(g, gc):
                dve.wait_ge(S["down_psum"], g + 1)
                if gc is not None:
                    dve.wait_ge(S["res_ready"], gc + 1)
                nc.vector.tensor_tensor(hC[:, :, :].rearrange("p (h t) c -> p h (t c)", h=2), ps[:, 2:4, 0:2 * C],
                                        hB[:, :, :].rearrange("p (h t) c -> p h (t c)", h=2),
                                        ALU.add).then_inc(S["hC_ready"], 1)
                dve.wait_ge(S["hC_ready"], g + 1)
                ln_stats(g, "c", hC, statsC, mvC)

            def b_stats(g):
                dve.wait_ge(S["hB_ready"], g + 1)
                ln_stats(g, "b", hB, statsB, mvB)

            def c_qk_stats(g):
                dve.wait_ge(S["qkv_out"], G * g + G)
                qkc.begin(g)
                statistics(qkc, lambda n: qk[:, n // 2, n % 2, :], stats_qk, mv_qk, 2 * G).then_inc(S["qk_stats"], 1)
                qkc.end()

            def heads(ap):
                return ap.rearrange("p (h d) -> p h d", d=HD)

            def c_k_norm(g):
                dve.wait_ge(S["qk_rstd"], g + 1)
                normalise(lambda t: kpad[:, t, :, 0:HD], lambda t: heads(qk[:, t, 1, :]), mv_qk, rstd_qk,
                          range(1, 2 * G, 2)).then_inc(S["k_norm"], 1)

            def c_q_norm(g):
                normalise(lambda t: qpad[:, t, :, 0:HD], lambda t: heads(qk[:, t, 0, :]), mv_qk, rstd_qk,
                          range(0, 2 * G, 2)).then_inc(S["q_norm"], 1)

            def c_keys(g, t):
                dve.wait_ge(S["kT_psum"], G * g + t + 1)
                nc.vector.tensor_copy(kT[:, t, :], ps[:, 4 + t, 0:HC * P]).then_inc(S["kT_ready"], 1)

            def c_queries(g, t):
                dve.wait_ge(S["qT_psum"], G * g + t + 1)
                for j in range(2, HJ):
                    last = nc.vector.tensor_copy(*queries_out(j, t))
                last.then_inc(S["q_high_heads"], 1)

            def c_max(g, t, c):
                dve.wait_ge(S["scores_psum"], HC * (G * g + t) + c + 1)
                nc.vector.tensor_reduce(nmax[:, t, HJ * c:HJ * c + HJ],
                                        ps[:, 4 + c, :].rearrange("p (j q) -> p j q", q=P),
                                        AX.X, ALU.max, negate=True).then_inc(S["max_ready"], 1)

            def c_values(g, t):
                if t == 0:
                    vch.begin(g)
                dve.wait_ge(S["exp_ready"], HC * (G * g + t + 1))
                vch.link(nc.vector.reciprocal(rsums[:, t, :], psums[:, t, :]))
                nc.vector.tensor_tensor(
                    vpad[:, t % 2, :, 0:HD], v_s[:, t, :].rearrange("p (h d) -> p h d", d=HD),
                    rsums[:, t, :].rearrange("p (h o) -> p h o", o=1).to_broadcast([P, HEADS, HD]),
                    ALU.mult).then_inc(S["vpad_ready"], 1)
                if t == G - 1:
                    vch.end()

            def c_attn_add(g):
                dve.wait_ge(S["aproj_psum"], g + 1)
                dve.wait_ge(S["res_ready"], g + 1)
                r2 = resC[:, :, :].rearrange("p (h t) c -> p h (t c)", h=2)
                nc.vector.tensor_tensor(r2, ps[:, 0:2, 0:2 * C], r2, ALU.add).then_inc(S["hF_ready"], 1)
                dve.wait_ge(S["hF_ready"], g + 1)
                ln_stats(g, "r", resC, statsR, mvR)

            def r_out(g):
                if not isinstance(g, int) or g > 0:
                    dve.wait_ge(S["scattered"], 16 * 2 * G * g)
                ln_out(g, "r", hnR, resC, mvR, rstdR)

            def r_pick(g):
                link = route.link
                route.begin(g)
                dve.wait_ge(S["logits_psum"], g + 1)
                link(nc.vector.tensor_copy(logits[:, :], ps[:, 6, 0:G * E]), stand_alone)
                for t in range(G):
                    last = nc.vector.max(top8[:, t, :], logits[:, t * E:(t + 1) * E])
                link(last, stand_alone)
                for t in range(G):
                    last = nc.vector.max_index(top_i[:, t, :], top8[:, t, :], logits[:, t * E:(t + 1) * E])
                link(last)
                nc.vector.tensor_tensor(gap[:, :], top8[:, :, 1], top8[:, :, 0],
                                        ALU.subtract).then_inc(S["gap_ready"], 1)
                link(nc.vector.tensor_copy(top_f[:, :, :], top_i[:, :, 0:2].rearrange("p t s -> p s t")))
                for s in range(2):
                    last = nc.vector.tensor_tensor(
                        hot[:, s, :, :], lane8[:, :, :],
                        top_f[:, s, :].rearrange("p (t o) -> p t o", o=1).to_broadcast([P, G, E]), ALU.is_equal)
                link(last)
                nc.vector.tensor_copy(run_counts[:, 0, :], run_counts[:, G, :])
                nc.vector.tensor_tensor(picked[:, :, :], hot[:, 0, :, :], hot[:, 1, :, :], ALU.add)
                link(nc.vector.tensor_tensor(picked_f[:, :, :], hot[:, 0, :, :], hot[:, 1, :, :], ALU.add))
                for t in range(G):
                    link(nc.vector.tensor_tensor(run_counts[:, t + 1, :], run_counts[:, t, :], picked_f[:, t, :],
                                                 ALU.add))
                nc.vector.tensor_copy(run_bf[:, :, :], run_counts[:, :, :]).then_inc(S["picked_ready"], 1)

            def r_place(g):
                link = route.link
                dve.wait_ge(S["egap_ready"], g + 1)
                link(nc.vector.tensor_scalar(esum[:, :], egap[:, :], 1.0, None, ALU.add))
                link(nc.vector.reciprocal(wts[:, 0:G], esum[:, :]))
                link(nc.vector.tensor_tensor(wts[:, G:2 * G], wts[:, 0:G], egap[:, :], ALU.mult))
                dve.wait_ge(S["place_psum"], g + 1)
                link(nc.vector.tensor_tensor(place[:, :], ps[:, 7, 0:G * E],
                                             region_off[:, :, :].rearrange("p t e -> p (t e)"), ALU.add))
                for s in range(2):
                    last = nc.vector.tensor_tensor(placed[:, s, :, :], hot[:, s, :, :],
                                                   place[:, :].rearrange("p (t e) -> p t e", e=E), ALU.mult)
                link(last)
                link(nc.vector.tensor_reduce(slot_f[:, :], placed[:, :, :, :].rearrange("p s t e -> p (s t) e"),
                                             AX.X, ALU.add))
                link(nc.vector.tensor_copy(slot_i[:, :], slot_f[:, :]))
                nc.vector.tensor_copy(rowR[:, :, 0:2], wts[:, :].rearrange("p (s t) -> p t s", s=2))
                nc.vector.tensor_copy(rowR[:, :, 2], top_f[:, 0, :])
                link(nc.vector.tensor_copy(rowR[:, :, 3], token_f[:, :]))
                nc.vector.tensor_scalar(token_f[:, :], token_f[:, :], float(N), None,
                                        ALU.add).then_inc(S["slots_ready"], 1)
                route.end()

            def round_(i):
                ga, gb, gc, gr = stages(i)
                A, B, CA, R = (g is not None for g in (ga, gb, gc, gr))
                if R: r_out(gr)
                if A: a_delta(ga)
                if CA: c_qk_stats(gc)
                if B: a_residual(gb)
                if B: b_stats(gb)
                if CA: c_k_norm(gc)
                if B: ln_out(gb, "b", hnB, hB, mvB, rstdB)
                if R: r_pick(gr)
                if A: a_tokens(ga)
                if A: a_normalise(ga)
                if R: r_place(gr)
                if A: a_mix(ga)
                if CA: c_keys(gc, 0)
                if CA: c_q_norm(gc)
                if CA: c_keys(gc, 1)
                if CA: c_keys(gc, 2)
                if CA: c_keys(gc, 3)
                if A: a_exponents(ga)
                if A: a_fraction_args(ga)
                if CA: c_queries(gc, 0)
                if CA: c_max(gc, 0, 0)
                if CA: c_max(gc, 0, 1)
                if CA: c_max(gc, 0, 2)
                if CA: c_queries(gc, 1)
                if B: b_mlp_add(gb, gc)
                if CA: c_max(gc, 1, 0)
                if CA: c_max(gc, 1, 1)
                if CA: c_values(gc, 0)
                if A: a_scan_p(ga)
                if CA: c_max(gc, 1, 2)
                if CA: c_queries(gc, 2)
                if B: ln_out(gb, "c", hnC, hC, mvC, rstdC)
                if CA: c_max(gc, 2, 0)
                if A: a_scan_q(ga)
                if CA: c_max(gc, 2, 1)
                if CA: c_values(gc, 1)
                if CA: c_queries(gc, 3)
                if CA: c_max(gc, 2, 2)
                if CA: c_max(gc, 3, 0)
                if CA: c_values(gc, 2)
                if CA: c_max(gc, 3, 1)
                if CA: c_max(gc, 3, 2)
                if A: a_denominator(ga)
                if CA: c_values(gc, 3)
                if A: a_reciprocal(ga, 0)
                if A: a_reciprocal(ga, 1)
                if A: a_reciprocal(ga, 2)
                if CA: c_attn_add(gc)
                if A: a_reciprocal(ga, 3)
                if A: a_gate(ga)

            rounds(dve, round_)

            table = Chain(dve, S["d_table"], 16)
            link = table.link
            table.begin(0)
            dve.wait_ge(S["x_summed"], NG)
            link(nc.vector.memset(pad_tile, 0.0))
            link(nc.vector.tensor_copy(pad_tile[:, :, 3], pad_token[:, :]))
            dve.wait_ge(S["counts_psum"], 1)
            link(nc.vector.tensor_copy(n_tok[:, :], ps[:, 7, 0:E]))
            nc.vector.tensor_tensor(pad_row[:, :], n_tok[0:1, :], region_off[0:1, 0, :],
                                    ALU.add).then_inc(S["pads_ready"], 1)
            link(nc.vector.tensor_tensor(mth[:, :, :], n_tok[:, :].rearrange("p (e o) -> p e o", o=1)
                                         .to_broadcast([P, E, MAXT]), mth[:, :, :], ALU.is_gt))
            link(nc.vector.tensor_reduce(n_tiles[:, :], mth[:, :, :], AX.X, ALU.add))
            link(nc.vector.tensor_tensor_scan(tile_end[:, :], one_row[:, :], n_tiles[:, :], 0.0, ALU.mult, ALU.add))
            link(nc.vector.tensor_tensor(passed[:, :, :], jth[:, :, :],
                                         tile_end[:, :].rearrange("p (o e) -> p o e", o=1).to_broadcast([P, NT, E]),
                                         ALU.is_ge))
            link(nc.vector.tensor_reduce(exp_f[:, :], passed[:, :, :], AX.X, ALU.add))
            link(nc.vector.tensor_tensor(passed[:, :, :], passed[:, :, :],
                                         n_tiles[:, :].rearrange("p (o e) -> p o e", o=1).to_broadcast([P, NT, E]),
                                         ALU.mult))
            link(nc.vector.tensor_reduce(off_f[:, :], passed[:, :, :], AX.X, ALU.add))
            link(nc.vector.tensor_tensor(off_f[:, :], jth[:, :, 0], off_f[:, :], ALU.subtract))
            link(nc.vector.tensor_scalar(ok_f[:, :], exp_f[:, :], float(E), float(ET), ALU.is_lt, ALU.mult))
            link(nc.vector.tensor_tensor(off_f[:, :], off_f[:, :], ok_f[:, :], ALU.mult))
            nc.vector.tensor_scalar(expert_of[:, :], exp_f[:, :], float(E - 1), None, ALU.min)
            link(nc.vector.tensor_scalar(exp_f[:, :], exp_f[:, :], float(REGION), None, ALU.mult))
            nc.vector.tensor_copy(tile_exp[:, :], expert_of[0:1, :])
            link(nc.vector.tensor_tensor(off_f[:, :], off_f[:, :], exp_f[:, :], ALU.add))
            link(nc.vector.tensor_copy(tile_row[:, :], off_f[0:1, :]))
            dve.sem_inc(S["table_ready"], 1)
            dve.wait_ge(S["scattered"], 16 * 2 * G * NG)
            dve.wait_ge(S["h_stored"], 16 * NG)
            for b in range(NBUF):
                nc.vector.memset(eup[b][CC:CC + 1, 1, :], 0.0)
                nc.vector.memset(exT_hi[b][CC:CC + 1, 0, :].bitcast(F32), 1.0)
                nc.vector.memset(exT_lo[b][CC:CC + 1, 0, :].bitcast(F32), 0.0).then_inc(S["extra_rows"], 1)
            table.end()

            exp_chain = Chain(dve, S["d_exp"], 4)

            def e_rows(i, b):
                dve.wait_ge(S["x_high"], NBUF * i + b + 1)
                nc.vector.tensor_tensor(exT_lo[b][0:CC, :, :], ps[0:CC, 0:2, :],
                                        exT_hi[b][0:CC, :, :].bitcast(F32), ALU.subtract).then_inc(S["x_low"], 1)

            def e_pick(i, b):
                j = NBUF * i + b
                exp_chain.begin(j)
                dve.wait_ge(e_w[b], (i + 1) * 16 * PER_TILE)
                dve.wait_ge(e_rows_in[b], (i + 1) * 16)
                if not isinstance(i, int) or i > 0:
                    dve.wait_ge(S["e_added"], 16 * ES * (j - NBUF + 1))
                nc.vector.tensor_copy(etoken[b][:, :], ex[b][:, :, 3])
                nc.vector.tensor_tensor(eweight[b][:, :], ex[b][:, :, 0], ex[b][:, :, 1], ALU.subtract)
                exp_chain.link(nc.vector.tensor_tensor(first_is[b][:, :], ex[b][:, :, 2],
                                                       expert_of[:, bass.ds(j, 1)].to_broadcast([P, ES]),
                                                       ALU.is_equal))
                exp_chain.link(nc.vector.tensor_tensor(eweight[b][:, :], eweight[b][:, :], first_is[b][:, :],
                                                       ALU.mult))
                exp_chain.link(nc.vector.tensor_tensor(eweight[b][:, :], eweight[b][:, :], ex[b][:, :, 1], ALU.add))

            def e_result(i, b):
                dve.wait_ge(S["e_down_psum"], NBUF * i + b + 1)
                for s in range(2):
                    last = nc.vector.tensor_tensor(
                        ey[b][:, 2 * s:2 * s + 2, :], ps[:, 6 + s, 0:2 * C].rearrange("p (t c) -> p t c", t=2),
                        eb2[b][:, :].rearrange("p (o c) -> p o c", o=1).to_broadcast([P, 2, C]), ALU.add)
                exp_chain.link(last)
                exp_chain.end()
                nc.vector.tensor_tensor(ey[b][:, :, :], ey[b][:, :, :],
                                        eweight[b][:, :].rearrange("p (s o) -> p s o", o=1).to_broadcast([P, ES, C]),
                                        ALU.mult).then_inc(S["e_y"], 1)

            def e_step(i, b):
                e_pick(i, b)
                if after(i, b):
                    e_rows(*after(i, b))
                e_result(i, b)

            e_rows(0, 0)
            expert_tiles(dve, e_step)


def kernel(**inputs):
    import numpy as _np
    import concourse.bacc as _bacc
    from concourse import mybir as _mybir
    from concourse.bass_utils import run_bass_kernel_spmd as _run

    nc = _bacc.Bacc("TRN2", target_bir_lowering=False, num_devices=1)
    w = {k: _np.asarray(v) for k, v in inputs.items()}

    def chunks(v):
        return v.reshape(2, -1).T

    laid = {
        "x": w["x"],
        "L0_tok_w": w["L0_tok_w"],
        "L0_attn_WrT": w["L0_attn_Wr"].T, "L0_attn_WkT": w["L0_attn_Wk"].T,
        "L0_attn_WvT": w["L0_attn_Wv"].T, "L0_attn_WoT": w["L0_attn_Wo"].T,
        "L0_chan": _np.stack([chunks(w[n].reshape(-1)) for n in (
            "L0_attn_time_decay", "L0_attn_time_first", "L0_attn_time_mix_k",
            "L0_attn_time_mix_v", "L0_attn_time_mix_r")], axis=1),
        "L0_ffn_upT": w["L0_ffn_in_weight"].T,
        "L0_ffn_bias": w["L0_ffn_in_bias"].reshape(-1, 128).T,
        "L0_ffn_out_weight": w["L0_ffn_out_weight"],
        "L1_attn_WqT": w["L1_attn_Wq"].T, "L1_attn_WkT": w["L1_attn_Wk"].T,
        "L1_attn_WvT": w["L1_attn_Wv"].T, "L1_attn_WoT": w["L1_attn_Wo"].T,
        "L1_attn_gq": w["L1_attn_gq"], "L1_attn_gk": w["L1_attn_gk"],
        "L1_attn_bk": w["L1_attn_bk"], "L1_attn_bv": w["L1_attn_bv"], "L1_attn_bo": w["L1_attn_bo"],
        "L1_ffn_routerT": w["L1_ffn_router_w"].T,
        "L1_ffn_w1": w["L1_ffn_w1"].reshape(-1, w["L1_ffn_w1"].shape[-1]),
        "L1_ffn_b1": w["L1_ffn_b1"],
        "L1_ffn_w2": w["L1_ffn_w2"].reshape(-1, w["L1_ffn_w2"].shape[-1]),
        "L1_ffn_b2": w["L1_ffn_b2"],
    }
    arrays, args = {}, {}
    for name, v in laid.items():
        v = _np.ascontiguousarray(v)
        arrays[f"in_{name}"] = v
        args[name] = nc.dram_tensor(f"in_{name}", v.shape, _mybir.dt.from_np(v.dtype), kind="ExternalInput").ap()
    B, T2, C = w["x"].shape
    out = nc.dram_tensor("out_0", (B, T2 // 2, C), _mybir.dt.float32, kind="ExternalOutput").ap()
    build_tower(nc, args, out)
    return _run(nc, [arrays], core_ids=[0]).results[0]["out_0"]
```
